# Optimizing a Trainium2 kernel written in Bass

```python
import numpy as np
import jax
import jax.numpy as jnp

def _softmax(x, axis=-1):
    return jax.nn.softmax(x, axis=axis)

def _gelu(x):
    return jax.nn.gelu(x, approximate=True)

def _silu(x):
    return jax.nn.silu(x)

def _sigmoid(x):
    return jax.nn.sigmoid(x)

def _layernorm(x, axis=-1, eps=1e-05):
    m = jnp.mean(x, axis=axis, keepdims=True)
    v = jnp.var(x, axis=axis, keepdims=True)
    return (x - m) / jnp.sqrt(v + eps)

def _scatter_add(tgt, idx, src, axis=0):
    return tgt.at[idx].add(src)

def _segment_sum(src, seg, n):
    return jax.ops.segment_sum(src, seg, n)
kernel_name = 'mk_prb_d2_jaxref_r8_96c548'

def setup_inputs(seed: int=0):
    np.random.seed(seed)
    _w = jnp.asarray

    def _L0_attn_setup():
        import jax, jax.numpy as jnp
        import numpy as np
        from jax import lax
        B_SZ, L, D_INNER, D_STATE, DT_RANK = (2, 256, 256, 16, 64)
        key = jax.random.key(seed)
        k = jax.random.split(key, 6)
        x = jax.random.normal(k[0], (B_SZ, L, D_INNER), dtype=jnp.float32)
        A = jnp.tile(jnp.arange(1, D_STATE + 1, dtype=jnp.float32)[None, :], (D_INNER, 1))
        A_log = jnp.log(A)
        D = jnp.ones((D_INNER,), dtype=jnp.float32)
        dt_init_std = DT_RANK ** (-0.5)
        W_x = jax.random.normal(k[1], (DT_RANK + 2 * D_STATE, D_INNER), dtype=jnp.float32) * D_INNER ** (-0.5)
        W_dt = jax.random.uniform(k[2], (D_INNER, DT_RANK), dtype=jnp.float32, minval=-dt_init_std, maxval=dt_init_std)
        dt = jnp.exp(jax.random.uniform(k[3], (D_INNER,), dtype=jnp.float32) * (np.log(0.1) - np.log(0.001)) + np.log(0.001))
        dt = jnp.clip(dt, 0.001, None)
        b_dt = dt + jnp.log(-jnp.expm1(-dt))
        return {'x': x, 'A_log': A_log, 'D': D, 'W_x': W_x, 'W_dt': W_dt, 'b_dt': b_dt}
    _L0_attn_in = _L0_attn_setup()

    def _L0_ffn_setup():
        import jax, jax.numpy as jnp
        import numpy as np
        B, S, D, H = (4, 256, 256, 1024)

        def fwht(x):
            orig_shape = x.shape
            n = orig_shape[-1]
            x = x.reshape(-1, n)
            h = 1
            while h < n:
                xb = x.reshape(-1, n // (2 * h), 2, h)
                a = xb[:, :, 0, :]
                b = xb[:, :, 1, :]
                x = jnp.stack([a + b, a - b], axis=2).reshape(-1, n)
                h *= 2
            scale = jnp.asarray(1.0 / np.sqrt(n), dtype=x.dtype)
            return (x * scale).reshape(orig_shape)
        key = jax.random.key(seed)
        kx, k1, k2, k3 = jax.random.split(key, 4)
        x = jax.random.normal(kx, (B, S, D), dtype=jnp.float32)
        W1 = jax.random.normal(k1, (H, D), dtype=jnp.float32) * (1.0 / np.sqrt(D))
        W2 = jax.random.normal(k2, (D, H), dtype=jnp.float32) * (1.0 / np.sqrt(H))
        W3 = jax.random.normal(k3, (H, D), dtype=jnp.float32) * (1.0 / np.sqrt(D))
        return {'x': x, 'W1': W1, 'W2': W2, 'W3': W3}
    _L0_ffn_in = _L0_ffn_setup()

    def _L1_attn_setup():
        import jax, jax.numpy as jnp
        import numpy as np
        EMBED_DIM = 256
        NUM_HEADS = 16
        HEAD_DIM = EMBED_DIM // NUM_HEADS
        D_K = 128
        SCALE = 1.0 / float(np.sqrt(HEAD_DIM))
        LAYER_DEPTH = 6 / 12
        BATCH, SEQ = (2, 256)
        key = jax.random.key(seed)
        ks = jax.random.split(key, 8)
        return {'hidden_states': jax.random.normal(ks[0], (BATCH, SEQ, EMBED_DIM), jnp.float32), 'c_attn_w': jax.random.normal(ks[1], (EMBED_DIM, 3 * EMBED_DIM), jnp.float32) * 0.02, 'c_attn_b': jax.random.normal(ks[2], (3 * EMBED_DIM,), jnp.float32) * 0.02, 'c_proj_w': jax.random.normal(ks[3], (EMBED_DIM, EMBED_DIM), jnp.float32) * 0.02, 'c_proj_b': jax.random.normal(ks[4], (EMBED_DIM,), jnp.float32) * 0.02, 'cam_gate': jax.random.normal(ks[5], (D_K,), jnp.float32) * 0.1, 'cam_w0': jax.random.normal(ks[6], (1,), jnp.float32), 'cam_w1': jax.random.normal(ks[7], (1,), jnp.float32)}
    _L1_attn_in = _L1_attn_setup()

    def _L1_ffn_setup():
        import jax, jax.numpy as jnp
        import numpy as np
        B, S, D = (4, 128, 256)
        H = 512
        NE = 8
        TOPK = 2
        key = jax.random.key(seed)
        ks = jax.random.split(key, 9)
        s = lambda fan_in: 1.0 / np.sqrt(fan_in)
        return {'x': jax.random.normal(ks[0], (B, S, D), dtype=jnp.float32), 'W1': jax.random.normal(ks[1], (NE, D, H), dtype=jnp.float32) * s(D), 'b1': jnp.zeros((NE, H), dtype=jnp.float32), 'W2': jax.random.normal(ks[2], (NE, H, H), dtype=jnp.float32) * s(H), 'b2': jnp.zeros((NE, H), dtype=jnp.float32), 'W3': jax.random.normal(ks[3], (NE, H, D), dtype=jnp.float32) * s(H), 'b3': jnp.zeros((NE, D), dtype=jnp.float32), 'Wg': jax.random.normal(ks[4], (D, NE), dtype=jnp.float32) * s(D), 'bg': jnp.zeros((NE,), dtype=jnp.float32)}
    _L1_ffn_in = _L1_ffn_setup()
    _d = {'L0_attn_x': _L0_attn_in['x'], 'L0_attn_A_log': _L0_attn_in['A_log'], 'L0_attn_D': _L0_attn_in['D'], 'L0_attn_W_x': _L0_attn_in['W_x'], 'L0_attn_W_dt': _L0_attn_in['W_dt'], 'L0_attn_b_dt': _L0_attn_in['b_dt'], 'L0_ffn_W1': _L0_ffn_in['W1'], 'L0_ffn_W2': _L0_ffn_in['W2'], 'L0_ffn_W3': _L0_ffn_in['W3'], 'L1_attn_c_attn_w': _L1_attn_in['c_attn_w'], 'L1_attn_c_attn_b': _L1_attn_in['c_attn_b'], 'L1_attn_c_proj_w': _L1_attn_in['c_proj_w'], 'L1_attn_c_proj_b': _L1_attn_in['c_proj_b'], 'L1_attn_cam_gate': _L1_attn_in['cam_gate'], 'L1_attn_cam_w0': _L1_attn_in['cam_w0'], 'L1_attn_cam_w1': _L1_attn_in['cam_w1'], 'L1_ffn_W1': _L1_ffn_in['W1'], 'L1_ffn_b1': _L1_ffn_in['b1'], 'L1_ffn_W2': _L1_ffn_in['W2'], 'L1_ffn_b2': _L1_ffn_in['b2'], 'L1_ffn_W3': _L1_ffn_in['W3'], 'L1_ffn_b3': _L1_ffn_in['b3'], 'L1_ffn_Wg': _L1_ffn_in['Wg'], 'L1_ffn_bg': _L1_ffn_in['bg']}
    _x0 = _d['L0_attn_x']
    _d['L0_attn_x'] = jax.random.normal(jax.random.fold_in(jax.random.key(seed), 1), (4, 256, 256), dtype=_x0.dtype)
    del _x0
    return _d

def reference(L0_attn_x, L0_attn_A_log, L0_attn_D, L0_attn_W_x, L0_attn_W_dt, L0_attn_b_dt, L0_ffn_W1, L0_ffn_W2, L0_ffn_W3, L1_attn_c_attn_w, L1_attn_c_attn_b, L1_attn_c_proj_w, L1_attn_c_proj_b, L1_attn_cam_gate, L1_attn_cam_w0, L1_attn_cam_w1, L1_ffn_W1, L1_ffn_b1, L1_ffn_W2, L1_ffn_b2, L1_ffn_W3, L1_ffn_b3, L1_ffn_Wg, L1_ffn_bg):

    def _L0_attn_ref(x, A_log, D, W_x, W_dt, b_dt):
        import jax, jax.numpy as jnp
        import numpy as np
        from jax import lax
        B_SZ, L, D_INNER, D_STATE, DT_RANK = (2, 256, 256, 16, 64)
        A = -jnp.exp(A_log)
        xp = jnp.einsum('bld,pd->blp', x, W_x)
        delta_p = xp[..., :DT_RANK]
        B_proj = xp[..., DT_RANK:DT_RANK + D_STATE]
        C_proj = xp[..., DT_RANK + D_STATE:]
        delta = jax.nn.softplus(jnp.einsum('blr,dr->bld', delta_p, W_dt) + b_dt)
        A_bar = jnp.exp(jnp.einsum('bld,dn->bldn', delta, A))
        Bx = jnp.einsum('bld,bln->bldn', delta, B_proj) * x[..., None]

        def step(h, inp):
            Ab_t, bx_t, c_t = inp
            h = Ab_t * h + bx_t
            y_t = jnp.einsum('bdn,bn->bd', h, c_t)
            return (h, y_t)
        h0 = jnp.zeros((x.shape[0], D_INNER, D_STATE), dtype=x.dtype)
        _, ys = lax.scan(step, h0, (A_bar.transpose(1, 0, 2, 3), Bx.transpose(1, 0, 2, 3), C_proj.transpose(1, 0, 2)))
        y = ys.transpose(1, 0, 2)
        return y + x * D

    def _L0_ffn_ref(x, W1, W2, W3):
        import jax, jax.numpy as jnp
        import numpy as np
        B, S, D, H = (4, 256, 256, 1024)

        def fwht(x):
            orig_shape = x.shape
            n = orig_shape[-1]
            x = x.reshape(-1, n)
            h = 1
            while h < n:
                xb = x.reshape(-1, n // (2 * h), 2, h)
                a = xb[:, :, 0, :]
                b = xb[:, :, 1, :]
                x = jnp.stack([a + b, a - b], axis=2).reshape(-1, n)
                h *= 2
            scale = jnp.asarray(1.0 / np.sqrt(n), dtype=x.dtype)
            return (x * scale).reshape(orig_shape)
        up_gate = jnp.einsum('bsd,hd->bsh', x, W1)
        up_lin = jnp.einsum('bsd,hd->bsh', x, W3)
        hidden = jax.nn.silu(up_gate) * up_lin
        hidden = fwht(hidden)
        out = jnp.einsum('bsh,dh->bsd', hidden, W2)
        return out

    def _L1_attn_ref(hidden_states, c_attn_w, c_attn_b, c_proj_w, c_proj_b, cam_gate, cam_w0, cam_w1):
        import jax, jax.numpy as jnp
        import numpy as np
        EMBED_DIM = 256
        NUM_HEADS = 16
        HEAD_DIM = EMBED_DIM // NUM_HEADS
        D_K = 128
        SCALE = 1.0 / float(np.sqrt(HEAD_DIM))
        LAYER_DEPTH = 6 / 12
        BATCH, SEQ = (2, 256)
        qkv = hidden_states @ c_attn_w + c_attn_b
        Q, K, V = jnp.split(qkv, 3, axis=2)
        attn_scores = jnp.einsum('bse,bte->bst', Q, K) * SCALE
        Q_cam, K_cam, V_cam = (Q[:, :, :D_K], K[:, :, :D_K], V[:, :, :D_K])
        base_A = jax.lax.stop_gradient(jax.nn.softmax(jnp.einsum('bsd,btd->bst', Q_cam, K_cam) * SCALE, axis=-1))
        layer_weight = jax.nn.sigmoid(cam_w0[0] + cam_w1[0] * LAYER_DEPTH)
        cam_ctx = jnp.einsum('bst,btd->bsd', base_A, V_cam)
        cam_bias = jnp.einsum('bsd,btd->bst', jnp.tanh(cam_ctx * cam_gate), K_cam)
        cam_bias = cam_bias * (SCALE * layer_weight)
        final_attn = jax.nn.softmax(attn_scores + cam_bias, axis=-1)
        context = jnp.einsum('bst,bte->bse', final_attn, V)
        output = context @ c_proj_w + c_proj_b
        return output

    def _L1_ffn_ref(x, W1, b1, W2, b2, W3, b3, Wg, bg):
        import jax, jax.numpy as jnp
        import numpy as np
        B, S, D = (4, 128, 256)
        H = 512
        NE = 8
        TOPK = 2
        gate_logits = jnp.einsum('bsd,dn->bsn', x, Wg) + bg
        gate_weights = jax.nn.softmax(gate_logits, axis=-1)
        topv, topi = jax.lax.top_k(gate_weights, TOPK)
        h = jax.nn.gelu(jnp.einsum('bsd,ndh->nbsh', x, W1) + b1[:, None, None, :], approximate=False)
        h = jax.nn.gelu(jnp.einsum('nbsh,nhf->nbsf', h, W2) + b2[:, None, None, :], approximate=False)
        eo = jnp.einsum('nbsf,nfd->nbsd', h, W3) + b3[:, None, None, :]
        comb = jnp.sum(jax.nn.one_hot(topi, NE, dtype=x.dtype) * topv[..., None], axis=-2)
        out = jnp.einsum('nbsd,bsn->bsd', eo, comb)
        return out
    x = L0_attn_x
    xn = _layernorm(x, axis=-1)
    x = x + _L0_attn_ref(xn, L0_attn_A_log, L0_attn_D, L0_attn_W_x, L0_attn_W_dt, L0_attn_b_dt) + _L0_ffn_ref(xn, L0_ffn_W1, L0_ffn_W2, L0_ffn_W3)
    xn = _layernorm(x, axis=-1)
    x = x + _L1_attn_ref(xn, L1_attn_c_attn_w, L1_attn_c_attn_b, L1_attn_c_proj_w, L1_attn_c_proj_b, L1_attn_cam_gate, L1_attn_cam_w0, L1_attn_cam_w1) + _L1_ffn_ref(xn, L1_ffn_W1, L1_ffn_b1, L1_ffn_W2, L1_ffn_b2, L1_ffn_W3, L1_ffn_b3, L1_ffn_Wg, L1_ffn_bg)
    return x

_drawn_inputs = setup_inputs


def setup_inputs(seed=0):
    import zlib

    import numpy as np

    out = dict(_drawn_inputs(seed))
    spreads = {'L0_attn_D': (1.0, 0.2),
     'L1_ffn_b1': (0.0, 2.0),
     'L1_ffn_b2': (0.0, 1.835),
     'L1_ffn_b3': (0.0, 1.218),
     'L1_ffn_bg': (0.0, 1.144)}
    factors = {'L1_attn_c_attn_w': 8.0,
     'L1_attn_c_attn_b': 8.0,
     'L1_attn_c_proj_w': 8.0,
     'L1_attn_c_proj_b': 19.167,
     'L1_attn_cam_gate': 8.0}
    for name, (base, spread) in spreads.items():
        noise = np.random.default_rng([zlib.crc32(name.encode()), seed]).standard_normal(out[name].shape)
        drawn = base * np.exp(spread * noise) if base else spread * noise
        out[name] = jnp.asarray(drawn.astype(out[name].dtype))
    for name, factor in factors.items():
        out[name] = (out[name] * factor).astype(out[name].dtype)
    return out
```

```python
from contextlib import ExitStack

import concourse.bass as bass
from concourse import mybir

F32 = mybir.dt.float32
BF16 = mybir.dt.bfloat16
I32 = mybir.dt.int32
U32 = mybir.dt.uint32
ALU = mybir.AluOpType
ACT = mybir.ActivationFunctionType
AX = mybir.AxisListType

P = 128
BATCH, SEQ, D = 4, 256, 256
TOK = BATCH * SEQ
NT = TOK // P
DH = D // P
NS, RANK = 16, 64
H0 = 1024
HC = H0 // P
QT_ = 4
QW = TOK // QT_
UNITS = NS * DH
UPQ = UNITS // QT_
NE, HM = 8, 512
KM = HM // P
MT = 2 * NT + NE - 1
BANK_OF_QK = (0, 1, 2, 3, 4, 5, 0, 1)
EPS = 1e-5
SCALE = 0.25

V_BDT, V_D, V_ALOG, V_QKB, V_GATE, V_W0, V_W1, V_B1, V_B2, V_WG, V_END = (
    0, 2, 4, 36, 40, 41, 42, 43, 75, 107, 123)
R_VB, R_PB, R_BG, R_END = 0, 256, 512, 520
C_ID, C_HAD, C_KEY, C_TILE, C_END = 0, 128, 256, 264, 264 + MT
B_TRI, B_ONE, B_END = 0, 128, 256


def build(nc, x, wx, wdt, w1, w3, w2, vecs, rows, consts, bconsts, sel, cattn, cproj,
          mw1, mw2, mw3, b3, zeros, out):
    assert UPQ == HC and UNITS == QT_ * UPQ

    with ExitStack() as ctx:
        def sb(name, shape, dt=F32):
            return ctx.enter_context(nc.sbuf_tensor(name, shape, dt))

        def sem(name):
            return ctx.enter_context(nc.semaphore(name))

        moe_w1 = sb("moe_w1", [P, NE, 2, HM])
        moe_w2 = sb("moe_w2", [P, NE, KM, HM])
        moe_w3 = sb("moe_w3", [P, NE, KM, D])
        loan3 = moe_w3[:].rearrange("p e k n -> p (e k n)")
        gate_w = loan3[:, 0:2048].rearrange("p (k h) -> p k h", k=DH)
        lin_w = loan3[:, 2048:4096].rearrange("p (k h) -> p k h", k=DH)
        down_w = loan3[:, 4096:6144]
        sel_w = loan3[:, 6144:8192].bitcast(BF16).rearrange("p (s m) -> p s m", m=P)
        loan2 = moe_w2[:, 6:8].rearrange("p e k n -> p (e k n)")
        ffn_out = loan2[:, 0:2048].rearrange("p (k t) -> p k t", k=DH)
        fly = loan2[:, 2048:4096]
        loan1 = moe_w1[:, 6:8].rearrange("p e k n -> p (e k n)")
        gl = [loan1[:, 512 * i:512 * i + 512] for i in range(2)]
        th = [loan1[:, 1024 + QW * i:1024 + QW * i + QW] for i in range(2)]
        hid = [loan1[:, 1536 + QW * i:1536 + QW * i + QW] for i in range(2)]

        res = sb("res", [P, NT, D])
        nrmT = sb("nrmT", [P, DH, TOK])
        area_c = sb("area_c", [P, 2048])
        nrm = area_c[:].rearrange("p (t d) -> p t d", t=NT)
        yacc = area_c[:].rearrange("p (k t) -> p k t", k=DH)
        area_d = sb("area_d", [P, 2048])
        delta = area_d[:].rearrange("p (k t) -> p k t", k=DH)
        qT = area_d[:].rearrange("p (k t) -> p k t", k=DH)
        area_e = sb("area_e", [P, 2048])
        du = area_e[:].rearrange("p (k t) -> p k t", k=DH)
        kT = area_e[:].rearrange("p (k t) -> p k t", k=DH)
        area_f = sb("area_f", [P, 2048])
        decay = area_f[:].rearrange("p (i t) -> p i t", i=2)
        val = area_f[:].rearrange("p (t d) -> p t d", t=NT)
        area_g = sb("area_g", [P, 2048])
        state = area_g[:].rearrange("p (i t) -> p i t", i=2)
        ctxT = area_g[:].rearrange("p (k t) -> p k t", k=DH)
        area_h = sb("area_h", [P, 2048])
        bc_split = area_h[:, 0:512].bitcast(BF16)
        wx_sb = area_h[:, 512:832].rearrange("p (k m) -> p k m", k=DH)
        wdt_sb = area_h[0:RANK, 832:1088]
        cattn_sb = sb("cattn_sb", [P, DH, 3 * D + NE])
        cproj_sb = sb("cproj_sb", [P, DH, D])
        vec = sb("vec", [P, V_END])
        row = sb("row", [P, R_END])
        cst = sb("cst", [P, C_END])
        bcst = sb("bcst", [P, B_END], BF16)
        ident = cst[:, C_ID:C_ID + P]
        hadamard = cst[:, C_HAD:C_HAD + P]
        amat = sb("amat", [P, 2 * NS])
        st6 = sb("st6", [P, NT, 6])
        mv = sb("mv", [P, NT, 2])
        ln_v = sb("ln_v", [P, NT])
        ln_s = sb("ln_s", [P, NT])
        ln_r = sb("ln_r", [P, NT])
        ln_t = sb("ln_t", [P, NT])

        gw = [area_g[:, 64 * i:64 * i + 64].rearrange("p (t e) -> p t e", e=NE) for i in range(8)]
        logit, expd, first, second, keyed, comb, place, tmp64 = gw
        hits = area_g[:, 512:512 + MT * NE].rearrange("p (m e) -> p m e", e=NE)
        g8 = [area_g[:, 768 + 8 * i:776 + 8 * i] for i in range(10)]
        top, esum, keymax, top2, e2, ones8, tiles8, upto8, base8, slotf = g8
        tile_int = area_g[:, 860:868].bitcast(I32)
        owner_f = area_g[:, 872:872 + MT]
        mask = sb("mask", [P, NT, NE], BF16)
        gain = sb("gain", [P, 2, NT])
        slot = sb("slot", [P, 2, NT], U32)
        owner = sb("owner", [P, MT], I32)
        lw = sb("lw", [P, 2])
        combT = cattn_sb[0:NE].rearrange("p k n -> p (k n)")[:, 0:TOK]
        b3_sb = cattn_sb[0:NE].rearrange("p k n -> p (k n)")[:, TOK:TOK + D]
        probs = area_h[:].rearrange("p (b i t) -> p b i t", b=BATCH, i=2)
        probsT = nrmT[:].rearrange("p k t -> p (k t)").rearrange("p (b k t) -> p b k t", b=BATCH, k=2)
        smax = sb("smax", [P, 2, BATCH, 2])
        ssum = sb("ssum", [P, 2, BATCH, 2])
        sinv = sb("sinv", [P, 2, BATCH, 2])
        xin = sb("xin", [P, D])[:]
        xT = sb("xT", [P, D])[:].rearrange("p (k t) -> p k t", k=DH)
        raw1 = area_d[:, 512:1024]
        raw2 = area_d[:, 1024:1536]
        yout = area_d[:, 1536:1792]
        h1T = area_e[:, 0:512].rearrange("p (k t) -> p k t", k=KM)
        h2T = area_e[:, 512:1024].rearrange("p (k t) -> p k t", k=KM)
        picked = [area_c[:].rearrange("p (t d) -> p t d", t=NT),
                  nrmT[:].rearrange("p k t -> p (k t)").rearrange("p (t d) -> p t d", t=NT)]
        xbuf = nc.dram_tensor("dispatched", (MT * P, D), F32, kind="Internal").ap()
        ybuf = nc.dram_tensor("expert_rows", (MT * P, D), F32, kind="Internal").ap()

        psum = ctx.enter_context(nc.psum_tensor("psum", [P, 8, 512], F32))

        def bank(i, n=1):
            return psum[:, i:i + n, :].rearrange("p b n -> p (b n)")

        L = {n: sem(f"load_{n}") for n in ("x", "x2", "wx", "wdt", "w1", "w3", "w2", "vec", "row", "cst", "bcst", "sel",
                                           "cattn", "cproj", "zero", "mw1", "mw2", "mw1_late", "mw2_late", "mw3", "b3")}
        dve_chain, act_chain, pool_chain = sem("dve_chain"), sem("act_chain"), sem("pool_chain")
        out_done = sem("out_done")
        var_ready, sqrt_ready, nrm_ready, nrmT_ready = (
            sem("var_ready"), sem("sqrt_ready"), sem("nrm_ready"), sem("nrmT_ready"))
        turned = sem("turned")
        fly_ready, had_ready, down_ready = sem("fly_ready"), sem("had_ready"), sem("down_ready")
        rank_ready, rank_copied, bc_ready, bc_done = sem("rank_ready"), sem("rank_copied"), sem("bc_ready"), sem("bc_done")
        z_ready, absexp_done, onepl_done, log_done, amat_ready, delta_ready, z_read = (
            sem("z_ready"), sem("absexp_done"), sem("onepl_done"), sem("log_done"), sem("amat_ready"),
            sem("delta_ready"), sem("z_read"))
        decay_zero, yinit_done = sem("decay_zero"), sem("yinit_done")
        b_ready, c_ready, decay_ready = sem("b_ready"), sem("c_ready"), sem("decay_ready")
        bx_done, scan_done, yc_done, y_added = sem("bx_done"), sem("scan_done"), sem("yc_done"), sem("y_added")
        up_ready, up_read, th_ready, prod_done, hid_ready, hid_used, acc_free = (
            sem("up_ready"), sem("up_read"), sem("th_ready"), sem("prod_done"), sem("hid_ready"), sem("hid_used"),
            sem("acc_free"))
        sumT_ready, back_ready, x1_ready = sem("sumT_ready"), sem("back_ready"), sem("x1_ready")

        z2_ready, lw_ready = sem("z2_ready"), sem("lw_ready")
        logits_ready, soft_in, soft_out, top2_ready, e2_ready, mask_ready, prefix_ready, slots_ready = (
            sem("logits_ready"), sem("soft_in"), sem("soft_out"), sem("top2_ready"), sem("e2_ready"),
            sem("mask_ready"), sem("prefix_ready"), sem("slots_ready"))
        owner_ready, comb_ready, combT_ready, combT_done = (
            sem("owner_ready"), sem("comb_ready"), sem("combT_ready"), sem("combT_done"))
        scattered = sem("scattered")
        qk_ready, qk_done, v_ready, v_done = sem("qk_ready"), sem("qk_done"), sem("v_ready"), sem("v_done")
        scores_ready, bias_ready, exp_done, probs_ready, probsT_ready, probsT_done = (
            sem("scores_ready"), sem("bias_ready"), sem("exp_done"), sem("probs_ready"), sem("probsT_ready"),
            sem("probsT_done"))
        context_ready, tanh_done, query_done, ctx_done = (
            sem("context_ready"), sem("tanh_done"), sem("query_done"), sem("ctx_done"))
        x_loaded, x_turned, xT_ready, l1_ready, r1_ready, t1_ready, h1_ready = (
            sem("x_loaded"), sem("x_turned"), sem("xT_ready"), sem("l1_ready"), sem("r1_ready"), sem("t1_ready"),
            sem("h1_ready"))
        l2_ready, r2_ready, t2_ready, h2_ready, l3_ready, y_ready, y_stored = (
            sem("l2_ready"), sem("r2_ready"), sem("t2_ready"), sem("h2_ready"), sem("l3_ready"), sem("y_ready"),
            sem("y_stored"))
        picked_ready = [sem(f"picked_ready{t}") for t in range(NT)]
        proj_ready, out_ready = sem("proj_ready"), sem("out_ready")

        block = ctx.enter_context(nc.Block())

        def attention_steps():
            return [[(s // 3, s % 3, b) for b in range(BATCH) for s in [d - b] if 0 <= s < 6] for d in range(BATCH + 5)]

        def nth(which, b):
            turns = sorted((3 * p + i, i, p) for p in range(2) for i in range(BATCH))
            return turns.index((3 * which + b, b, which)) + 1

        def n_of(q, c):
            return q * (UPQ // DH) + c // DH

        @block.sync
        def _(sp):
            x_t = x.rearrange("(t p) d -> p t d", p=P)
            sp.dma_start(res[:, 0:4, :], x_t[:, 0:4, :]).then_inc(L["x"], 16)
            sp.dma_start(res[:, 4:8, :], x_t[:, 4:8, :]).then_inc(L["x2"], 16)
            sp.dma_start(cst[:], consts).then_inc(L["cst"], 16)
            sp.dma_start(wx_sb, wx.rearrange("(k p) m -> p k m", p=P)).then_inc(L["wx"], 16)
            sp.dma_start(wdt_sb, wdt).then_inc(L["wdt"], 16)
            sp.dma_start(vec[:], vecs).then_inc(L["vec"], 16)
            sp.dma_start(gate_w, w1.rearrange("(k p) h -> p k h", p=P)).then_inc(L["w1"], 16)
            sp.dma_start(lin_w, w3.rearrange("(k p) h -> p k h", p=P)).then_inc(L["w3"], 16)
            sp.dma_start(bcst[:], bconsts.bitcast(BF16)).then_inc(L["bcst"], 16)
            sp.dma_start(row[:], rows).then_inc(L["row"], 16)
            sp.dma_start(cattn_sb[:, :, 0:3 * D], cattn.rearrange("(k p) n -> p k n", p=P)).then_inc(L["cattn"], 16)
            sp.dma_start(cproj_sb[:], cproj.rearrange("(k p) n -> p k n", p=P)).then_inc(L["cproj"], 16)
            e1 = mw1.rearrange("e (k p) n -> p e k n", p=P)
            e2_ = mw2.rearrange("e (k p) n -> p e k n", p=P)
            e3 = mw3.rearrange("e (k p) n -> p e k n", p=P)
            sp.dma_start(xbuf, zeros).then_inc(L["zero"], 16)
            for e in range(6):
                sp.dma_start(moe_w1[:, e], e1[:, e]).then_inc(L["mw1"], 16)
                sp.dma_start(moe_w2[:, e], e2_[:, e]).then_inc(L["mw2"], 16)
            sp.wait_ge(hid_used, UNITS + 2)
            sp.wait_ge(b_ready, UNITS)
            sp.wait_ge(c_ready, UNITS)
            for e in (6, 7):
                sp.dma_start(moe_w1[:, e], e1[:, e]).then_inc(L["mw1_late"], 16)
            for e in range(NE):
                sp.dma_start(moe_w3[:, e], e3[:, e]).then_inc(L["mw3"], 16)
            sp.wait_ge(sumT_ready, 4)
            for e in (6, 7):
                sp.dma_start(moe_w2[:, e], e2_[:, e]).then_inc(L["mw2_late"], 16)
            sp.wait_ge(qk_ready, 8)
            sp.dma_start(b3_sb, b3).then_inc(L["b3"], 16)

            def load_x(m):
                sp.dma_start(xin, xbuf[bass.ds(m * P, P), :]).then_inc(x_loaded, 16)

            def store_y(m):
                sp.wait_ge(y_ready, m + 2)
                sp.dma_start(ybuf[bass.ds(m * P, P), :], yout).then_inc(y_stored, 16)

            sp.wait_ge(scattered, 16 * 2 * NT)
            load_x(0)
            for m in (1, 2):
                sp.wait_ge(x_turned, m)
                load_x(m)
            sp.wait_ge(x_turned, 3)
            load_x(3)
            with sp.Fori(1, MT - 3) as m:
                sp.wait_ge(x_turned, m + 3)
                load_x(m + 3)
                store_y(m - 1)
            for m in range(MT - 4, MT):
                store_y(m)
            out_t = out.rearrange("(t p) d -> p t d", p=P)
            for t in range(NT):
                sp.wait_ge(out_ready, t + 1)
                sp.dma_start(out_t[:, t, :], res[:, t, :]).then_inc(out_done, 16)
            sp.wait_ge(out_done, 16 * NT)

        @block.gpsimd
        def _(pool):
            pool.dma_start(down_w.rearrange("p (c d) -> p c d", c=HC),
                           w2.rearrange("(c p) d -> p c d", p=P)).then_inc(L["w2"], 16)
            pool.dma_start(sel_w, sel.bitcast(BF16).rearrange("p (s m) -> p s m", m=P)).then_inc(L["sel"], 16)
            nc.gpsimd.memset(bc_split[96:128, :], 0.0).then_inc(hid_ready, 2)
            pool.wait_ge(hid_ready, 2)
            pool.wait_ge(L["w2"], 16)
            src, dst = down_w, fly
            done = 0
            for stage, half in enumerate((1, 2, 4)):
                a = src.rearrange("p (g two n) -> p g two n", two=2, n=half * D)
                o = dst.rearrange("p (g two n) -> p g two n", two=2, n=half * D)
                if stage:
                    pool.wait_ge(fly_ready, 2 * stage)
                nc.gpsimd.tensor_tensor(o[:, :, 0, :], a[:, :, 0, :], a[:, :, 1, :], ALU.add).then_inc(fly_ready, 1)
                nc.gpsimd.tensor_tensor(o[:, :, 1, :], a[:, :, 0, :], a[:, :, 1, :], ALU.subtract).then_inc(fly_ready, 1)
                src, dst = dst, src
            pool.wait_ge(nrmT_ready, 4)
            pool.wait_ge(L["vec"], 16)
            for k in range(DH):
                nc.gpsimd.tensor_scalar(yacc[:, k, :], nrmT[:, k, :], vec[:, V_D + k:V_D + k + 1], None,
                                        ALU.mult).then_inc(y_added, 1)

            def unit(q, c):
                u = q * UPQ + c
                g = gl[c % 2]
                pool.wait_ge(th_ready, u + 1)
                nc.gpsimd.tensor_tensor(g[:, 0:QW], g[:, 0:QW], g[:, QW:2 * QW], ALU.mult).then_inc(prod_done, 1)
                pool.wait_ge(prod_done, u + 1)
                pool.wait_ge(hid_used, u + 1)
                nc.gpsimd.tensor_tensor(hid[c % 2], g[:, 0:QW], th[c % 2], ALU.mult).then_inc(hid_ready, 1)
                pool.wait_ge(yc_done, u + 1)
                pool.wait_ge(y_added, u + 1)
                nc.gpsimd.tensor_tensor(yacc[:, c % 2, :], yacc[:, c % 2, :], state[:, c % 2, :],
                                        ALU.add).then_inc(y_added, 1)

            with pool.Fori(0, QT_) as q:
                for c in range(UPQ):
                    unit(q, c)

            pool.wait_ge(acc_free, QT_ + 1)
            pool.wait_ge(y_added, UNITS + 2)
            for g in range(4):
                t = slice(g * QW, g * QW + QW)
                nc.gpsimd.tensor_tensor(yacc[:, :, t], yacc[:, :, t], ffn_out[:, :, t], ALU.add).then_inc(sumT_ready, 1)

            pool.wait_ge(L["zero"], 16)
            pool.wait_ge(slots_ready, 1)
            for t in range(NT):
                for k in range(2):
                    pool.indirect_dma_start(out=xbuf, out_offset=bass.IndirectOffsetOnAxis(ap=slot[:, k, t:t + 1], axis=0),
                                            in_=nrm[:, t, :], in_offset=None).then_inc(scattered, 16)
            pool.wait_ge(scattered, 16 * 2 * NT)
            pool.wait_ge(ctx_done, BATCH)
            pool.wait_ge(y_stored, 16 * (MT + 1))
            for t in range(NT):
                for k in range(2):
                    pool.indirect_dma_start(out=picked[k][:, t, :], out_offset=None, in_=ybuf,
                                            in_offset=bass.IndirectOffsetOnAxis(ap=slot[:, k, t:t + 1], axis=0),
                                            ).then_inc(picked_ready[t], 16)

        @block.scalar
        def _(act):
            act.wait_ge(L["vec"], 16)
            nc.scalar.activation(amat[:], vec[:, V_ALOG:V_ALOG + 2 * NS], ACT.Exp).then_inc(act_chain, 1)
            act.wait_ge(act_chain, 1)
            nc.scalar.mul(amat[:], amat[:], -1.0).then_inc(amat_ready, 1)
            act.wait_ge(z2_ready, 1)
            nc.scalar.activation(lw[:, 1:2], lw[:, 0:1], ACT.Tanh, scale=0.5).then_inc(lw_ready, 1)

            act.wait_ge(var_ready, 1)
            nc.scalar.activation(ln_s[:], ln_v[:], ACT.Sqrt).then_inc(sqrt_ready, 1)
            for g in (0, 2):
                act.wait_ge(turned, g + 1)
                nc.scalar.copy(nrmT[:, g // 2, 0:512], bank(g)).then_inc(nrmT_ready, 1)
            act.wait_ge(rank_ready, 1)
            nc.scalar.copy(area_f[0:RANK, 0:TOK], bank(0, 2)[0:RANK, :]).then_inc(rank_copied, 1)
            for k in range(DH):
                act.wait_ge(z_ready, k + 1)
                nc.scalar.activation(area_g[:, TOK * k:TOK * k + TOK], bank(2 + 2 * k, 2), ACT.Abs,
                                     bias=vec[:, V_BDT + k:V_BDT + k + 1]).then_inc(z_read, 1)
            act.wait_ge(z_read, 2)
            nc.scalar.activation(area_g[:], area_g[:], ACT.Exp, scale=-1.0).then_inc(absexp_done, 1)
            act.wait_ge(onepl_done, 1)
            nc.scalar.activation(loan2[:, 0:2048], loan2[:, 0:2048], ACT.Ln).then_inc(log_done, 1)
            for g, b in enumerate((0, 1, 6, 7)):
                act.wait_ge(had_ready, g + 1)
                nc.scalar.mul(down_w[:, 512 * g:512 * g + 512], bank(b), 0.5 / H0 ** 0.5).then_inc(down_ready, 1)

            act.wait_ge(decay_zero, 1)
            act.wait_ge(delta_ready, 1)

            def unit(q, c):
                u = q * UPQ + c
                act.wait_ge(scan_done, u + 1)
                nc.scalar.activation(decay[:, c % 2, :].rearrange("p (b t) -> p b t", b=BATCH)[:, :, 1:SEQ],
                                     delta[:, c % 2, :].rearrange("p (b t) -> p b t", b=BATCH)[:, :, 1:SEQ],
                                     ACT.Exp, scale=amat[:, bass.ds((c % DH) * NS + n_of(q, c), 1)]).then_inc(decay_ready, 1)
                act.wait_ge(up_ready, u + 1)
                act.wait_ge(hid_ready, u + 1)
                nc.scalar.copy(gl[c % 2], bank(6)).then_inc(up_read, 1)
                nc.scalar.activation(th[c % 2], bank(6)[:, 0:QW], ACT.Tanh, scale=0.5).then_inc(up_read, 1)
                act.wait_ge(up_read, 2 * u + 4)
                nc.scalar.add(th[c % 2], th[c % 2], 1.0).then_inc(th_ready, 1)

            with act.Fori(0, QT_) as q:
                for c in range(UPQ):
                    unit(q, c)
                act.wait_ge(hid_used, q * UPQ + UPQ + 2)
                nc.scalar.copy(ffn_out[:, :, bass.ds(q * QW, QW)],
                               bank(7).rearrange("p (k t) -> p k t", k=DH)).then_inc(acc_free, 1)

            act.wait_ge(var_ready, 2)
            nc.scalar.activation(ln_s[:], ln_v[:], ACT.Sqrt).then_inc(sqrt_ready, 1)
            for g in (0, 2):
                act.wait_ge(turned, 4 + g + 1)
                nc.scalar.copy(nrmT[:, g // 2, 0:512], bank(g)).then_inc(nrmT_ready, 1)

            def qk_out(g):
                m, t = g // 2, g % 2
                act.wait_ge(qk_ready, g + 1)
                dst = (qT, kT)[m // 2][:, m % 2, 512 * t:512 * t + 512]
                nc.scalar.activation(dst, bank(BANK_OF_QK[g]), ACT.Identity, bias=vec[:, V_QKB + m:V_QKB + m + 1]).then_inc(qk_done, 1)

            act.wait_ge(soft_in, 1)
            nc.scalar.activation(expd, logit, ACT.Exp).then_inc(soft_out, 1)
            for g in range(2):
                qk_out(g)
            act.wait_ge(top2_ready, 1)
            nc.scalar.activation(e2, top2, ACT.Exp).then_inc(e2_ready, 1)
            for g in range(2, 8):
                qk_out(g)
            act.wait_ge(combT_ready, 1)
            act.wait_ge(qk_ready, 8)
            nc.scalar.copy(combT, bank(4, 2)[0:NE, :]).then_inc(combT_done, 1)

            for steps in attention_steps():
                for which, step, b in steps:
                    a_bank, b_bank = (2 * b, 2 * b + 1) if which == 0 else (2 * b + 1, 2 * b)
                    if step == 0:
                        act.wait_ge(bias_ready, nth(which, b))
                        for i in range(2):
                            nc.scalar.activation(probs[:, b, i, :], bank(a_bank)[:, SEQ * i:SEQ * i + SEQ], ACT.Exp,
                                                 bias=smax[:, which, b, i:i + 1], scale=SCALE,
                                                 accum_out=ssum[:, which, b, i:i + 1]).then_inc(exp_done, 1)
                    if step == 1:
                        act.wait_ge(probsT_ready, nth(which, b))
                        nc.scalar.copy(probsT[:, b].rearrange("p k t -> p (k t)"), bank(b_bank)).then_inc(probsT_done, 1)
                    if step == 2 and which == 0:
                        act.wait_ge(context_ready, nth(0, b))
                        nc.scalar.activation(probs[:, b, 0, :], bank(a_bank)[:, 0:SEQ], ACT.Tanh,
                                             scale=vec[:, V_GATE:V_GATE + 1]).then_inc(tanh_done, 1)
                    if step == 2 and which == 1:
                        act.wait_ge(context_ready, nth(1, b))
                        act.wait_ge(slots_ready, 2)
                        act.wait_ge(combT_ready, 1)
                        nc.scalar.copy(ctxT[:, :, SEQ * b:SEQ * b + SEQ],
                                       bank(a_bank).rearrange("p (k t) -> p k t", k=DH)).then_inc(ctx_done, 1)

            def gelus(src, dst, bias_col, e, done):
                for k in range(KM):
                    last = nc.scalar.activation(dst[:, k, :], bank(src)[:, P * k:P * k + P], ACT.Gelu,
                                                bias=vec[:, bass.ds(bias_col + KM * e + k, 1)])
                last.then_inc(done, 1)

            def layer1_out(m, first_tile=False):
                e = act.value_load(owner[0:1, bass.ds(m, 1)], min_val=0, max_val=NE - 1)
                act.wait_ge(t1_ready, m + 1)
                if not first_tile:
                    act.wait_ge(l2_ready, m)
                gelus(2, h1T, V_B1, e, h1_ready)

            def layer2_out(m, first_tile=False):
                e = act.value_load(owner[0:1, bass.ds(m, 1)], min_val=0, max_val=NE - 1)
                act.wait_ge(t2_ready, m + 1)
                if not first_tile:
                    act.wait_ge(l3_ready, m)
                gelus(4, h2T, V_B2, e, h2_ready)

            act.wait_ge(owner_ready, 1)
            layer1_out(0, first_tile=True)
            layer1_out(1)
            layer2_out(0, first_tile=True)
            with act.Fori(1, MT - 1) as m:
                layer1_out(m + 1)
                layer2_out(m)
            layer2_out(MT - 1)

        @block.tensor
        def _(pe):
            pe.wait_ge(L["cst"], 16)

            def turn_tiles(phase):
                for g in range(4):
                    k, th4 = g // 2, g % 2
                    for j in range(4):
                        t = 4 * th4 + j
                        if k == 0:
                            pe.wait_ge(nrm_ready, phase * NT + t + 1)
                        last = nc.tensor.transpose(bank(g)[:, P * j:P * j + P], nrm[:, t, P * k:P * k + P], ident)
                    last.then_inc(turned, 1)

            turn_tiles(0)
            pe.wait_ge(nrmT_ready, 4)
            pe.wait_ge(L["wx"], 16)
            for cols, b, ready in ((slice(0, RANK), 0, rank_ready), (slice(RANK, RANK + 96), 6, bc_ready)):
                m = cols.stop - cols.start
                for t in range(2):
                    for k in range(DH):
                        last = nc.tensor.matmul(bank(b + t)[0:m, :], wx_sb[:, k, cols], nrmT[:, k, 512 * t:512 * t + 512],
                                                start=(k == 0), stop=(k == DH - 1))
                last.then_inc(ready, 1)
            pe.wait_ge(rank_copied, 1)
            pe.wait_ge(L["wdt"], 16)
            for k in range(DH):
                for t in range(2):
                    last = nc.tensor.matmul(bank(2 + 2 * k + t), wdt_sb[:, P * k:P * k + P],
                                            area_f[0:RANK, 512 * t:512 * t + 512], start=True, stop=True)
                last.then_inc(z_ready, 1)
            pe.wait_ge(fly_ready, 6)
            pe.wait_ge(bc_done, 2)
            for g, b in enumerate((0, 1, 6, 7)):
                nc.tensor.matmul(bank(b), hadamard, fly[:, 512 * g:512 * g + 512], start=True, stop=True).then_inc(had_ready, 1)

            def select(b, which, n):
                for t in range(2):
                    last = nc.tensor.matmul(bank(b + t), sel_w[:, bass.ds(which * NS + n, 1), :].rearrange("p s m -> p (s m)"),
                                            bc_split[:, 512 * t:512 * t + 512], start=True, stop=True)
                return last

            def up(q, c):
                for i, w in enumerate((gate_w, lin_w)):
                    for k in range(DH):
                        last = nc.tensor.matmul(bank(6)[:, QW * i:QW * i + QW], w[:, k, P * c:P * c + P],
                                                nrmT[:, k, bass.ds(q * QW, QW)], start=(k == 0), stop=(k == DH - 1))
                return last

            pe.wait_ge(L["sel"], 16)
            pe.wait_ge(L["w1"], 16)
            pe.wait_ge(L["w3"], 16)
            pe.wait_ge(hid_ready, 2)
            pe.wait_ge(bc_done, 5)
            pe.wait_ge(z_read, 4)
            pe.wait_ge(down_ready, 4)
            select(0, 0, 0).then_inc(b_ready, 1)
            select(2, 0, n_of(0, 1)).then_inc(b_ready, 1)
            select(4, 1, 0).then_inc(c_ready, 1)
            up(0, 0).then_inc(up_ready, 1)
            pe.wait_ge(up_read, 4)
            up(0, 1).then_inc(up_ready, 1)

            def ahead(q, c, n):
                return (q, c + n) if c + n < UPQ else (q + 1, c + n - UPQ)

            def unit(q, c, last_quarter):
                u = q * UPQ + c
                left = UPQ - 1 - c if last_quarter else UPQ
                if left >= 2:
                    q2, c2 = ahead(q, c, 2)
                    pe.wait_ge(scan_done, u + 3)
                    select(2 * (c2 % 2), 0, n_of(q2, c2)).then_inc(b_ready, 1)
                pe.wait_ge(hid_ready, u + 3)
                if c == 0:
                    pe.wait_ge(acc_free, q + 1)
                for k in range(DH):
                    last = nc.tensor.matmul(bank(7)[:, QW * k:QW * k + QW], down_w[:, D * c + P * k:D * c + P * k + P], hid[c % 2],
                                            start=(c == 0 and k == 0), stop=(c == UPQ - 1), skip_group_check=True)
                last.then_inc(hid_used, 1)
                if left >= 1:
                    q1, c1 = ahead(q, c, 1)
                    pe.wait_ge(yc_done, u + 1)
                    select(4, 1, n_of(q1, c1)).then_inc(c_ready, 1)
                if left >= 2:
                    pe.wait_ge(up_read, 2 * u + 6)
                    up(q2, c2).then_inc(up_ready, 1)

            with pe.Fori(0, QT_ - 1) as q:
                for c in range(UPQ):
                    unit(q, c, False)
            for c in range(UPQ):
                unit(QT_ - 1, c, True)

            for j in range(NT):
                pe.wait_ge(sumT_ready, j // 2 + 1)
                for k in range(DH):
                    last = nc.tensor.transpose(bank(j // 2)[:, D * (j % 2) + P * k:D * (j % 2) + P * k + P],
                                               yacc[:, k, P * j:P * j + P], ident)
                if j % 2:
                    last.then_inc(back_ready, 1)

            pe.wait_ge(x1_ready, NT)
            turn_tiles(1)
            pe.wait_ge(nrmT_ready, 8)
            pe.wait_ge(L["cattn"], 16)
            pe.wait_ge(v_done, 1)
            for t in range(NT):
                for k in range(DH):
                    last = nc.tensor.matmul(bank(t)[:, 0:D + NE], nrmT[:, k, P * t:P * t + P],
                                            cattn_sb[:, k, 2 * D:3 * D + NE], start=(k == 0), stop=(k == DH - 1))
                last.then_inc(v_ready, 1)

            def qk(g):
                m, t = g // 2, g % 2
                pe.wait_ge(v_done, 1 + BANK_OF_QK[g] + 1)
                if g >= 6:
                    pe.wait_ge(qk_done, g - 5)
                for k in range(DH):
                    last = nc.tensor.matmul(bank(BANK_OF_QK[g]), cattn_sb[:, k, P * m:P * m + P], nrmT[:, k, 512 * t:512 * t + 512],
                                            start=(k == 0), stop=(k == DH - 1))
                last.then_inc(qk_ready, 1)

            for g in range(5):
                qk(g)
            pe.wait_ge(mask_ready, 1)
            pe.wait_ge(L["bcst"], 16)
            tri, ones = bcst[:, B_TRI:B_TRI + P], bcst[:, B_ONE:B_ONE + P]
            pe.wait_ge(v_done, 1 + NT)
            counts, totals = bank(7)[:, 0:NT * NE], bank(7)[:, NT * NE:NT * NE + NE]
            nc.tensor.matmul(counts, tri, mask[:].rearrange("p t e -> p (t e)"), start=True, stop=False)
            for i in range(NT - 1):
                later = counts[:, NE * (i + 1):].rearrange("p (t e) -> p t e", e=NE)
                nc.tensor.matmul(later, ones, mask[:, i:i + 1, :].to_broadcast([P, NT - 1 - i, NE]),
                                 start=False, stop=(i == NT - 2))
            for i in range(NT):
                last = nc.tensor.matmul(totals, ones, mask[:, i, :], start=(i == 0), stop=(i == NT - 1))
            last.then_inc(prefix_ready, 1)
            for g in range(5, 8):
                qk(g)
            pe.wait_ge(comb_ready, 1)
            pe.wait_ge(qk_done, 6)
            for t in range(NT):
                last = nc.tensor.transpose(bank(4, 2)[0:NE, P * t:P * t + P], comb[:, t, :], ident)
            last.then_inc(combT_ready, 1)

            pe.wait_ge(qk_done, 8)
            for steps in attention_steps():
                for which, step, b in steps:
                    a, o = (bank(2 * b), bank(2 * b + 1)) if which == 0 else (bank(2 * b + 1), bank(2 * b))
                    tokens = slice(SEQ * b, SEQ * b + SEQ)
                    if step == 0:
                        if which == 0 and b == 2:
                            pe.wait_ge(combT_done, 1)
                        if which == 0 and b == 3:
                            pe.wait_ge(slots_ready, 1)
                        if which:
                            pe.wait_ge(query_done, b + 1)
                        for i in range(2):
                            own = slice(SEQ * b + P * i, SEQ * b + P * i + P)
                            for k in range(which + 1):
                                last = nc.tensor.matmul(a[:, SEQ * i:SEQ * i + SEQ], qT[:, k, own], kT[:, k, tokens],
                                                        start=(k == 0), stop=(k == which))
                        last.then_inc(scores_ready, 1)
                    if step == 1:
                        pe.wait_ge(probs_ready, nth(which, b))
                        for i in range(2):
                            for k in range(2):
                                last = nc.tensor.transpose(o[:, SEQ * k + P * i:SEQ * k + P * i + P],
                                                           probs[:, b, i, P * k:P * k + P], ident)
                        last.then_inc(probsT_ready, 1)
                    if step == 2:
                        pe.wait_ge(probsT_done, nth(which, b))
                        for h in range(which + 1):
                            for k in range(2):
                                last = nc.tensor.matmul(a[:, SEQ * h:SEQ * h + SEQ], val[:, 2 * b + k, P * h:P * h + P],
                                                        probsT[:, b, k, :], start=(k == 0), stop=(k == 1))
                        last.then_inc(context_ready, 1)

            def turn_x(m):
                pe.wait_ge(x_loaded, 16 * m + 16)
                for k in range(DH):
                    last = nc.tensor.transpose(bank(0)[:, P * k:P * k + P], xin[:, P * k:P * k + P], ident)
                last.then_inc(x_turned, 1)

            def expert_of(m):
                return pe.value_load(owner[0:1, bass.ds(m, 1)], min_val=0, max_val=NE - 1)

            def layer1(m):
                e = expert_of(m)
                pe.wait_ge(xT_ready, m + 1)
                for k in range(DH):
                    last = nc.tensor.matmul(bank(1), xT[:, k, :], moe_w1[:, bass.ds(e, 1), k, :].rearrange("p e n -> p (e n)"),
                                            start=(k == 0), stop=(k == DH - 1))
                last.then_inc(l1_ready, 1)

            def turn(src, dst, need, ready, m):
                pe.wait_ge(need, m + 1)
                for k in range(KM):
                    last = nc.tensor.transpose(bank(dst)[:, P * k:P * k + P], src[:, P * k:P * k + P], ident)
                last.then_inc(ready, 1)

            def layer2(m):
                e = expert_of(m)
                pe.wait_ge(h1_ready, m + 1)
                for k in range(KM):
                    last = nc.tensor.matmul(bank(3), h1T[:, k, :], moe_w2[:, bass.ds(e, 1), k, :].rearrange("p e n -> p (e n)"),
                                            start=(k == 0), stop=(k == KM - 1))
                last.then_inc(l2_ready, 1)

            def layer3(m):
                e = expert_of(m)
                pe.wait_ge(h2_ready, m + 1)
                pe.wait_ge(y_ready, m + 1)
                for k in range(KM):
                    last = nc.tensor.matmul(bank(5)[:, 0:D], h2T[:, k, :], moe_w3[:, bass.ds(e, 1), k, :].rearrange("p e n -> p (e n)"),
                                            start=(k == 0), stop=(k == KM - 1))
                last.then_inc(l3_ready, 1)

            def loaded(*names):
                for n in names:
                    pe.wait_ge(L[n], 16 * {"mw1": 6, "mw2": 6, "mw1_late": 2, "mw3": NE, "mw2_late": 2}[n])

            def expert_step(m, first_tile=False, left=MT):
                layer2(m)
                if left >= 1:
                    turn(raw1, 2, r1_ready, t1_ready, m + 1)
                if not first_tile:
                    layer3(m - 1)
                if left >= 2:
                    layer1(m + 2)
                turn(raw2, 4, r2_ready, t2_ready, m)
                if left >= 3:
                    turn_x(m + 3)

            pe.wait_ge(owner_ready, 1)
            turn_x(0)
            loaded("mw1", "mw1_late")
            pe.wait_ge(ctx_done, 1)
            layer1(0)
            turn_x(1)
            pe.wait_ge(ctx_done, 2)
            turn(raw1, 2, r1_ready, t1_ready, 0)
            layer1(1)
            turn_x(2)
            loaded("mw2", "mw2_late")
            expert_step(0, first_tile=True)
            loaded("mw3")
            pe.wait_ge(ctx_done, BATCH)
            with pe.Fori(1, MT - 3) as m:
                expert_step(m)
            for left in (2, 1, 0):
                expert_step(MT - 1 - left, left=left)
            layer3(MT - 1)

            pe.wait_ge(L["cproj"], 16)
            pe.wait_ge(L["b3"], 16)
            pe.wait_ge(y_ready, MT + 1)
            for t in range(NT):
                o = bank(t)[:, 0:D]
                for k in range(DH):
                    nc.tensor.matmul(o, ctxT[:, k, P * t:P * t + P], cproj_sb[:, k, :], start=(k == 0), stop=False)
                nc.tensor.matmul(o, combT[:, P * t:P * t + P], b3_sb, start=False, stop=True).then_inc(proj_ready, 1)

        @block.vector
        def _(dve):
            chain = [0]

            def link(ins):
                chain[0] += 1
                ins.then_inc(dve_chain, 1)
                dve.wait_ge(dve_chain, chain[0])

            def statistics(t):
                link(nc.vector.bn_stats(st6[:, t, :], res[:, t, :]))
                nc.vector.bn_aggr(mv[:, t, :], st6[:, t, :]).then_inc(dve_chain, 1)
                chain[0] += 1

            def normalise(phase):
                dve.wait_ge(dve_chain, chain[0])
                nc.vector.tensor_scalar(ln_v[:], mv[:, :, 1], EPS, None, ALU.add).then_inc(var_ready, 1)
                dve.wait_ge(sqrt_ready, phase + 1)
                link(nc.vector.reciprocal(ln_r[:], ln_s[:]))
                link(nc.vector.tensor_tensor(ln_t[:], ln_r[:], ln_r[:], ALU.mult))
                link(nc.vector.tensor_tensor(ln_t[:], ln_t[:], ln_v[:], ALU.mult))
                link(nc.vector.tensor_scalar(ln_t[:], ln_t[:], -0.5, 1.5, ALU.mult, ALU.add))
                link(nc.vector.tensor_tensor(ln_r[:], ln_r[:], ln_t[:], ALU.mult))
                for t in range(NT):
                    nc.vector.tensor_scalar(nrm[:, t, :], res[:, t, :], mv[:, t, 0:1], ln_r[:, t:t + 1],
                                            ALU.subtract, ALU.mult).then_inc(nrm_ready, 1)

            dve.wait_ge(L["vec"], 16)
            nc.vector.tensor_copy(cattn_sb[:, :, 3 * D:3 * D + NE],
                                  vec[:, V_WG:V_WG + DH * NE].rearrange("p (k e) -> p k e", k=DH)).then_inc(v_done, 1)
            nc.vector.scalar_tensor_tensor(lw[:, 0:1], vec[:, V_W1:V_W1 + 1], 0.5, vec[:, V_W0:V_W0 + 1],
                                           ALU.mult, ALU.add).then_inc(z2_ready, 1)
            dve.wait_ge(lw_ready, 1)
            nc.vector.tensor_scalar(lw[:, 1:2], lw[:, 1:2], 0.5, 0.5, ALU.mult, ALU.add).then_inc(lw_ready, 1)
            for t in range(NT):
                if t == 0:
                    dve.wait_ge(L["x"], 16)
                if t == 4:
                    dve.wait_ge(L["x2"], 16)
                statistics(t)
            normalise(0)
            for g in (1, 3):
                dve.wait_ge(turned, g + 1)
                nc.vector.tensor_copy(nrmT[:, g // 2, 512:1024], bank(g)).then_inc(nrmT_ready, 1)
            v = bank(6, 2)
            dve.wait_ge(bc_ready, 1)
            nc.vector.tensor_copy(bc_split[0:96, :], v[0:96, :]).then_inc(bc_done, 1)
            dve.wait_ge(bc_done, 1)
            nc.vector.tensor_tensor(area_e[0:96, 0:TOK], v[0:96, :], bc_split[0:96, :], ALU.subtract).then_inc(bc_done, 1)
            dve.wait_ge(bc_done, 2)
            nc.vector.tensor_copy(bc_split[32:64, :], area_e[32:64, 0:TOK]).then_inc(bc_done, 1)
            nc.vector.tensor_copy(bc_split[64:96, :], area_e[64:96, 0:TOK]).then_inc(bc_done, 1)
            dve.wait_ge(bc_done, 4)
            link(nc.vector.tensor_tensor(area_e[64:96, 0:TOK], area_e[64:96, 0:TOK], bc_split[64:96, :], ALU.subtract))
            nc.vector.tensor_copy(bc_split[64:96, :], area_e[64:96, 0:TOK]).then_inc(bc_done, 1)
            dve.wait_ge(L["vec"], 16)
            for k in range(DH):
                dve.wait_ge(z_ready, k + 1)
                dve.wait_ge(z_read, 2)
                nc.vector.tensor_scalar(delta[:, k, :], bank(2 + 2 * k, 2), vec[:, V_BDT + k:V_BDT + k + 1], 0.0,
                                        ALU.add, ALU.max).then_inc(z_read, 1)
            dve.wait_ge(absexp_done, 1)
            u1, e = loan2[:, 0:2048], area_g
            link(nc.vector.tensor_scalar(u1, e[:], 1.0, None, ALU.add))
            nc.vector.scalar_tensor_tensor(e[:], u1, -1.0, e[:], ALU.add, ALU.subtract).then_inc(onepl_done, 1)
            nc.vector.memset(decay.rearrange("p i (b t) -> p (i b) t", b=BATCH)[:, :, 0:1], 0.0).then_inc(decay_zero, 1)
            dve.wait_ge(onepl_done, 1)
            dve.wait_ge(z_read, 4)
            link(nc.vector.tensor_tensor(area_d[:], area_d[:], e[:], ALU.subtract))
            dve.wait_ge(log_done, 1)
            nc.vector.tensor_tensor(area_d[:], area_d[:], u1, ALU.add).then_inc(delta_ready, 1)
            dve.wait_ge(delta_ready, 1)
            dve.wait_ge(nrmT_ready, 4)
            link(nc.vector.tensor_tensor(area_e[:], area_d[:], nrmT[:].rearrange("p k t -> p (k t)"), ALU.mult))

            def product(q, c):
                u = q * UPQ + c
                dve.wait_ge(b_ready, u + 1)
                b = bank(2 * (c % 2), 2)
                nc.vector.tensor_tensor(b, du[:, c % DH, :], b, ALU.mult).then_inc(bx_done, 1)

            nc.vector.memset(ln_t[:, 0:1], 0.0).then_inc(scan_done, 2)
            nc.vector.memset(ln_t[:, 1:2], 0.0).then_inc(hid_used, 2)
            nc.vector.memset(ln_t[:, 2:3], 0.0).then_inc(up_read, 2)
            nc.vector.memset(ln_t[:, 3:4], 0.0).then_inc(acc_free, 1)
            product(0, 0)

            def unit(q, c, last_quarter):
                u = q * UPQ + c
                dve.wait_ge(bx_done, u + 1)
                dve.wait_ge(decay_ready, u + 1)
                dve.wait_ge(y_added, u + 1)
                nc.vector.tensor_tensor_scan(state[:, c % 2, :], decay[:, c % 2, :], bank(2 * (c % 2), 2), 0.0,
                                             ALU.mult, ALU.add).then_inc(scan_done, 1)
                if not (last_quarter and c == UPQ - 1):
                    product(*((q, c + 1) if c + 1 < UPQ else (q + 1, 0)))
                dve.wait_ge(scan_done, u + 3)
                dve.wait_ge(c_ready, u + 1)
                nc.vector.tensor_tensor(state[:, c % 2, :], state[:, c % 2, :], bank(4, 2), ALU.mult).then_inc(yc_done, 1)

            with dve.Fori(0, QT_ - 1) as q:
                for c in range(UPQ):
                    unit(q, c, False)
            for c in range(UPQ):
                unit(QT_ - 1, c, True)

            for g in range(4):
                dve.wait_ge(back_ready, g + 1)
                nc.vector.tensor_tensor(res[:, 2 * g:2 * g + 2, :].rearrange("p t d -> p (t d)"),
                                        res[:, 2 * g:2 * g + 2, :].rearrange("p t d -> p (t d)"), bank(g), ALU.add).then_inc(x1_ready, 2)

            dve.wait_ge(x1_ready, NT)
            for t in range(NT):
                statistics(t)
            normalise(1)
            for g in (1, 3):
                dve.wait_ge(turned, 4 + g + 1)
                nc.vector.tensor_copy(nrmT[:, g // 2, 512:1024], bank(g)).then_inc(nrmT_ready, 1)

            dve.wait_ge(L["row"], 16)
            wide = lambda a: a.unsqueeze(2).to_broadcast([P, NT, NE])
            over_tiles = lambda a: a.unsqueeze(1).to_broadcast([P, NT, NE])
            key = over_tiles(cst[:, C_KEY:C_KEY + NE])
            for t in range(NT):
                dve.wait_ge(v_ready, t + 1)
                nc.vector.tensor_tensor(logit[:, t, :], bank(t)[:, D:D + NE], row[:, R_BG:R_BG + NE],
                                        ALU.add).then_inc(dve_chain, 1)
                chain[0] += 1
                nc.vector.tensor_tensor(val[:, t, :], bank(t)[:, 0:D], row[:, R_VB:R_VB + D], ALU.add).then_inc(v_done, 1)
            dve.wait_ge(dve_chain, chain[0])
            link(nc.vector.tensor_reduce(top, logit, AX.X, ALU.max))
            link(nc.vector.tensor_tensor(logit, logit, wide(top), ALU.subtract))
            nc.vector.tensor_scalar(first, logit, 0.0, None, ALU.is_equal).then_inc(soft_in, 1)
            dve.wait_ge(soft_in, 1)

            def lowest(choice):
                link(nc.vector.tensor_tensor(keyed, choice, key, ALU.mult))
                link(nc.vector.tensor_reduce(keymax, keyed, AX.X, ALU.max))
                link(nc.vector.tensor_tensor(choice, keyed, wide(keymax), ALU.is_equal))

            lowest(first)
            dve.wait_ge(soft_out, 1)
            link(nc.vector.scalar_tensor_tensor(logit, first, -1e30, logit, ALU.mult, ALU.add))
            nc.vector.tensor_reduce(top2, logit, AX.X, ALU.max).then_inc(top2_ready, 1)
            dve.wait_ge(top2_ready, 1)
            link(nc.vector.tensor_tensor(second, logit, wide(top2), ALU.is_equal))
            lowest(second)
            nc.vector.tensor_tensor(mask[:], first, second, ALU.add).then_inc(mask_ready, 1)
            link(nc.vector.tensor_reduce(esum, expd, AX.X, ALU.add))
            link(nc.vector.reciprocal(gain[:, 0, :], esum))
            dve.wait_ge(e2_ready, 1)
            link(nc.vector.tensor_tensor(gain[:, 1, :], gain[:, 0, :], e2, ALU.mult))
            link(nc.vector.tensor_tensor(comb, first, wide(gain[:, 0, :]), ALU.mult))
            link(nc.vector.tensor_tensor(tmp64, second, wide(gain[:, 1, :]), ALU.mult))
            nc.vector.tensor_tensor(comb, comb, tmp64, ALU.add).then_inc(comb_ready, 1)
            dve.wait_ge(prefix_ready, 1)
            dve.wait_ge(comb_ready, 1)
            link(nc.vector.tensor_scalar(tile_int, bank(7)[:, NT * NE:NT * NE + NE], float(P - 1), None, ALU.add))
            link(nc.vector.tensor_scalar(tile_int, tile_int, 7, None, ALU.logical_shift_right))
            link(nc.vector.tensor_copy(tiles8, tile_int))
            link(nc.vector.tensor_scalar(ones8, tiles8, 0.0, None, ALU.is_ge))
            link(nc.vector.tensor_tensor_scan(upto8, ones8, tiles8, 0.0, ALU.mult, ALU.add))
            link(nc.vector.tensor_tensor(base8, upto8, tiles8, ALU.subtract))
            link(nc.vector.tensor_scalar(base8, base8, float(P), None, ALU.mult))
            link(nc.vector.tensor_tensor(place, bank(7)[:, 0:NT * NE].rearrange("p (t e) -> p t e", e=NE),
                                         over_tiles(base8), ALU.add))
            for k, choice in enumerate((first, second)):
                link(nc.vector.tensor_tensor(tmp64, choice, place, ALU.mult))
                link(nc.vector.tensor_reduce(slotf, tmp64, AX.X, ALU.add))
                ins = nc.vector.tensor_copy(slot[:, k, :], slotf)
                if k == 0:
                    link(ins)
                else:
                    ins.then_inc(slots_ready, 1)
            link(nc.vector.tensor_tensor(hits, upto8.unsqueeze(1).to_broadcast([P, MT, NE]),
                                         cst[:, C_TILE:C_TILE + MT].unsqueeze(2).to_broadcast([P, MT, NE]), ALU.is_le))
            link(nc.vector.tensor_reduce(owner_f, hits, AX.X, ALU.add))
            link(nc.vector.tensor_scalar(owner_f, owner_f, float(NE - 1), None, ALU.min))
            nc.vector.tensor_copy(owner[:], owner_f).then_inc(owner_ready, 1)
            dve.wait_ge(owner_ready, 1)
            nc.vector.memset(ln_t[:, 4:5], 0.0).then_inc(slots_ready, 1)

            for steps in attention_steps():
                for which, step, b in steps:
                    if step == 0:
                        src = bank(2 * b + which).rearrange("p (i t) -> p i t", i=2)
                        dve.wait_ge(scores_ready, nth(which, b))
                        link(nc.vector.tensor_reduce(smax[:, which, b, :], src, AX.X, ALU.max))
                        nc.vector.tensor_scalar(smax[:, which, b, :], smax[:, which, b, :], -SCALE, None,
                                                ALU.mult).then_inc(bias_ready, 1)
                for which, step, b in steps:
                    if step == 0:
                        dve.wait_ge(exp_done, 2 * nth(which, b))
                        link(nc.vector.reciprocal(sinv[:, which, b, :], ssum[:, which, b, :]))
                        for i in range(2):
                            ins = nc.vector.tensor_scalar(probs[:, b, i, :], probs[:, b, i, :], sinv[:, which, b, i:i + 1], None,
                                                          ALU.mult)
                        ins.then_inc(probs_ready, 1)
                for which, step, b in steps:
                    if step == 2 and which == 0:
                        dve.wait_ge(tanh_done, b + 1)
                        q0 = qT[:, 0, SEQ * b:SEQ * b + SEQ]
                        nc.vector.scalar_tensor_tensor(q0, probs[:, b, 0, :], lw[:, 1:2], q0, ALU.mult, ALU.add).then_inc(query_done, 1)

            nc.vector.memset(ln_t[:, 5:6], 0.0).then_inc(y_ready, 1)
            nc.vector.memset(ln_t[:, 6:7], 0.0).then_inc(y_stored, 16)

            def x_out(m, first_tile):
                dve.wait_ge(x_turned, m + 1)
                if not first_tile:
                    dve.wait_ge(l1_ready, m)
                nc.vector.tensor_copy(xT.rearrange("p k t -> p (k t)"), bank(0)[:, 0:D]).then_inc(xT_ready, 1)

            def raw_out(dst, src, product, used, done, m, first_tile):
                dve.wait_ge(product, m + 1)
                if not first_tile:
                    dve.wait_ge(used, m)
                nc.vector.tensor_copy(dst, bank(src)).then_inc(done, 1)

            def y_out(m):
                dve.wait_ge(l3_ready, m + 1)
                dve.wait_ge(y_stored, 16 * m + 16)
                nc.vector.tensor_copy(yout, bank(5)[:, 0:D]).then_inc(y_ready, 1)

            def expert_step(m, first_tile=False, left=MT):
                raw_out(raw2, 3, l2_ready, t2_ready, r2_ready, m, first_tile)
                if not first_tile:
                    y_out(m - 1)
                if left >= 2:
                    raw_out(raw1, 1, l1_ready, t1_ready, r1_ready, m + 2, False)
                if left >= 3:
                    x_out(m + 3, False)

            x_out(0, True)
            raw_out(raw1, 1, l1_ready, t1_ready, r1_ready, 0, True)
            x_out(1, False)
            raw_out(raw1, 1, l1_ready, t1_ready, r1_ready, 1, False)
            x_out(2, False)
            expert_step(0, first_tile=True)
            with dve.Fori(1, MT - 3) as m:
                expert_step(m)
            for left in (2, 1, 0):
                expert_step(MT - 1 - left, left=left)
            y_out(MT - 1)

            pb = row[:, R_PB:R_PB + D]
            for t in range(NT):
                link(nc.vector.tensor_tensor(res[:, t, :], res[:, t, :], pb, ALU.add))
                dve.wait_ge(proj_ready, t + 1)
                link(nc.vector.tensor_tensor(res[:, t, :], res[:, t, :], bank(t)[:, 0:D], ALU.add))
            for t in range(NT):
                dve.wait_ge(picked_ready[t], 32)
                link(nc.vector.scalar_tensor_tensor(res[:, t, :], picked[0][:, t, :], gain[:, 0, t:t + 1], res[:, t, :],
                                                    ALU.mult, ALU.add))
                nc.vector.scalar_tensor_tensor(res[:, t, :], picked[1][:, t, :], gain[:, 1, t:t + 1], res[:, t, :],
                                               ALU.mult, ALU.add).then_inc(out_ready, 1)


def _layouts(v):
    import numpy as np

    f = lambda n: np.ascontiguousarray(v[n])
    wx = f("L0_attn_W_x")
    bc = wx[RANK:].T
    cols = lambda a: a.reshape(-1, P).T
    attn_b = f("L1_attn_c_attn_b")
    one = lambda n: np.broadcast_to(f(n).reshape(1, 1), (P, 1))
    vecs = np.concatenate([
        cols(f("L0_attn_b_dt")), cols(f("L0_attn_D")),
        f("L0_attn_A_log").reshape(DH, P, NS).transpose(1, 0, 2).reshape(P, DH * NS),
        cols(attn_b[:2 * D]), f("L1_attn_cam_gate").reshape(P, 1), one("L1_attn_cam_w0"), one("L1_attn_cam_w1"),
        cols(f("L1_ffn_b1").reshape(-1)), cols(f("L1_ffn_b2").reshape(-1)),
        f("L1_ffn_Wg").reshape(DH, P, NE).transpose(1, 0, 2).reshape(P, DH * NE)], axis=1)
    rows = np.concatenate([attn_b[2 * D:], f("L1_attn_c_proj_b"), f("L1_ffn_bg")])
    had = np.ones((1, 1), np.float32)
    while had.shape[0] < P:
        had = np.block([[had, had], [had, -had]])
    consts = np.concatenate([np.eye(P), had, np.broadcast_to(np.arange(NE, 0, -1), (P, NE)),
                             np.broadcast_to(np.arange(MT), (P, MT))], axis=1).astype(np.float32)
    one_bf16 = 0x3F80
    bconsts = (np.concatenate([np.triu(np.ones((P, P)), 1), np.ones((P, P))], axis=1) * one_bf16).astype(np.uint16)
    sel = np.zeros((P, 2 * NS, P), np.uint16)
    for s in range(2 * NS):
        for part in range(3):
            sel[32 * part + s, s, :] = one_bf16
    return {
        "x": f("L0_attn_x").reshape(TOK, D), "wx": np.concatenate([wx[:RANK].T, bc, bc, bc], axis=1),
        "wdt": f("L0_attn_W_dt").T, "w1": f("L0_ffn_W1").T, "w3": f("L0_ffn_W3").T, "w2": f("L0_ffn_W2").T,
        "vecs": vecs, "rows": np.broadcast_to(rows[None], (P, R_END)), "consts": consts, "bconsts": bconsts,
        "sel": sel.reshape(P, -1), "cattn": f("L1_attn_c_attn_w"), "cproj": f("L1_attn_c_proj_w"),
        "mw1": f("L1_ffn_W1"), "mw2": f("L1_ffn_W2"), "mw3": f("L1_ffn_W3"), "b3": f("L1_ffn_b3"),
        "zeros": np.zeros((MT * P, D), np.float32),
    }


def kernel(**inputs):
    import numpy as np
    import concourse.bacc as bacc
    from concourse.bass_utils import run_bass_kernel_spmd

    nc = bacc.Bacc("TRN2", target_bir_lowering=False, num_devices=1)
    arrays = {f"in_{n}": np.ascontiguousarray(a) for n, a in _layouts(inputs).items()}
    args = [nc.dram_tensor(n, a.shape, mybir.dt.from_np(a.dtype), kind="ExternalInput").ap() for n, a in arrays.items()]
    result = nc.dram_tensor("out_0", (TOK, D), F32, kind="ExternalOutput").ap()
    build(nc, *args, result)
    got = run_bass_kernel_spmd(nc, [arrays], core_ids=[0]).results[0]["out_0"]
    return got.reshape(BATCH, SEQ, D)
```

```python
from contextlib import ExitStack

import concourse.bass as bass
from concourse import mybir

F32 = mybir.dt.float32
BF16 = mybir.dt.bfloat16
I32 = mybir.dt.int32
U32 = mybir.dt.uint32
ALU = mybir.AluOpType
ACT = mybir.ActivationFunctionType
AX = mybir.AxisListType

P = 128
BATCH, SEQ, D = 4, 256, 256
TOK = BATCH * SEQ
NT = TOK // P
DH = D // P
NS, RANK = 16, 64
H0 = 1024
HC = H0 // P
QT_ = 4
QW = TOK // QT_
UNITS = NS * DH
UPQ = UNITS // QT_
NE, HM = 8, 512
KM = HM // P
MT = 2 * NT + NE - 1
BANK_OF_QK = (0, 1, 2, 3, 4, 5, 0, 1)
EPS = 1e-5
SCALE = 0.25

V_BDT, V_D, V_ALOG, V_QKB, V_GATE, V_W0, V_W1, V_B1, V_B2, V_WG, V_END = (
    0, 2, 4, 36, 40, 41, 42, 43, 75, 107, 123)
R_VB, R_PB, R_BG, R_END = 0, 256, 512, 520
C_ID, C_HAD, C_KEY, C_TILE, C_END = 0, 128, 256, 264, 264 + MT
B_TRI, B_ONE, B_END = 0, 128, 256


def build(nc, x, wx, wdt, w1, w3, w2, vecs, rows, consts, bconsts, sel, cattn, cproj,
          mw1, mw2, mw3, b3, zeros, home_of, no_home, out):
    assert UPQ == HC and UNITS == QT_ * UPQ

    with ExitStack() as ctx:
        def sb(name, shape, dt=F32):
            return ctx.enter_context(nc.sbuf_tensor(name, shape, dt))

        def sem(name):
            return ctx.enter_context(nc.semaphore(name))

        moe_w1 = sb("moe_w1", [P, NE, 2, HM])
        moe_w2 = sb("moe_w2", [P, NE, KM, HM])
        moe_w3 = sb("moe_w3", [P, NE, KM, D])
        loan3 = moe_w3[:].rearrange("p e k n -> p (e k n)")
        gate_w = loan3[:, 0:2048].rearrange("p (k h) -> p k h", k=DH)
        lin_w = loan3[:, 2048:4096].rearrange("p (k h) -> p k h", k=DH)
        down_w = loan3[:, 4096:6144]
        sel_w = loan3[:, 6144:8192].bitcast(BF16).rearrange("p (s m) -> p s m", m=P)
        loan2 = moe_w2[:, 6:8].rearrange("p e k n -> p (e k n)")
        ffn_out = loan2[:, 0:2048].rearrange("p (k t) -> p k t", k=DH)
        fly = loan2[:, 2048:4096]
        loan1 = moe_w1[:, 6:8].rearrange("p e k n -> p (e k n)")
        gl = [loan1[:, 512 * i:512 * i + 512] for i in range(2)]
        th = [loan1[:, 1024 + QW * i:1024 + QW * i + QW] for i in range(2)]
        hid = [loan1[:, 1536 + QW * i:1536 + QW * i + QW] for i in range(2)]

        res = sb("res", [P, NT, D])
        nrmT = sb("nrmT", [P, DH, TOK])
        area_c = sb("area_c", [P, 2048])
        nrm = area_c[:].rearrange("p (t d) -> p t d", t=NT)
        yacc = area_c[:].rearrange("p (k t) -> p k t", k=DH)
        area_d = sb("area_d", [P, 2048])
        delta = area_d[:].rearrange("p (k t) -> p k t", k=DH)
        qT = area_d[:].rearrange("p (k t) -> p k t", k=DH)
        area_e = sb("area_e", [P, 2048])
        du = area_e[:].rearrange("p (k t) -> p k t", k=DH)
        kT = area_e[:].rearrange("p (k t) -> p k t", k=DH)
        area_f = sb("area_f", [P, 2048])
        decay = area_f[:].rearrange("p (i t) -> p i t", i=2)
        val = area_f[:].rearrange("p (t d) -> p t d", t=NT)
        area_g = sb("area_g", [P, 2048])
        state = area_g[:].rearrange("p (i t) -> p i t", i=2)
        ctxT = area_g[:].rearrange("p (k t) -> p k t", k=DH)
        area_h = sb("area_h", [P, 2048])
        bc_split = area_h[:, 0:512].bitcast(BF16)
        wx_sb = area_h[:, 512:832].rearrange("p (k m) -> p k m", k=DH)
        wdt_sb = area_h[0:RANK, 832:1088]
        cattn_sb = sb("cattn_sb", [P, DH, 3 * D + NE])
        cproj_sb = sb("cproj_sb", [P, DH, D])
        vec = sb("vec", [P, V_END])
        row = sb("row", [P, R_END])
        cst = sb("cst", [P, C_END])
        bcst = sb("bcst", [P, B_END], BF16)
        ident = cst[:, C_ID:C_ID + P]
        hadamard = cst[:, C_HAD:C_HAD + P]
        amat = sb("amat", [P, 2 * NS])
        st6 = sb("st6", [P, NT, 6])
        mv = sb("mv", [P, NT, 2])
        ln_v = sb("ln_v", [P, NT])
        ln_s = sb("ln_s", [P, NT])
        ln_r = sb("ln_r", [P, NT])
        ln_t = sb("ln_t", [P, NT])

        gw = [area_g[:, 64 * i:64 * i + 64].rearrange("p (t e) -> p t e", e=NE) for i in range(7)]
        logit, expd, first, second, keyed, place, tmp64 = gw
        hits = area_g[:, 512:512 + MT * NE].rearrange("p (m e) -> p m e", e=NE)
        g8 = [area_g[:, 768 + 8 * i:776 + 8 * i] for i in range(10)]
        top, esum, keymax, top2, e2, ones8, tiles8, upto8, base8, slotf = g8
        tile_int = area_g[:, 860:868].bitcast(I32)
        owner_f = area_g[:, 872:872 + MT]
        mask = sb("mask", [P, NT, NE], BF16)
        slot = sb("slot", [P, 2, NT], U32)
        home_slot = sb("home_slot", [P, 2, NT], U32)
        owner = sb("owner", [P, MT], I32)
        lw = sb("lw", [P, 2])
        probs = area_h[:].rearrange("p (b i t) -> p b i t", b=BATCH, i=2)
        probsT = nrmT[:].rearrange("p k t -> p (k t)").rearrange("p (b k t) -> p b k t", b=BATCH, k=2)
        smax = sb("smax", [P, 2, BATCH, 2])
        ssum = sb("ssum", [P, 2, BATCH, 2])
        sinv = sb("sinv", [P, 2, BATCH, 2])
        home_sb = sb("home_sb", [P, 2 * NT, 2], I32)
        gain = home_sb[:].bitcast(F32).rearrange("p (k t) two -> p k t two", k=2)[:, :, :, 1]
        homes = sb("homes_sb", [P, 2 * MT], I32)
        home_gain = homes[:].bitcast(F32)
        home = sb("home", [P, 1], I32)
        home_seen = sb("home_seen", [P, 1], I32)
        xin = sb("xin", [P, D])[:]
        xT = sb("xT", [P, D])[:].rearrange("p (k t) -> p k t", k=DH)
        raw1 = area_d[:, 512:1024]
        raw2 = area_d[:, 1024:1536]
        yraw = area_d[:, 1536:1792]
        yout = area_d[:, 1792:2048]
        b3_sb = area_h[:].rearrange("p (e d) -> p e d", e=NE)
        h1T = area_e[:, 0:512].rearrange("p (k t) -> p k t", k=KM)
        h2T = area_e[:, 512:1024].rearrange("p (k t) -> p k t", k=KM)
        xbuf = nc.dram_tensor("dispatched", (MT * P, D), F32, kind="Internal").ap()
        home_buf = nc.dram_tensor("homes", (P * MT, 2), I32, kind="Internal").ap()
        sums = nc.dram_tensor("sums", (TOK + MT * P, D), F32, kind="Internal").ap()

        psum = ctx.enter_context(nc.psum_tensor("psum", [P, 8, 512], F32))

        def bank(i, n=1):
            return psum[:, i:i + n, :].rearrange("p b n -> p (b n)")

        L = {n: sem(f"load_{n}") for n in ("x", "x2", "wx", "wdt", "w1", "w3", "w2", "vec", "row", "cst", "bcst", "sel",
                                           "cattn", "cproj", "zero", "mw1", "mw2", "mw1_late", "mw2_late", "mw3", "b3", "home", "no_home", "zero_sums")}
        dve_chain, act_chain, pool_chain = sem("dve_chain"), sem("act_chain"), sem("pool_chain")
        out_done = sem("out_done")
        stats_done = sem("stats_done")
        var_ready, sqrt_ready, nrm_ready, nrmT_ready = (
            sem("var_ready"), sem("sqrt_ready"), sem("nrm_ready"), sem("nrmT_ready"))
        turned = sem("turned")
        fly_ready, had_ready, down_ready = sem("fly_ready"), sem("had_ready"), sem("down_ready")
        rank_ready, rank_copied, bc_ready, bc_done = sem("rank_ready"), sem("rank_copied"), sem("bc_ready"), sem("bc_done")
        z_ready, absexp_done, onepl_done, log_done, amat_ready, delta_ready, z_read = (
            sem("z_ready"), sem("absexp_done"), sem("onepl_done"), sem("log_done"), sem("amat_ready"),
            sem("delta_ready"), sem("z_read"))
        decay_zero, less_lost = sem("decay_zero"), sem("less_lost")
        b_ready, c_ready, decay_ready = sem("b_ready"), sem("c_ready"), sem("decay_ready")
        bx_done, scan_done, yc_done, y_added = sem("bx_done"), sem("scan_done"), sem("yc_done"), sem("y_added")
        up_ready, up_read, th_ready, prod_done, hid_ready, hid_used, acc_free = (
            sem("up_ready"), sem("up_read"), sem("th_ready"), sem("prod_done"), sem("hid_ready"), sem("hid_used"),
            sem("acc_free"))
        sumT_ready, late_sumT_ready, back_ready, x1_ready = sem("sumT_ready"), sem("late_sumT_ready"), sem("back_ready"), sem("x1_ready")

        z2_ready, lw_ready = sem("z2_ready"), sem("lw_ready")
        logits_ready, soft_in, soft_out, top2_ready, e2_ready, mask_ready, prefix_ready, slots_ready = (
            sem("logits_ready"), sem("soft_in"), sem("soft_out"), sem("top2_ready"), sem("e2_ready"),
            sem("mask_ready"), sem("prefix_ready"), sem("slots_ready"))
        owner_ready = sem("owner_ready")
        scattered, homes_scattered, homes_loaded, home_ready, home_read = sem("scattered"), sem("homes_scattered"), sem("homes_loaded"), sem("home_ready"), sem("home_read")
        bias_added, proj_added = sem("bias_added"), sem("proj_added")
        qk_ready, qk_done, v_ready, v_done = sem("qk_ready"), sem("qk_done"), sem("v_ready"), sem("v_done")
        scores_ready, bias_ready, exp_done, probs_ready, probsT_ready, probsT_done = (
            sem("scores_ready"), sem("bias_ready"), sem("exp_done"), sem("probs_ready"), sem("probsT_ready"),
            sem("probsT_done"))
        context_ready, tanh_done, query_done, ctx_done = (
            sem("context_ready"), sem("tanh_done"), sem("query_done"), sem("ctx_done"))
        x_loaded, x_turned, xT_ready, l1_ready, r1_ready, t1_ready, h1_ready = (
            sem("x_loaded"), sem("x_turned"), sem("xT_ready"), sem("l1_ready"), sem("r1_ready"), sem("t1_ready"),
            sem("h1_ready"))
        l2_ready, r2_ready, t2_ready, h2_ready, l3_ready, y_ready, y_stored = (
            sem("l2_ready"), sem("r2_ready"), sem("t2_ready"), sem("h2_ready"), sem("l3_ready"), sem("y_ready"),
            sem("y_stored"))
        y_read, proj_ready, sums_ready = sem("y_read"), sem("proj_ready"), sem("sums_ready")

        block = ctx.enter_context(nc.Block())

        def attention_steps():
            return [[(s // 3, s % 3, b) for b in range(BATCH) for s in [d - b // 2] if 0 <= s < 6]
                    for d in range(BATCH // 2 + 5)]

        def nth(which, b):
            turns = sorted((3 * p + i // 2, i, p) for p in range(2) for i in range(BATCH))
            return turns.index((3 * which + b // 2, b, which)) + 1

        def n_of(q, c):
            return q * (UPQ // DH) + c // DH

        @block.sync
        def _(sp):
            x_t = x.rearrange("(t p) d -> p t d", p=P)
            sp.dma_start(res[:, 0:4, :], x_t[:, 0:4, :]).then_inc(L["x"], 16)
            sp.dma_start(res[:, 4:8, :], x_t[:, 4:8, :]).then_inc(L["x2"], 16)
            sp.dma_start(cst[:], consts).then_inc(L["cst"], 16)
            sp.dma_start(vec[:], vecs).then_inc(L["vec"], 16)
            sp.dma_start(wx_sb, wx.rearrange("(k p) m -> p k m", p=P)).then_inc(L["wx"], 16)
            sp.dma_start(wdt_sb, wdt).then_inc(L["wdt"], 16)
            sp.dma_start(gate_w, w1.rearrange("(k p) h -> p k h", p=P)).then_inc(L["w1"], 16)
            sp.dma_start(lin_w, w3.rearrange("(k p) h -> p k h", p=P)).then_inc(L["w3"], 16)
            sp.dma_start(bcst[:], bconsts.bitcast(BF16)).then_inc(L["bcst"], 16)
            sp.dma_start(row[:], rows).then_inc(L["row"], 16)
            sp.dma_start(cattn_sb[:, :, 0:3 * D], cattn.rearrange("(k p) n -> p k n", p=P)).then_inc(L["cattn"], 16)
            sp.dma_start(cproj_sb[:], cproj.rearrange("(k p) n -> p k n", p=P)).then_inc(L["cproj"], 16)
            e1 = mw1.rearrange("e (k p) n -> p e k n", p=P)
            e2_ = mw2.rearrange("e (k p) n -> p e k n", p=P)
            e3 = mw3.rearrange("e (k p) n -> p e k n", p=P)
            sp.dma_start(xbuf, zeros).then_inc(L["zero"], 16)
            sp.dma_start(sums[TOK:], zeros).then_inc(L["zero_sums"], 16)
            sp.dma_start(home_buf, no_home).then_inc(L["no_home"], 16)
            sp.dma_start(home_sb[:], home_of.rearrange("p (n two) -> p n two", two=2)).then_inc(L["home"], 16)
            for e in range(6):
                sp.dma_start(moe_w1[:, e], e1[:, e]).then_inc(L["mw1"], 16)
                sp.dma_start(moe_w2[:, e], e2_[:, e]).then_inc(L["mw2"], 16)
            sp.wait_ge(hid_used, UNITS + 2)
            sp.wait_ge(b_ready, UNITS)
            sp.wait_ge(c_ready, UNITS)
            for e in (6, 7):
                sp.dma_start(moe_w1[:, e], e1[:, e]).then_inc(L["mw1_late"], 16)
            for e in range(NE):
                sp.dma_start(moe_w3[:, e], e3[:, e]).then_inc(L["mw3"], 16)
            sp.wait_ge(sumT_ready, 2)
            sp.wait_ge(late_sumT_ready, 2)
            for e in (6, 7):
                sp.dma_start(moe_w2[:, e], e2_[:, e]).then_inc(L["mw2_late"], 16)
            def load_x(m):
                sp.dma_start(xin, xbuf[bass.ds(m * P, P), :]).then_inc(x_loaded, 16)

            sp.wait_ge(scattered, 16 * 2 * NT)
            load_x(0)
            sp.wait_ge(probsT_ready, 2 * BATCH)
            sp.dma_start(b3_sb, b3.unsqueeze(0).to_broadcast([P, NE, D])).then_inc(L["b3"], 16)
            sp.wait_ge(x_turned, 1)
            load_x(1)
            sp.wait_ge(proj_added, BATCH)
            sp.dma_start(sums[0:TOK].rearrange("(t p) d -> p t d", p=P), res[:]).then_inc(sums_ready, 16)
            for m in (2, 3):
                sp.wait_ge(x_turned, m)
                load_x(m)
            sp.wait_ge(homes_scattered, 16 * 2 * NT)
            sp.dma_start(homes[:], home_buf.rearrange("(p m) two -> p (m two)", p=P)).then_inc(homes_loaded, 16)
            with sp.Fori(1, MT - 3) as m:
                sp.wait_ge(x_turned, m + 3)
                load_x(m + 3)
            sp.wait_ge(y_stored, 16 * MT)
            sp.dma_start(out[0:TOK // 2], sums[0:TOK // 2]).then_inc(out_done, 16)
            sp.wait_ge(out_done, 32)

        @block.gpsimd
        def _(pool):
            pool.dma_start(down_w.rearrange("p (c d) -> p c d", c=HC),
                           w2.rearrange("(c p) d -> p c d", p=P)).then_inc(L["w2"], 16)
            pool.dma_start(sel_w, sel.bitcast(BF16).rearrange("p (s m) -> p s m", m=P)).then_inc(L["sel"], 16)
            nc.gpsimd.memset(bc_split[96:128, :], 0.0).then_inc(hid_ready, 2)
            pool.wait_ge(hid_ready, 2)
            pool.wait_ge(L["w2"], 16)
            src, dst = down_w, fly
            done = 0
            for stage, half in enumerate((1, 2, 4)):
                a = src.rearrange("p (g two n) -> p g two n", two=2, n=half * D)
                o = dst.rearrange("p (g two n) -> p g two n", two=2, n=half * D)
                if stage:
                    pool.wait_ge(fly_ready, 2 * stage)
                nc.gpsimd.tensor_tensor(o[:, :, 0, :], a[:, :, 0, :], a[:, :, 1, :], ALU.add).then_inc(fly_ready, 1)
                nc.gpsimd.tensor_tensor(o[:, :, 1, :], a[:, :, 0, :], a[:, :, 1, :], ALU.subtract).then_inc(fly_ready, 1)
                src, dst = dst, src
            for k in range(DH):
                pool.wait_ge(z_read, 2 * k + 2)
                pool.wait_ge(onepl_done, k + 1)
                nc.gpsimd.tensor_tensor(delta[:, k, :], delta[:, k, :], area_g[:, TOK * k:TOK * k + TOK],
                                        ALU.subtract).then_inc(less_lost, 1)
            pool.wait_ge(nrmT_ready, 4)
            pool.wait_ge(L["vec"], 16)
            for k in range(DH):
                nc.gpsimd.tensor_scalar(yacc[:, k, :], nrmT[:, k, :], vec[:, V_D + k:V_D + k + 1], None,
                                        ALU.mult).then_inc(y_added, 1)

            def add_state(c):
                nc.gpsimd.tensor_tensor(yacc[:, c % 2, :], yacc[:, c % 2, :], state[:, c % 2, :],
                                        ALU.add).then_inc(y_added, 1)

            def unit(q, c, late=False, last=False):
                u = q * UPQ + c
                g = gl[c % 2]
                pool.wait_ge(th_ready, u + 1)
                nc.gpsimd.tensor_tensor(g[:, 0:QW], g[:, 0:QW], g[:, QW:2 * QW], ALU.mult).then_inc(prod_done, 1)
                pool.wait_ge(prod_done, u + 1)
                pool.wait_ge(hid_used, u + 1)
                nc.gpsimd.tensor_tensor(hid[c % 2], g[:, 0:QW], th[c % 2], ALU.mult).then_inc(hid_ready, 1)
                if late:
                    return
                n = u - last
                pool.wait_ge(yc_done, n + 1)
                pool.wait_ge(y_added, n + 1)
                add_state(c - last)

            with pool.Fori(0, QT_ - 1) as q:
                for c in range(UPQ):
                    unit(q, c)
            for c in range(UPQ):
                unit(QT_ - 1, c, late=(c == UPQ - 2), last=(c == UPQ - 1))

            pool.wait_ge(acc_free, QT_ + 1)
            pool.wait_ge(y_added, UNITS + 2)
            for g in (2, 3):
                t = slice(g * QW, g * QW + QW)
                nc.gpsimd.tensor_tensor(yacc[:, :, t], yacc[:, :, t], ffn_out[:, :, t], ALU.add).then_inc(late_sumT_ready, 1)

            pool.wait_ge(nrm_ready, 2 * NT)
            pool.wait_ge(L["row"], 16)
            nc.gpsimd.tensor_tensor(res[:], res[:], row[:, R_PB:R_PB + D].unsqueeze(1).to_broadcast([P, NT, D]),
                                    ALU.add).then_inc(bias_added, 1)

            def at(slots, k, t):
                return bass.IndirectOffsetOnAxis(ap=slots[:, k, t:t + 1], axis=0)

            pool.wait_ge(L["zero"], 16)
            pool.wait_ge(slots_ready, 1)
            for t in range(NT):
                for k in range(2):
                    pool.indirect_dma_start(out=xbuf, out_offset=at(slot, k, t), in_=nrm[:, t, :],
                                            in_offset=None).then_inc(scattered, 16)
            pool.wait_ge(slots_ready, 2)
            pool.wait_ge(L["no_home"], 16)
            pool.wait_ge(L["home"], 16)
            for t in range(NT):
                for k in range(2):
                    pool.indirect_dma_start(out=home_buf, out_offset=at(home_slot, k, t),
                                            in_=home_sb[:, k * NT + t, :],
                                            in_offset=None).then_inc(homes_scattered, 16)
            def store_y(m):
                nc.gpsimd.tensor_copy(home[:], homes[:, bass.ds(2 * m, 1)]).then_inc(home_ready, 1)
                pool.wait_ge(home_ready, m + 1)
                pool.wait_ge(y_ready, m + 2)
                nc.gpsimd.tensor_tensor(home_seen[:], home[:], home[:], ALU.add).then_inc(home_read, 1)
                pool.indirect_dma_start(out=sums, out_offset=bass.IndirectOffsetOnAxis(ap=home[:, 0:1], axis=0),
                                        in_=yout, in_offset=None, compute_op=ALU.add).then_inc(y_stored, 16)

            pool.wait_ge(homes_loaded, 16)
            pool.wait_ge(L["zero_sums"], 16)
            pool.wait_ge(sums_ready, 16)
            store_y(0)
            with pool.Fori(1, MT) as m:
                pool.wait_ge(home_read, m)
                pool.wait_ge(y_stored, 16 * m)
                store_y(m)

        @block.scalar
        def _(act):
            act.wait_ge(var_ready, 1)
            nc.scalar.activation(ln_s[:], ln_v[:], ACT.Sqrt).then_inc(sqrt_ready, 1)
            act.wait_ge(L["vec"], 16)
            nc.scalar.activation(amat[:], vec[:, V_ALOG:V_ALOG + 2 * NS], ACT.Exp).then_inc(act_chain, 1)
            act.wait_ge(act_chain, 1)
            nc.scalar.mul(amat[:], amat[:], -1.0).then_inc(amat_ready, 1)
            for g in (0, 2):
                act.wait_ge(turned, g + 1)
                nc.scalar.copy(nrmT[:, g // 2, 0:512], bank(g)).then_inc(nrmT_ready, 1)
            act.wait_ge(rank_ready, 1)
            nc.scalar.copy(area_f[0:RANK, 0:TOK], bank(0, 2)[0:RANK, :]).then_inc(rank_copied, 1)
            for k in range(DH):
                z, e = bank(2 + 2 * k, 2), area_g[:, TOK * k:TOK * k + TOK]
                act.wait_ge(z_ready, k + 1)
                nc.scalar.activation(e, z, ACT.Abs, bias=vec[:, V_BDT + k:V_BDT + k + 1]).then_inc(z_read, 1)
                act.wait_ge(z_read, 2 * k + 1)
                nc.scalar.activation(e, e, ACT.Exp, scale=-1.0).then_inc(absexp_done, 1)
                nc.scalar.activation(delta[:, k, :], z, ACT.Relu, bias=vec[:, V_BDT + k:V_BDT + k + 1]).then_inc(z_read, 1)
            act.wait_ge(bc_ready, 1)
            act.wait_ge(hid_ready, 2)
            nc.scalar.copy(bc_split[0:96, :], bank(6, 2)[0:96, :]).then_inc(bc_done, 1)
            for k in range(DH):
                act.wait_ge(onepl_done, k + 1)
                nc.scalar.activation(loan2[:, TOK * k:TOK * k + TOK], loan2[:, TOK * k:TOK * k + TOK],
                                     ACT.Ln).then_inc(log_done, 1)
            act.wait_ge(z2_ready, 1)
            nc.scalar.activation(lw[:, 1:2], lw[:, 0:1], ACT.Tanh, scale=0.5).then_inc(lw_ready, 1)
            for g, b in enumerate((0, 1, 6, 7)):
                act.wait_ge(had_ready, g + 1)
                nc.scalar.mul(down_w[:, 512 * g:512 * g + 512], bank(b), 0.5 / H0 ** 0.5).then_inc(down_ready, 1)

            act.wait_ge(decay_zero, 1)
            act.wait_ge(delta_ready, 1)

            def decays(q, c):
                act.wait_ge(scan_done, q * UPQ + c + 1)
                nc.scalar.activation(decay[:, c % 2, :].rearrange("p (b t) -> p b t", b=BATCH)[:, :, 1:SEQ],
                                     delta[:, c % 2, :].rearrange("p (b t) -> p b t", b=BATCH)[:, :, 1:SEQ],
                                     ACT.Exp, scale=amat[:, bass.ds((c % DH) * NS + n_of(q, c), 1)]).then_inc(decay_ready, 1)

            def unit(q, c, last_quarter):
                u = q * UPQ + c
                if not (last_quarter and c == UPQ - 1):
                    decays(*((q, c + 1) if c + 1 < UPQ else (q + 1, 0)))
                act.wait_ge(up_ready, u + 1)
                act.wait_ge(hid_ready, u + 1)
                nc.scalar.copy(gl[c % 2], bank(6)).then_inc(up_read, 1)
                nc.scalar.activation(th[c % 2], bank(6)[:, 0:QW], ACT.Tanh, scale=0.5).then_inc(up_read, 1)
                act.wait_ge(up_read, 2 * u + 4)
                nc.scalar.add(th[c % 2], th[c % 2], 1.0).then_inc(th_ready, 1)

            def quarter(q, last_quarter):
                for c in range(1, UPQ):
                    unit(q, c, last_quarter)
                if not last_quarter:
                    unit(q + 1, 0, False)
                act.wait_ge(hid_used, q * UPQ + UPQ + 2)
                nc.scalar.copy(ffn_out[:, :, bass.ds(q * QW, QW)],
                               bank(7).rearrange("p (k t) -> p k t", k=DH)).then_inc(acc_free, 1)

            act.wait_ge(amat_ready, 1)
            decays(0, 0)
            unit(0, 0, False)
            with act.Fori(0, QT_ - 1) as q:
                quarter(q, False)
            quarter(QT_ - 1, True)

            act.wait_ge(var_ready, 2)
            nc.scalar.activation(ln_s[:], ln_v[:], ACT.Sqrt).then_inc(sqrt_ready, 1)
            for g in (0, 2):
                act.wait_ge(turned, 4 + g + 1)
                nc.scalar.copy(nrmT[:, g // 2, 0:512], bank(g)).then_inc(nrmT_ready, 1)

            def qk_out(g):
                m, t = g // 2, g % 2
                act.wait_ge(qk_ready, g + 1)
                dst = (qT, kT)[m // 2][:, m % 2, 512 * t:512 * t + 512]
                nc.scalar.activation(dst, bank(BANK_OF_QK[g]), ACT.Identity, bias=vec[:, V_QKB + m:V_QKB + m + 1]).then_inc(qk_done, 1)

            act.wait_ge(soft_in, 1)
            nc.scalar.activation(expd, logit, ACT.Exp).then_inc(soft_out, 1)
            for g in range(2):
                qk_out(g)
            act.wait_ge(top2_ready, 1)
            nc.scalar.activation(e2, top2, ACT.Exp).then_inc(e2_ready, 1)
            for g in range(2, 8):
                qk_out(g)

            for steps in attention_steps():
                for which, step, b in steps:
                    a_bank, b_bank = (2 * b, 2 * b + 1) if which == 0 else (2 * b + 1, 2 * b)
                    if step == 0:
                        act.wait_ge(bias_ready, nth(which, b))
                        for i in range(2):
                            nc.scalar.activation(probs[:, b, i, :], bank(a_bank)[:, SEQ * i:SEQ * i + SEQ], ACT.Exp,
                                                 bias=smax[:, which, b, i:i + 1], scale=SCALE,
                                                 accum_out=ssum[:, which, b, i:i + 1]).then_inc(exp_done, 1)
                    if step == 1:
                        act.wait_ge(probsT_ready, nth(which, b))
                        nc.scalar.copy(probsT[:, b].rearrange("p k t -> p (k t)"), bank(b_bank)).then_inc(probsT_done, 1)
                    if step == 2 and which == 0:
                        act.wait_ge(context_ready, nth(0, b))
                        nc.scalar.activation(probs[:, b, 0, :], bank(a_bank)[:, 0:SEQ], ACT.Tanh,
                                             scale=vec[:, V_GATE:V_GATE + 1]).then_inc(tanh_done, 1)
                    if step == 2 and which == 1:
                        act.wait_ge(context_ready, nth(1, b))
                        act.wait_ge(slots_ready, 2)
                        nc.scalar.copy(ctxT[:, :, SEQ * b:SEQ * b + SEQ],
                                       bank(a_bank).rearrange("p (k t) -> p k t", k=DH)).then_inc(ctx_done, 1)

            nc.scalar.activation(ln_s[:, 0:1], amat[:, 0:1], ACT.Gelu)

            def gelus(src, dst, bias_col, e, done):
                for k in range(KM):
                    last = nc.scalar.activation(dst[:, k, :], bank(src)[:, P * k:P * k + P], ACT.Gelu,
                                                bias=vec[:, bass.ds(bias_col + KM * e + k, 1)])
                last.then_inc(done, 1)

            def layer1_out(m, first_tile=False):
                e = act.value_load(owner[0:1, bass.ds(m, 1)], min_val=0, max_val=NE - 1)
                act.wait_ge(t1_ready, m + 1)
                if not first_tile:
                    act.wait_ge(l2_ready, m)
                gelus(2, h1T, V_B1, e, h1_ready)

            def layer2_out(m, first_tile=False):
                e = act.value_load(owner[0:1, bass.ds(m, 1)], min_val=0, max_val=NE - 1)
                act.wait_ge(t2_ready, m + 1)
                if not first_tile:
                    act.wait_ge(l3_ready, m)
                gelus(4, h2T, V_B2, e, h2_ready)

            act.wait_ge(owner_ready, 1)
            layer1_out(0, first_tile=True)
            layer1_out(1)
            layer2_out(0, first_tile=True)
            with act.Fori(1, MT - 1) as m:
                layer1_out(m + 1)
                layer2_out(m)
            layer2_out(MT - 1)
            act.wait_ge(y_stored, 16 * MT)
            act.dma_start(out[TOK // 2:], sums[TOK // 2:TOK]).then_inc(out_done, 16)

        @block.tensor
        def _(pe):
            pe.wait_ge(L["cst"], 16)

            def turn_tiles(phase):
                for g in range(4):
                    k, th4 = g // 2, g % 2
                    for j in range(4):
                        t = 4 * th4 + j
                        if k == 0:
                            pe.wait_ge(nrm_ready, phase * NT + t + 1)
                        last = nc.tensor.transpose(bank(g)[:, P * j:P * j + P], nrm[:, t, P * k:P * k + P], ident)
                    last.then_inc(turned, 1)

            turn_tiles(0)
            pe.wait_ge(nrmT_ready, 4)
            pe.wait_ge(L["wx"], 16)
            def project_norm(cols, b, ready):
                m = cols.stop - cols.start
                for t in range(2):
                    for k in range(DH):
                        last = nc.tensor.matmul(bank(b + t)[0:m, :], wx_sb[:, k, cols], nrmT[:, k, 512 * t:512 * t + 512],
                                                start=(k == 0), stop=(k == DH - 1))
                last.then_inc(ready, 1)

            project_norm(slice(0, RANK), 0, rank_ready)
            pe.wait_ge(rank_copied, 1)
            pe.wait_ge(L["wdt"], 16)
            for k in range(DH):
                for t in range(2):
                    last = nc.tensor.matmul(bank(2 + 2 * k + t), wdt_sb[:, P * k:P * k + P],
                                            area_f[0:RANK, 512 * t:512 * t + 512], start=True, stop=True)
                last.then_inc(z_ready, 1)
            project_norm(slice(RANK, RANK + 96), 6, bc_ready)
            pe.wait_ge(fly_ready, 6)
            for g, b in enumerate((0, 1, 6, 7)):
                if g == 2:
                    pe.wait_ge(bc_done, 2)
                nc.tensor.matmul(bank(b), hadamard, fly[:, 512 * g:512 * g + 512], start=True, stop=True).then_inc(had_ready, 1)

            def select(b, which, n):
                for t in range(2):
                    last = nc.tensor.matmul(bank(b + t), sel_w[:, bass.ds(which * NS + n, 1), :].rearrange("p s m -> p (s m)"),
                                            bc_split[:, 512 * t:512 * t + 512], start=True, stop=True)
                return last

            def up(q, c):
                for i, w in enumerate((gate_w, lin_w)):
                    for k in range(DH):
                        last = nc.tensor.matmul(bank(6)[:, QW * i:QW * i + QW], w[:, k, P * c:P * c + P],
                                                nrmT[:, k, bass.ds(q * QW, QW)], start=(k == 0), stop=(k == DH - 1))
                return last

            pe.wait_ge(L["sel"], 16)
            pe.wait_ge(L["w1"], 16)
            pe.wait_ge(L["w3"], 16)
            pe.wait_ge(hid_ready, 2)
            pe.wait_ge(bc_done, 5)
            pe.wait_ge(z_read, 4)
            pe.wait_ge(down_ready, 4)
            select(0, 0, 0).then_inc(b_ready, 1)
            select(2, 0, n_of(0, 1)).then_inc(b_ready, 1)
            select(4, 1, 0).then_inc(c_ready, 1)
            up(0, 0).then_inc(up_ready, 1)
            pe.wait_ge(up_read, 4)
            up(0, 1).then_inc(up_ready, 1)

            def ahead(q, c, n):
                return (q, c + n) if c + n < UPQ else (q + 1, c + n - UPQ)

            def unit(q, c, last_quarter):
                u = q * UPQ + c
                left = UPQ - 1 - c if last_quarter else UPQ
                if left >= 2:
                    q2, c2 = ahead(q, c, 2)
                    pe.wait_ge(scan_done, u + 3)
                    select(2 * (c2 % 2), 0, n_of(q2, c2)).then_inc(b_ready, 1)
                pe.wait_ge(hid_ready, u + 3)
                if c == 0:
                    pe.wait_ge(acc_free, q + 1)
                for k in range(DH):
                    last = nc.tensor.matmul(bank(7)[:, QW * k:QW * k + QW], down_w[:, D * c + P * k:D * c + P * k + P], hid[c % 2],
                                            start=(c == 0 and k == 0), stop=(c == UPQ - 1), skip_group_check=True)
                last.then_inc(hid_used, 1)
                if left >= 1:
                    q1, c1 = ahead(q, c, 1)
                    pe.wait_ge(yc_done, u + 1)
                    select(4, 1, n_of(q1, c1)).then_inc(c_ready, 1)
                if left >= 2:
                    pe.wait_ge(up_read, 2 * u + 6)
                    up(q2, c2).then_inc(up_ready, 1)

            with pe.Fori(0, QT_ - 1) as q:
                for c in range(UPQ):
                    unit(q, c, False)
            for c in range(UPQ):
                unit(QT_ - 1, c, True)

            for j in range(NT):
                pe.wait_ge((sumT_ready, late_sumT_ready)[j // 4], j // 2 % 2 + 1)
                for k in range(DH):
                    last = nc.tensor.transpose(bank(j // 2)[:, D * (j % 2) + P * k:D * (j % 2) + P * k + P],
                                               yacc[:, k, P * j:P * j + P], ident)
                if j % 2:
                    last.then_inc(back_ready, 1)

            pe.wait_ge(x1_ready, NT)
            turn_tiles(1)
            pe.wait_ge(nrmT_ready, 8)
            pe.wait_ge(L["cattn"], 16)
            pe.wait_ge(v_done, 1)
            for t in range(NT):
                for k in range(DH):
                    last = nc.tensor.matmul(bank(t)[:, 0:D + NE], nrmT[:, k, P * t:P * t + P],
                                            cattn_sb[:, k, 2 * D:3 * D + NE], start=(k == 0), stop=(k == DH - 1))
                last.then_inc(v_ready, 1)

            def qk(g):
                m, t = g // 2, g % 2
                pe.wait_ge(v_done, 1 + BANK_OF_QK[g] + 1)
                if g >= 6:
                    pe.wait_ge(qk_done, g - 5)
                for k in range(DH):
                    last = nc.tensor.matmul(bank(BANK_OF_QK[g]), cattn_sb[:, k, P * m:P * m + P], nrmT[:, k, 512 * t:512 * t + 512],
                                            start=(k == 0), stop=(k == DH - 1))
                last.then_inc(qk_ready, 1)

            for g in range(5):
                qk(g)
            pe.wait_ge(mask_ready, 1)
            pe.wait_ge(L["bcst"], 16)
            tri, ones = bcst[:, B_TRI:B_TRI + P], bcst[:, B_ONE:B_ONE + P]
            pe.wait_ge(v_done, 1 + NT)
            counts, totals = bank(7)[:, 0:NT * NE], bank(7)[:, NT * NE:NT * NE + NE]
            nc.tensor.matmul(counts, tri, mask[:].rearrange("p t e -> p (t e)"), start=True, stop=False)
            for i in range(NT - 1):
                later = counts[:, NE * (i + 1):].rearrange("p (t e) -> p t e", e=NE)
                nc.tensor.matmul(later, ones, mask[:, i:i + 1, :].to_broadcast([P, NT - 1 - i, NE]),
                                 start=False, stop=(i == NT - 2))
            for i in range(NT):
                last = nc.tensor.matmul(totals, ones, mask[:, i, :], start=(i == 0), stop=(i == NT - 1))
            last.then_inc(prefix_ready, 1)
            for g in range(5, 8):
                qk(g)

            def project(b):
                pe.wait_ge(ctx_done, b + 1)
                for i in range(2):
                    o, own = bank(2 * b)[:, D * i:D * i + D], slice(SEQ * b + P * i, SEQ * b + P * i + P)
                    for k in range(DH):
                        last = nc.tensor.matmul(o, ctxT[:, k, own], cproj_sb[:, k, :], start=(k == 0), stop=(k == DH - 1))
                last.then_inc(proj_ready, 1)

            pe.wait_ge(qk_done, 8)
            for steps in attention_steps():
                for which, step, b in steps:
                    a, o = (bank(2 * b), bank(2 * b + 1)) if which == 0 else (bank(2 * b + 1), bank(2 * b))
                    tokens = slice(SEQ * b, SEQ * b + SEQ)
                    if step == 0:
                        if which == 0 and b == 3:
                            pe.wait_ge(slots_ready, 1)
                        if which:
                            pe.wait_ge(query_done, b + 1)
                        for i in range(2):
                            own = slice(SEQ * b + P * i, SEQ * b + P * i + P)
                            for k in range(which + 1):
                                last = nc.tensor.matmul(a[:, SEQ * i:SEQ * i + SEQ], qT[:, k, own], kT[:, k, tokens],
                                                        start=(k == 0), stop=(k == which))
                        last.then_inc(scores_ready, 1)
                    if step == 1:
                        pe.wait_ge(probs_ready, nth(which, b))
                        for i in range(2):
                            for k in range(2):
                                last = nc.tensor.transpose(o[:, SEQ * k + P * i:SEQ * k + P * i + P],
                                                           probs[:, b, i, P * k:P * k + P], ident)
                        last.then_inc(probsT_ready, 1)
                    if step == 2:
                        pe.wait_ge(probsT_done, nth(which, b))
                        for h in range(which + 1):
                            for k in range(2):
                                last = nc.tensor.matmul(a[:, SEQ * h:SEQ * h + SEQ], val[:, 2 * b + k, P * h:P * h + P],
                                                        probsT[:, b, k, :], start=(k == 0), stop=(k == 1))
                        last.then_inc(context_ready, 1)
            pe.wait_ge(L["cproj"], 16)
            for b in range(BATCH // 2):
                project(b)

            def turn_x(m):
                pe.wait_ge(x_loaded, 16 * m + 16)
                for k in range(DH):
                    last = nc.tensor.transpose(bank(0)[:, P * k:P * k + P], xin[:, P * k:P * k + P], ident)
                last.then_inc(x_turned, 1)

            def expert_of(m):
                return pe.value_load(owner[0:1, bass.ds(m, 1)], min_val=0, max_val=NE - 1)

            def layer1(m):
                e = expert_of(m)
                pe.wait_ge(xT_ready, m + 1)
                for k in range(DH):
                    last = nc.tensor.matmul(bank(1), xT[:, k, :], moe_w1[:, bass.ds(e, 1), k, :].rearrange("p e n -> p (e n)"),
                                            start=(k == 0), stop=(k == DH - 1))
                last.then_inc(l1_ready, 1)

            def turn(src, dst, need, ready, m):
                pe.wait_ge(need, m + 1)
                for k in range(KM):
                    last = nc.tensor.transpose(bank(dst)[:, P * k:P * k + P], src[:, P * k:P * k + P], ident)
                last.then_inc(ready, 1)

            def layer2(m):
                e = expert_of(m)
                pe.wait_ge(h1_ready, m + 1)
                for k in range(KM):
                    last = nc.tensor.matmul(bank(3), h1T[:, k, :], moe_w2[:, bass.ds(e, 1), k, :].rearrange("p e n -> p (e n)"),
                                            start=(k == 0), stop=(k == KM - 1))
                last.then_inc(l2_ready, 1)

            def layer3(m):
                e = expert_of(m)
                pe.wait_ge(h2_ready, m + 1)
                pe.wait_ge(y_read, m + 1)
                for k in range(KM):
                    last = nc.tensor.matmul(bank(5)[:, 0:D], h2T[:, k, :], moe_w3[:, bass.ds(e, 1), k, :].rearrange("p e n -> p (e n)"),
                                            start=(k == 0), stop=(k == KM - 1))
                last.then_inc(l3_ready, 1)

            def loaded(*names):
                for n in names:
                    pe.wait_ge(L[n], 16 * {"mw1": 6, "mw2": 6, "mw1_late": 2, "mw3": NE, "mw2_late": 2}[n])

            def expert_step(m, first_tile=False, left=MT):
                layer2(m)
                if left >= 1:
                    turn(raw1, 2, r1_ready, t1_ready, m + 1)
                if not first_tile:
                    layer3(m - 1)
                if left >= 2:
                    layer1(m + 2)
                turn(raw2, 4, r2_ready, t2_ready, m)
                if left >= 3:
                    turn_x(m + 3)

            pe.wait_ge(owner_ready, 1)
            pe.wait_ge(proj_added, 1)
            turn_x(0)
            for b in range(BATCH // 2, BATCH):
                project(b)
            loaded("mw1", "mw1_late")
            layer1(0)
            turn_x(1)
            pe.wait_ge(proj_added, 2)
            turn(raw1, 2, r1_ready, t1_ready, 0)
            layer1(1)
            turn_x(2)
            pe.wait_ge(proj_added, 3)
            loaded("mw2", "mw2_late")
            expert_step(0, first_tile=True)
            loaded("mw3")
            with pe.Fori(1, MT - 3) as m:
                expert_step(m)
            for left in (2, 1, 0):
                expert_step(MT - 1 - left, left=left)
            layer3(MT - 1)

        @block.vector
        def _(dve):
            chain = [0]

            def link(ins):
                chain[0] += 1
                ins.then_inc(dve_chain, 1)
                dve.wait_ge(dve_chain, chain[0])

            def normalise(phase):
                dve.wait_ge(stats_done, (phase + 1) * NT)
                for t in range(NT):
                    ins = nc.vector.bn_aggr(mv[:, t, :], st6[:, t, :])
                link(ins)
                nc.vector.tensor_scalar(ln_v[:], mv[:, :, 1], EPS, None, ALU.add).then_inc(var_ready, 1)
                dve.wait_ge(sqrt_ready, phase + 1)
                link(nc.vector.reciprocal(ln_r[:], ln_s[:]))
                link(nc.vector.tensor_tensor(ln_t[:], ln_r[:], ln_r[:], ALU.mult))
                link(nc.vector.tensor_tensor(ln_t[:], ln_t[:], ln_v[:], ALU.mult))
                link(nc.vector.tensor_scalar(ln_t[:], ln_t[:], -0.5, 1.5, ALU.mult, ALU.add))
                link(nc.vector.tensor_tensor(ln_r[:], ln_r[:], ln_t[:], ALU.mult))
                for t in range(NT):
                    nc.vector.tensor_scalar(nrm[:, t, :], res[:, t, :], mv[:, t, 0:1], ln_r[:, t:t + 1],
                                            ALU.subtract, ALU.mult).then_inc(nrm_ready, 1)

            for t in range(NT):
                if t == 0:
                    dve.wait_ge(L["x"], 16)
                if t == 4:
                    dve.wait_ge(L["x2"], 16)
                nc.vector.bn_stats(st6[:, t, :], res[:, t, :]).then_inc(stats_done, 1)
            normalise(0)
            for g in (1, 3):
                dve.wait_ge(turned, g + 1)
                nc.vector.tensor_copy(nrmT[:, g // 2, 512:1024], bank(g)).then_inc(nrmT_ready, 1)
            dve.wait_ge(L["vec"], 16)
            nc.vector.tensor_copy(cattn_sb[:, :, 3 * D:3 * D + NE],
                                  vec[:, V_WG:V_WG + DH * NE].rearrange("p (k e) -> p k e", k=DH)).then_inc(v_done, 1)
            nc.vector.scalar_tensor_tensor(lw[:, 0:1], vec[:, V_W1:V_W1 + 1], 0.5, vec[:, V_W0:V_W0 + 1],
                                           ALU.mult, ALU.add).then_inc(z2_ready, 1)
            u1 = loan2[:, 0:2048].rearrange("p (k t) -> p k t", k=DH)
            e = area_g[:].rearrange("p (k t) -> p k t", k=DH)
            for k in range(DH):
                dve.wait_ge(absexp_done, k + 1)
                link(nc.vector.tensor_scalar(u1[:, k, :], e[:, k, :], 1.0, None, ALU.add))
                nc.vector.scalar_tensor_tensor(e[:, k, :], u1[:, k, :], -1.0, e[:, k, :], ALU.add,
                                               ALU.subtract).then_inc(onepl_done, 1)
            v = bank(6, 2)
            dve.wait_ge(bc_done, 1)
            nc.vector.tensor_tensor(area_e[0:96, 0:TOK], v[0:96, :], bc_split[0:96, :], ALU.subtract).then_inc(bc_done, 1)
            dve.wait_ge(bc_done, 2)
            nc.vector.tensor_copy(bc_split[32:64, :], area_e[32:64, 0:TOK]).then_inc(bc_done, 1)
            nc.vector.tensor_copy(bc_split[64:96, :], area_e[64:96, 0:TOK]).then_inc(bc_done, 1)
            dve.wait_ge(bc_done, 4)
            link(nc.vector.tensor_tensor(area_e[64:96, 0:TOK], area_e[64:96, 0:TOK], bc_split[64:96, :], ALU.subtract))
            nc.vector.tensor_copy(bc_split[64:96, :], area_e[64:96, 0:TOK]).then_inc(bc_done, 1)
            nc.vector.memset(decay.rearrange("p i (b t) -> p (i b) t", b=BATCH)[:, :, 0:1], 0.0).then_inc(decay_zero, 1)
            dve.wait_ge(bc_done, 5)
            dve.wait_ge(nrmT_ready, 4)
            for k in range(DH):
                dve.wait_ge(less_lost, k + 1)
                dve.wait_ge(log_done, k + 1)
                nc.vector.tensor_tensor(delta[:, k, :], delta[:, k, :], u1[:, k, :], ALU.add).then_inc(delta_ready, 1)
                dve.wait_ge(delta_ready, k + 1)
                link(nc.vector.tensor_tensor(du[:, k, :], delta[:, k, :], nrmT[:, k, :], ALU.mult))
            dve.wait_ge(lw_ready, 1)
            nc.vector.tensor_scalar(lw[:, 1:2], lw[:, 1:2], 0.5, 0.5, ALU.mult, ALU.add).then_inc(lw_ready, 1)

            def product(q, c):
                u = q * UPQ + c
                dve.wait_ge(b_ready, u + 1)
                b = bank(2 * (c % 2), 2)
                nc.vector.tensor_tensor(b, du[:, c % DH, :], b, ALU.mult).then_inc(bx_done, 1)

            nc.vector.memset(ln_t[:, 0:1], 0.0).then_inc(scan_done, 2)
            nc.vector.memset(ln_t[:, 1:2], 0.0).then_inc(hid_used, 2)
            nc.vector.memset(ln_t[:, 2:3], 0.0).then_inc(up_read, 2)
            nc.vector.memset(ln_t[:, 3:4], 0.0).then_inc(acc_free, 1)
            product(0, 0)

            def unit(q, c, last_quarter):
                u = q * UPQ + c
                dve.wait_ge(bx_done, u + 1)
                dve.wait_ge(decay_ready, u + 1)
                dve.wait_ge(y_added, u + 1)
                nc.vector.tensor_tensor_scan(state[:, c % 2, :], decay[:, c % 2, :], bank(2 * (c % 2), 2), 0.0,
                                             ALU.mult, ALU.add).then_inc(scan_done, 1)
                if not (last_quarter and c == UPQ - 1):
                    product(*((q, c + 1) if c + 1 < UPQ else (q + 1, 0)))
                dve.wait_ge(scan_done, u + 3)
                dve.wait_ge(c_ready, u + 1)
                nc.vector.tensor_tensor(state[:, c % 2, :], state[:, c % 2, :], bank(4, 2), ALU.mult).then_inc(yc_done, 1)

            with dve.Fori(0, QT_ - 1) as q:
                for c in range(UPQ):
                    unit(q, c, False)
            for c in range(UPQ):
                unit(QT_ - 1, c, True)

            dve.wait_ge(yc_done, UNITS)
            dve.wait_ge(y_added, UNITS)
            nc.vector.tensor_tensor(yacc[:, 1, :], yacc[:, 1, :], state[:, 1, :], ALU.add).then_inc(y_added, 1)
            dve.wait_ge(acc_free, QT_ + 1)
            dve.wait_ge(y_added, UNITS + 2)
            for g in (0, 1):
                t = slice(g * QW, g * QW + QW)
                nc.vector.tensor_tensor(yacc[:, :, t], yacc[:, :, t], ffn_out[:, :, t], ALU.add).then_inc(sumT_ready, 1)

            def statistics(g):
                dve.wait_ge(x1_ready, 2 * g + 2)
                for t in (2 * g, 2 * g + 1):
                    nc.vector.bn_stats(st6[:, t, :], res[:, t, :]).then_inc(stats_done, 1)

            for g in range(4):
                dve.wait_ge(back_ready, g + 1)
                nc.vector.tensor_tensor(res[:, 2 * g:2 * g + 2, :].rearrange("p t d -> p (t d)"),
                                        res[:, 2 * g:2 * g + 2, :].rearrange("p t d -> p (t d)"), bank(g), ALU.add).then_inc(x1_ready, 2)
                if g:
                    statistics(g - 1)
            statistics(3)

            normalise(1)
            for g in (1, 3):
                dve.wait_ge(turned, 4 + g + 1)
                nc.vector.tensor_copy(nrmT[:, g // 2, 512:1024], bank(g)).then_inc(nrmT_ready, 1)

            dve.wait_ge(L["row"], 16)
            wide = lambda a: a.unsqueeze(2).to_broadcast([P, NT, NE])
            over_tiles = lambda a: a.unsqueeze(1).to_broadcast([P, NT, NE])
            key = over_tiles(cst[:, C_KEY:C_KEY + NE])
            for t in range(NT):
                dve.wait_ge(v_ready, t + 1)
                nc.vector.tensor_tensor(logit[:, t, :], bank(t)[:, D:D + NE], row[:, R_BG:R_BG + NE],
                                        ALU.add).then_inc(dve_chain, 1)
                chain[0] += 1
                nc.vector.tensor_tensor(val[:, t, :], bank(t)[:, 0:D], row[:, R_VB:R_VB + D], ALU.add).then_inc(v_done, 1)
            dve.wait_ge(dve_chain, chain[0])
            link(nc.vector.tensor_reduce(top, logit, AX.X, ALU.max))
            link(nc.vector.tensor_tensor(logit, logit, wide(top), ALU.subtract))
            nc.vector.tensor_scalar(first, logit, 0.0, None, ALU.is_equal).then_inc(soft_in, 1)
            dve.wait_ge(soft_in, 1)

            def lowest(choice):
                link(nc.vector.tensor_tensor(keyed, choice, key, ALU.mult))
                link(nc.vector.tensor_reduce(keymax, keyed, AX.X, ALU.max))
                link(nc.vector.tensor_tensor(choice, keyed, wide(keymax), ALU.is_equal))

            lowest(first)
            dve.wait_ge(soft_out, 1)
            link(nc.vector.scalar_tensor_tensor(logit, first, -1e30, logit, ALU.mult, ALU.add))
            nc.vector.tensor_reduce(top2, logit, AX.X, ALU.max).then_inc(top2_ready, 1)
            dve.wait_ge(top2_ready, 1)
            link(nc.vector.tensor_tensor(second, logit, wide(top2), ALU.is_equal))
            lowest(second)
            nc.vector.tensor_tensor(mask[:], first, second, ALU.add).then_inc(mask_ready, 1)
            link(nc.vector.tensor_reduce(esum, expd, AX.X, ALU.add))
            dve.wait_ge(L["home"], 16)
            link(nc.vector.reciprocal(gain[:, 0, :], esum))
            dve.wait_ge(e2_ready, 1)
            link(nc.vector.tensor_tensor(gain[:, 1, :], gain[:, 0, :], e2, ALU.mult))
            dve.wait_ge(prefix_ready, 1)
            link(nc.vector.tensor_scalar(tile_int, bank(7)[:, NT * NE:NT * NE + NE], float(P - 1), None, ALU.add))
            link(nc.vector.tensor_scalar(tile_int, tile_int, 7, None, ALU.logical_shift_right))
            link(nc.vector.tensor_copy(tiles8, tile_int))
            link(nc.vector.tensor_scalar(ones8, tiles8, 0.0, None, ALU.is_ge))
            link(nc.vector.tensor_tensor_scan(upto8, ones8, tiles8, 0.0, ALU.mult, ALU.add))
            link(nc.vector.tensor_tensor(base8, upto8, tiles8, ALU.subtract))
            link(nc.vector.tensor_scalar(base8, base8, float(P), None, ALU.mult))
            link(nc.vector.tensor_tensor(place, bank(7)[:, 0:NT * NE].rearrange("p (t e) -> p t e", e=NE),
                                         over_tiles(base8), ALU.add))
            for k, choice in enumerate((first, second)):
                link(nc.vector.tensor_tensor(tmp64, choice, place, ALU.mult))
                link(nc.vector.tensor_reduce(slotf, tmp64, AX.X, ALU.add))
                ins = nc.vector.tensor_copy(slot[:, k, :], slotf)
                if k == 0:
                    link(ins)
                else:
                    ins.then_inc(slots_ready, 1)
            link(nc.vector.tensor_tensor(hits, upto8.unsqueeze(1).to_broadcast([P, MT, NE]),
                                         cst[:, C_TILE:C_TILE + MT].unsqueeze(2).to_broadcast([P, MT, NE]), ALU.is_le))
            link(nc.vector.tensor_reduce(owner_f, hits, AX.X, ALU.add))
            link(nc.vector.tensor_scalar(owner_f, owner_f, float(NE - 1), None, ALU.min))
            nc.vector.tensor_copy(owner[:], owner_f).then_inc(owner_ready, 1)
            dve.wait_ge(owner_ready, 1)
            row_of, tile_of = (area_g[:, 900 + 16 * i:916 + 16 * i].bitcast(U32).rearrange("p (k t) -> p k t", k=2)
                               for i in range(2))
            nc.vector.tensor_scalar(row_of, slot[:], P - 1, None, ALU.bitwise_and).then_inc(dve_chain, 1)
            chain[0] += 1
            link(nc.vector.tensor_scalar(tile_of, slot[:], 7, None, ALU.logical_shift_right))
            link(nc.vector.scalar_tensor_tensor(home_slot[:], row_of, float(MT), tile_of, ALU.mult, ALU.add))
            nc.vector.memset(ln_t[:, 4:5], 0.0).then_inc(slots_ready, 1)

            for steps in attention_steps():
                for which, step, b in steps:
                    if step == 0:
                        src = bank(2 * b + which).rearrange("p (i t) -> p i t", i=2)
                        dve.wait_ge(scores_ready, nth(which, b))
                        link(nc.vector.tensor_reduce(smax[:, which, b, :], src, AX.X, ALU.max))
                        nc.vector.tensor_scalar(smax[:, which, b, :], smax[:, which, b, :], -SCALE, None,
                                                ALU.mult).then_inc(bias_ready, 1)
                for which, step, b in steps:
                    if step == 0:
                        dve.wait_ge(exp_done, 2 * nth(which, b))
                        link(nc.vector.reciprocal(sinv[:, which, b, :], ssum[:, which, b, :]))
                        for i in range(2):
                            ins = nc.vector.tensor_scalar(probs[:, b, i, :], probs[:, b, i, :], sinv[:, which, b, i:i + 1], None,
                                                          ALU.mult)
                        ins.then_inc(probs_ready, 1)
                for which, step, b in steps:
                    if step == 2 and which == 0:
                        dve.wait_ge(tanh_done, b + 1)
                        q0 = qT[:, 0, SEQ * b:SEQ * b + SEQ]
                        nc.vector.scalar_tensor_tensor(q0, probs[:, b, 0, :], lw[:, 1:2], q0, ALU.mult, ALU.add).then_inc(query_done, 1)

            nc.vector.memset(ln_t[:, 5:6], 0.0).then_inc(y_ready, 1)
            nc.vector.memset(ln_t[:, 6:7], 0.0).then_inc(y_read, 1)

            def x_out(m, first_tile):
                dve.wait_ge(x_turned, m + 1)
                if not first_tile:
                    dve.wait_ge(l1_ready, m)
                nc.vector.tensor_copy(xT.rearrange("p k t -> p (k t)"), bank(0)[:, 0:D]).then_inc(xT_ready, 1)

            def raw_out(dst, src, product, used, done, m, first_tile):
                dve.wait_ge(product, m + 1)
                if not first_tile:
                    dve.wait_ge(used, m)
                nc.vector.tensor_copy(dst, bank(src)).then_inc(done, 1)

            def y_out(m):
                e = dve.value_load(owner[0:1, bass.ds(m, 1)], min_val=0, max_val=NE - 1)
                dve.wait_ge(l3_ready, m + 1)
                dve.wait_ge(y_ready, m + 1)
                nc.vector.tensor_tensor(yraw, bank(5)[:, 0:D], b3_sb[:, bass.ds(e, 1), :].rearrange("p e d -> p (e d)"),
                                        ALU.add).then_inc(y_read, 1)
                dve.wait_ge(y_read, m + 2)
                dve.wait_ge(home_ready, m + 1)
                nc.vector.tensor_scalar(yout, yraw, home_gain[:, bass.ds(2 * m + 1, 1)], None, ALU.mult).then_inc(y_ready, 1)

            def expert_step(m, first_tile=False, left=MT):
                raw_out(raw2, 3, l2_ready, t2_ready, r2_ready, m, first_tile)
                if not first_tile:
                    y_out(m - 1)
                if left >= 2:
                    raw_out(raw1, 1, l1_ready, t1_ready, r1_ready, m + 2, False)
                if left >= 3:
                    x_out(m + 3, False)

            def add_projection(b):
                dve.wait_ge(proj_ready, b + 1)
                both = res[:, 2 * b:2 * b + 2, :].rearrange("p t d -> p (t d)")
                nc.vector.tensor_tensor(both, both, bank(2 * b), ALU.add).then_inc(proj_added, 1)

            dve.wait_ge(bias_added, 1)
            add_projection(0)
            add_projection(1)
            x_out(0, True)
            add_projection(2)
            add_projection(3)
            raw_out(raw1, 1, l1_ready, t1_ready, r1_ready, 0, True)
            x_out(1, False)
            raw_out(raw1, 1, l1_ready, t1_ready, r1_ready, 1, False)
            x_out(2, False)
            expert_step(0, first_tile=True)
            dve.wait_ge(homes_loaded, 16)
            dve.wait_ge(L["b3"], 16)
            with dve.Fori(1, MT - 3) as m:
                expert_step(m)
            for left in (2, 1, 0):
                expert_step(MT - 1 - left, left=left)
            y_out(MT - 1)


def _layouts(v):
    import numpy as np

    f = lambda n: np.ascontiguousarray(v[n])
    wx = f("L0_attn_W_x")
    bc = wx[RANK:].T
    cols = lambda a: a.reshape(-1, P).T
    attn_b = f("L1_attn_c_attn_b")
    one = lambda n: np.broadcast_to(f(n).reshape(1, 1), (P, 1))
    vecs = np.concatenate([
        cols(f("L0_attn_b_dt")), cols(f("L0_attn_D")),
        f("L0_attn_A_log").reshape(DH, P, NS).transpose(1, 0, 2).reshape(P, DH * NS),
        cols(attn_b[:2 * D]), f("L1_attn_cam_gate").reshape(P, 1), one("L1_attn_cam_w0"), one("L1_attn_cam_w1"),
        cols(f("L1_ffn_b1").reshape(-1)), cols(f("L1_ffn_b2").reshape(-1)),
        f("L1_ffn_Wg").reshape(DH, P, NE).transpose(1, 0, 2).reshape(P, DH * NE)], axis=1)
    rows = np.concatenate([attn_b[2 * D:], f("L1_attn_c_proj_b"), f("L1_ffn_bg")])
    had = np.ones((1, 1), np.float32)
    while had.shape[0] < P:
        had = np.block([[had, had], [had, -had]])
    consts = np.concatenate([np.eye(P), had, np.broadcast_to(np.arange(NE, 0, -1), (P, NE)),
                             np.broadcast_to(np.arange(MT), (P, MT))], axis=1).astype(np.float32)
    one_bf16 = 0x3F80
    bconsts = (np.concatenate([np.triu(np.ones((P, P)), 1), np.ones((P, P))], axis=1) * one_bf16).astype(np.uint16)
    sel = np.zeros((P, 2 * NS, P), np.uint16)
    for s in range(2 * NS):
        for part in range(3):
            sel[32 * part + s, s, :] = one_bf16
    return {
        "x": f("L0_attn_x").reshape(TOK, D), "wx": np.concatenate([wx[:RANK].T, bc, bc, bc], axis=1),
        "wdt": f("L0_attn_W_dt").T, "w1": f("L0_ffn_W1").T, "w3": f("L0_ffn_W3").T, "w2": f("L0_ffn_W2").T,
        "vecs": vecs, "rows": np.broadcast_to(rows[None], (P, R_END)), "consts": consts, "bconsts": bconsts,
        "sel": sel.reshape(P, -1), "cattn": f("L1_attn_c_attn_w"), "cproj": f("L1_attn_c_proj_w"),
        "mw1": f("L1_ffn_W1"), "mw2": f("L1_ffn_W2"), "mw3": f("L1_ffn_W3"), "b3": f("L1_ffn_b3"),
        "zeros": np.zeros((MT * P, D), np.float32),
        "home_of": np.stack([np.arange(2 * NT)[None] % NT * P + np.arange(P)[:, None], np.zeros((P, 2 * NT))],
                            axis=2).astype(np.int32).reshape(P, 4 * NT),
        "no_home": np.stack([np.arange(TOK, TOK + MT * P).reshape(MT, P).T, np.zeros((P, MT))],
                            axis=2).astype(np.int32).reshape(P * MT, 2),
    }


def kernel(**inputs):
    import numpy as np
    import concourse.bacc as bacc
    from concourse.bass_utils import run_bass_kernel_spmd

    nc = bacc.Bacc("TRN2", target_bir_lowering=False, num_devices=1)
    arrays = {f"in_{n}": np.ascontiguousarray(a) for n, a in _layouts(inputs).items()}
    args = [nc.dram_tensor(n, a.shape, mybir.dt.from_np(a.dtype), kind="ExternalInput").ap() for n, a in arrays.items()]
    result = nc.dram_tensor("out_0", (TOK, D), F32, kind="ExternalOutput").ap()
    build(nc, *args, result)
    got = run_bass_kernel_spmd(nc, [arrays], core_ids=[0]).results[0]["out_0"]
    return got.reshape(BATCH, SEQ, D)
```

```python
from contextlib import ExitStack

import concourse.bass as bass
from concourse import mybir

F32 = mybir.dt.float32
BF16 = mybir.dt.bfloat16
I32 = mybir.dt.int32
U32 = mybir.dt.uint32
ALU = mybir.AluOpType
ACT = mybir.ActivationFunctionType
AX = mybir.AxisListType

P = 128
BATCH, SEQ, D = 4, 256, 256
TOK = BATCH * SEQ
NT = TOK // P
DH = D // P
NS, RANK = 16, 64
H0 = 1024
HC = H0 // P
QT_ = 4
QW = TOK // QT_
UNITS = NS * DH
UPQ = UNITS // QT_
NE, HM = 8, 512
KM = HM // P
MT = 2 * NT + NE - 1
QK_ORDER = ((0, 0), (4, 2), (1, 1), (5, 3), (2, 4), (6, 5), (3, 6), (7, 4))
OWN = 112
BANK_OF_V = (0, 2, 4, 5, 1, 3, 6, 7)
EPS = 1e-5
SCALE = 0.25

V_BDT, V_D, V_ALOG, V_QKB, V_GATE, V_W0, V_W1, V_B1, V_B2, V_WG, V_END = (
    0, 2, 4, 36, 40, 41, 42, 43, 75, 107, 123)
R_VB, R_PB, R_BG, R_END = 0, 256, 512, 520
C_ID, C_HAD, C_KEY, C_TILE, C_END = 0, 128, 256, 264, 264 + MT
B_TRI, B_ONE, B_END = 0, 128, 256


def build(nc, x, wx, wdt, w1, w3, w2, vecs, rows, consts, bconsts, sel, cattn, cproj,
          mw1, mw2, mw3, b3, zeros, home_of, no_home, out):
    assert UPQ == HC and UNITS == QT_ * UPQ

    with ExitStack() as ctx:
        def sb(name, shape, dt=F32):
            return ctx.enter_context(nc.sbuf_tensor(name, shape, dt))

        def sem(name):
            return ctx.enter_context(nc.semaphore(name))

        moe_w1 = sb("moe_w1", [P, NE, 2, HM])
        moe_w2 = sb("moe_w2", [P, NE, KM, HM])
        moe_w3 = sb("moe_w3", [P, NE, KM, D])
        loan3 = moe_w3[:].rearrange("p e k n -> p (e k n)")
        gate_w = loan3[:, 0:2048].rearrange("p (k h) -> p k h", k=DH)
        lin_w = loan3[:, 2048:4096].rearrange("p (k h) -> p k h", k=DH)
        down_w = loan3[:, 4096:6144]
        sel_w = loan3[:, 6144:8192].bitcast(BF16).rearrange("p (s m) -> p s m", m=P)
        loan2 = moe_w2[:, 6:8].rearrange("p e k n -> p (e k n)")
        ffn_out = loan2[:, 0:2048].rearrange("p (k t) -> p k t", k=DH)
        fly = loan2[:, 2048:4096]
        loan1 = moe_w1[:, 6:8].rearrange("p e k n -> p (e k n)")
        gl = [loan1[:, 512 * i:512 * i + 512] for i in range(2)]
        th = [loan1[:, 1024 + QW * i:1024 + QW * i + QW] for i in range(2)]
        hid = [loan1[:, 1536 + QW * i:1536 + QW * i + QW] for i in range(2)]

        res = sb("res", [P, NT, D])
        nrmT = sb("nrmT", [P, DH, TOK])
        area_c = sb("area_c", [P, 2048])
        nrm = area_c[:].rearrange("p (t d) -> p t d", t=NT)
        yacc = area_c[:].rearrange("p (k t) -> p k t", k=DH)
        area_d = sb("area_d", [P, 2048])
        delta = area_d[:].rearrange("p (k t) -> p k t", k=DH)
        qT = area_d[:].rearrange("p (k t) -> p k t", k=DH)
        area_e = sb("area_e", [P, 2048])
        du = area_e[:].rearrange("p (k t) -> p k t", k=DH)
        kT = area_e[:].rearrange("p (k t) -> p k t", k=DH)
        area_f = sb("area_f", [P, 2048])
        decay = area_f[:].rearrange("p (i t) -> p i t", i=2)
        val = area_f[:].rearrange("p (t d) -> p t d", t=NT)
        area_g = sb("area_g", [P, 2048])
        state = area_g[:].rearrange("p (i t) -> p i t", i=2)
        ctxT = area_g[:].rearrange("p (k t) -> p k t", k=DH)
        area_h = sb("area_h", [P, 2048])
        bc_split = area_h[:, 0:512].bitcast(BF16)
        wx_sb = area_h[:, 512:832].rearrange("p (k m) -> p k m", k=DH)
        wdt_sb = area_h[0:RANK, 832:1088]
        cattn_sb = sb("cattn_sb", [P, DH, 3 * D + NE])
        cproj_sb = sb("cproj_sb", [P, DH, D])
        vec = sb("vec", [P, V_END])
        row = sb("row", [P, R_END])
        cst = sb("cst", [P, C_END])
        bcst = sb("bcst", [P, B_END], BF16)
        ident = cst[:, C_ID:C_ID + P]
        hadamard = cst[:, C_HAD:C_HAD + P]
        amat = sb("amat", [P, 2 * NS])
        st6 = sb("st6", [P, NT, 6])
        mv = sb("mv", [P, NT, 2])
        ln_v = sb("ln_v", [P, NT])
        ln_s = sb("ln_s", [P, NT])
        ln_r = sb("ln_r", [P, NT])
        ln_t = sb("ln_t", [P, NT])

        gw = [area_g[:, 64 * i:64 * i + 64].rearrange("p (t e) -> p t e", e=NE) for i in range(7)]
        logit, expd, first, second, keyed, place, tmp64 = gw
        hits = area_g[:, 512:512 + MT * NE].rearrange("p (m e) -> p m e", e=NE)
        g8 = [area_g[:, 768 + 8 * i:776 + 8 * i] for i in range(10)]
        top, esum, keymax, top2, e2, ones8, tiles8, upto8, base8, slotf = g8
        tile_int = area_g[:, 860:868].bitcast(I32)
        owner_f = area_g[:, 872:872 + MT]
        mask = sb("mask", [P, NT, NE], BF16)
        slot = sb("slot", [P, 2, NT], U32)
        home_slot = sb("home_slot", [P, 2, NT], U32)
        owner = sb("owner", [P, MT], I32)
        lw = sb("lw", [P, 2])
        probs = area_h[:].rearrange("p (b i t) -> p b i t", b=BATCH, i=2)
        probsT = nrmT[:].rearrange("p k t -> p (k t)").rearrange("p (b k t) -> p b k t", b=BATCH, k=2)
        smax = sb("smax", [P, 2, BATCH, 2])
        ssum = sb("ssum", [P, 2, BATCH, 2])
        sinv = sb("sinv", [P, 2, BATCH, 2])
        home_sb = sb("home_sb", [P, 2 * NT, 2], I32)
        gain = home_sb[:].bitcast(F32).rearrange("p (k t) two -> p k t two", k=2)[:, :, :, 1]
        homes = sb("homes_sb", [P, 2 * MT], I32)
        home_gain = homes[:].bitcast(F32)
        home = sb("home", [P, 1], I32)
        home_seen = sb("home_seen", [P, 1], I32)
        xin = [area_c[:, D * i:D * i + D] for i in range(4)]
        xT = sb("xT", [P, D])[:].rearrange("p (k t) -> p k t", k=DH)
        raw1 = area_d[:, 512:1024]
        raw2 = area_d[:, 1024:1536]
        yraw = area_d[:, 1536:1792]
        yout = area_d[:, 1792:2048]
        b3_sb = area_h[:].rearrange("p (e d) -> p e d", e=NE)
        h1T = area_e[:, 0:512].rearrange("p (k t) -> p k t", k=KM)
        h2T = area_e[:, 512:1024].rearrange("p (k t) -> p k t", k=KM)
        xbuf = nc.dram_tensor("dispatched", (MT * P, D), F32, kind="Internal").ap()
        home_buf = nc.dram_tensor("homes", (P * MT, 2), I32, kind="Internal").ap()
        sums = nc.dram_tensor("sums", (TOK + MT * P, D), F32, kind="Internal").ap()

        psum = ctx.enter_context(nc.psum_tensor("psum", [P, 8, 512], F32))

        def bank(i, n=1):
            return psum[:, i:i + n, :].rearrange("p b n -> p (b n)")

        L = {n: sem(f"load_{n}") for n in ("x", "x2", "wx", "wdt", "w1", "w3", "w2", "vec", "row", "cst", "bcst", "sel",
                                           "cattn", "cproj", "zero", "mw1", "mw2", "mw1_late", "mw2_late", "mw3", "b3",
                                           "home", "no_home", "zero_sums")}
        dve_chain, act_chain = sem("dve_chain"), sem("act_chain")
        out_done = sem("out_done")
        stats_done = sem("stats_done")
        var_ready, sqrt_ready, nrm_ready, front_nrmT, rear_nrmT = (
            sem("var_ready"), sem("sqrt_ready"), sem("nrm_ready"), sem("front_nrmT"), sem("rear_nrmT"))
        turned = sem("turned")
        fly_ready, had_ready, down_ready = sem("fly_ready"), sem("had_ready"), sem("down_ready")
        rank_ready, rank_copied, bc_ready, bc_done = sem("rank_ready"), sem("rank_copied"), sem("bc_ready"), sem("bc_done")
        z_ready, absexp_done, onepl_done, log_done, amat_ready, delta_ready, z_read = (
            sem("z_ready"), sem("absexp_done"), sem("onepl_done"), sem("log_done"), sem("amat_ready"),
            sem("delta_ready"), sem("z_read"))
        decay_zero, less_lost, delta1_ready, du1_ready = (
            sem("decay_zero"), sem("less_lost"), sem("delta1_ready"), sem("du1_ready"))
        b_ready, c_ready, decay_ready = sem("b_ready"), sem("c_ready"), sem("decay_ready")
        own_added = sem("own_added")
        bx_done, scan_done, yc_done, y_added = sem("bx_done"), sem("scan_done"), sem("yc_done"), sem("y_added")
        up_ready, up_read, th_ready, prod_done, hid_ready, hid_used, acc_free = (
            sem("up_ready"), sem("up_read"), sem("th_ready"), sem("prod_done"), sem("hid_ready"), sem("hid_used"),
            sem("acc_free"))
        sumT_ready, late_sumT_ready, back_ready, x1_ready = (
            sem("sumT_ready"), sem("late_sumT_ready"), sem("back_ready"), sem("x1_ready"))

        z2_ready, lw_ready = sem("z2_ready"), sem("lw_ready")
        soft_in, soft_out, top2_ready, e2_ready, mask_ready, prefix_ready, slots_ready = (
            sem("soft_in"), sem("soft_out"), sem("top2_ready"), sem("e2_ready"),
            sem("mask_ready"), sem("prefix_ready"), sem("slots_ready"))
        owner_ready = sem("owner_ready")
        scattered, homes_scattered, homes_loaded, home_ready, home_read = (
            sem("scattered"), sem("homes_scattered"), sem("homes_loaded"), sem("home_ready"), sem("home_read"))
        bias_added, proj_added = sem("bias_added"), sem("proj_added")
        qk_ready, qk_done, v_ready, v_done = sem("qk_ready"), sem("qk_done"), sem("v_ready"), sem("v_done")
        scores_ready, bias_ready, exp_done, probs_ready, probsT_ready, probsT_done = (
            sem("scores_ready"), sem("bias_ready"), sem("exp_done"), sem("probs_ready"), sem("probsT_ready"),
            sem("probsT_done"))
        context_ready, tanh_done, query_done, ctx_done = (
            sem("context_ready"), sem("tanh_done"), sem("query_done"), sem("ctx_done"))
        x_loaded, x_turned, xT_ready, l1_ready, r1_ready, t1_ready, h1_ready = (
            sem("x_loaded"), sem("x_turned"), sem("xT_ready"), sem("l1_ready"), sem("r1_ready"), sem("t1_ready"),
            sem("h1_ready"))
        l2_ready, r2_ready, t2_ready, h2_ready, l3_ready, y_ready, y_stored = (
            sem("l2_ready"), sem("r2_ready"), sem("t2_ready"), sem("h2_ready"), sem("l3_ready"), sem("y_ready"),
            sem("y_stored"))
        y_read, proj_ready, sums_ready = sem("y_read"), sem("proj_ready"), sem("sums_ready")

        block = ctx.enter_context(nc.Block())

        def attention_steps():
            return [[(s // 3, s % 3, b) for b in range(BATCH) for s in [d - b // 2] if 0 <= s < 6]
                    for d in range(BATCH // 2 + 5)]

        def nth(which, b):
            turns = sorted((3 * p + i // 2, i, p) for p in range(2) for i in range(BATCH))
            return turns.index((3 * which + b // 2, b, which)) + 1

        def n_of(q, c):
            return q * (UPQ // DH) + c // DH

        @block.sync
        def _(sp):
            x_t = x.rearrange("(t p) d -> p t d", p=P)
            sp.dma_start(res[:, 0:4, :], x_t[:, 0:4, :]).then_inc(L["x"], 16)
            sp.dma_start(cst[:], consts).then_inc(L["cst"], 16)
            sp.dma_start(res[:, 4:8, :], x_t[:, 4:8, :]).then_inc(L["x2"], 16)
            sp.dma_start(vec[:], vecs).then_inc(L["vec"], 16)
            sp.dma_start(down_w.rearrange("p (c d) -> p c d", c=HC),
                         w2.rearrange("(c p) d -> p c d", p=P)).then_inc(L["w2"], 16)
            sp.dma_start(wx_sb, wx.rearrange("(k p) m -> p k m", p=P)).then_inc(L["wx"], 16)
            sp.dma_start(wdt_sb, wdt).then_inc(L["wdt"], 16)
            sp.dma_start(sel_w, sel.bitcast(BF16).rearrange("p (s m) -> p s m", m=P)).then_inc(L["sel"], 16)
            sp.dma_start(gate_w, w1.rearrange("(k p) h -> p k h", p=P)).then_inc(L["w1"], 16)
            sp.dma_start(lin_w, w3.rearrange("(k p) h -> p k h", p=P)).then_inc(L["w3"], 16)
            sp.dma_start(bcst[:], bconsts.bitcast(BF16)).then_inc(L["bcst"], 16)
            sp.dma_start(row[:], rows).then_inc(L["row"], 16)
            sp.dma_start(cattn_sb[:, :, 0:3 * D], cattn.rearrange("(k p) n -> p k n", p=P)).then_inc(L["cattn"], 16)
            sp.dma_start(cproj_sb[:], cproj.rearrange("(k p) n -> p k n", p=P)).then_inc(L["cproj"], 16)
            e1 = mw1.rearrange("e (k p) n -> p e k n", p=P)
            e2_ = mw2.rearrange("e (k p) n -> p e k n", p=P)
            e3 = mw3.rearrange("e (k p) n -> p e k n", p=P)
            sp.dma_start(xbuf, zeros).then_inc(L["zero"], 16)
            sp.dma_start(sums[TOK:], zeros).then_inc(L["zero_sums"], 16)
            sp.dma_start(home_buf, no_home).then_inc(L["no_home"], 16)
            sp.dma_start(home_sb[:], home_of.rearrange("p (n two) -> p n two", two=2)).then_inc(L["home"], 16)
            for e in range(6):
                sp.dma_start(moe_w1[:, e], e1[:, e]).then_inc(L["mw1"], 16)
                sp.dma_start(moe_w2[:, e], e2_[:, e]).then_inc(L["mw2"], 16)
            sp.wait_ge(hid_used, UNITS + 2)
            sp.wait_ge(b_ready, UNITS)
            sp.wait_ge(c_ready, UNITS // DH)
            for e in (6, 7):
                sp.dma_start(moe_w1[:, e], e1[:, e]).then_inc(L["mw1_late"], 16)
            for e in range(NE):
                sp.dma_start(moe_w3[:, e], e3[:, e]).then_inc(L["mw3"], 16)
            sp.wait_ge(sumT_ready, 2)
            sp.wait_ge(late_sumT_ready, 2)
            for e in (6, 7):
                sp.dma_start(moe_w2[:, e], e2_[:, e]).then_inc(L["mw2_late"], 16)
            def load_x(m, buffer=3):
                sp.dma_start(xin[buffer], xbuf[bass.ds(m * P, P), :]).then_inc(x_loaded, 16)

            sp.wait_ge(scattered, 16 * 2 * NT)
            for m in range(4):
                load_x(m, buffer=m)
            sp.wait_ge(probsT_ready, 2 * BATCH)
            sp.dma_start(b3_sb, b3.unsqueeze(0).to_broadcast([P, NE, D])).then_inc(L["b3"], 16)
            sp.wait_ge(proj_added, BATCH)
            sp.dma_start(sums[0:TOK].rearrange("(t p) d -> p t d", p=P), res[:]).then_inc(sums_ready, 16)
            sp.wait_ge(homes_scattered, 16 * 2 * NT)
            sp.dma_start(homes[:], home_buf.rearrange("(p m) two -> p (m two)", p=P)).then_inc(homes_loaded, 16)
            with sp.Fori(1, MT - 3) as m:
                sp.wait_ge(x_turned, m + 3)
                load_x(m + 3)
            sp.wait_ge(y_stored, 16 * MT)
            sp.dma_start(out[0:TOK // 2], sums[0:TOK // 2]).then_inc(out_done, 16)
            sp.wait_ge(out_done, 32)

        @block.gpsimd
        def _(pool):
            nc.gpsimd.memset(bc_split[96:128, :], 0.0).then_inc(hid_ready, 2)
            pool.wait_ge(hid_ready, 2)
            pool.wait_ge(L["w2"], 16)
            src, dst = down_w, fly
            done = 0
            for stage, half in enumerate((1, 2, 4)):
                a = src.rearrange("p (g two n) -> p g two n", two=2, n=half * D)
                o = dst.rearrange("p (g two n) -> p g two n", two=2, n=half * D)
                if stage:
                    pool.wait_ge(fly_ready, 2 * stage)
                nc.gpsimd.tensor_tensor(o[:, :, 0, :], a[:, :, 0, :], a[:, :, 1, :], ALU.add).then_inc(fly_ready, 1)
                nc.gpsimd.tensor_tensor(o[:, :, 1, :], a[:, :, 0, :], a[:, :, 1, :], ALU.subtract).then_inc(fly_ready, 1)
                src, dst = dst, src
            for k in range(DH):
                pool.wait_ge(z_read, 2 * k + 2)
                pool.wait_ge(onepl_done, k + 1)
                nc.gpsimd.tensor_tensor(delta[:, k, :], delta[:, k, :], area_g[:, TOK * k:TOK * k + TOK],
                                        ALU.subtract).then_inc(less_lost, 1)
            pool.wait_ge(less_lost, 2)
            pool.wait_ge(log_done, 2)
            nc.gpsimd.tensor_tensor(delta[:, 1, :], delta[:, 1, :], loan2[:, TOK:2 * TOK], ALU.add).then_inc(delta1_ready, 1)
            pool.wait_ge(delta1_ready, 1)
            pool.wait_ge(front_nrmT, 2)
            pool.wait_ge(rear_nrmT, 2)
            pool.wait_ge(bc_done, 5)
            nc.gpsimd.tensor_tensor(du[:, 1, :], delta[:, 1, :], nrmT[:, 1, :], ALU.mult).then_inc(du1_ready, 1)

            def add_state(c):
                nc.gpsimd.tensor_tensor(yacc[:, c % 2, OWN:], yacc[:, c % 2, OWN:], state[:, c % 2, OWN:],
                                        ALU.add).then_inc(y_added, 1)

            def unit(q, c, late=False, last=False):
                u = q * UPQ + c
                g = gl[c % 2]
                pool.wait_ge(th_ready, u + 1)
                nc.gpsimd.tensor_tensor(g[:, 0:QW], g[:, 0:QW], g[:, QW:2 * QW], ALU.mult).then_inc(prod_done, 1)
                pool.wait_ge(prod_done, u + 1)
                pool.wait_ge(hid_used, u + 1)
                nc.gpsimd.tensor_tensor(hid[c % 2], g[:, 0:QW], th[c % 2], ALU.mult).then_inc(hid_ready, 1)
                if late:
                    return
                n = u - last
                pool.wait_ge(yc_done, n + 2)
                pool.wait_ge(y_added, n + 1)
                add_state(c - last)

            with pool.Fori(0, QT_ - 1) as q:
                for c in range(UPQ):
                    unit(q, c)
            for c in range(UPQ):
                unit(QT_ - 1, c, late=(c == UPQ - 2), last=(c == UPQ - 1))

            pool.wait_ge(acc_free, QT_ + 1)
            pool.wait_ge(y_added, UNITS + 2)
            for g in (2, 3):
                t = slice(g * QW, g * QW + QW)
                nc.gpsimd.tensor_tensor(yacc[:, :, t], yacc[:, :, t], ffn_out[:, :, t], ALU.add).then_inc(late_sumT_ready, 1)

            pool.wait_ge(nrm_ready, 2 * NT)
            pool.wait_ge(L["row"], 16)
            nc.gpsimd.tensor_tensor(res[:], res[:], row[:, R_PB:R_PB + D].unsqueeze(1).to_broadcast([P, NT, D]),
                                    ALU.add).then_inc(bias_added, 1)

            def at(slots, k, t):
                return bass.IndirectOffsetOnAxis(ap=slots[:, k, t:t + 1], axis=0)

            pool.wait_ge(L["zero"], 16)
            pool.wait_ge(slots_ready, 1)
            for t in range(NT):
                for k in range(2):
                    pool.indirect_dma_start(out=xbuf, out_offset=at(slot, k, t), in_=nrm[:, t, :],
                                            in_offset=None).then_inc(scattered, 16)
            pool.wait_ge(slots_ready, 2)
            pool.wait_ge(L["no_home"], 16)
            pool.wait_ge(L["home"], 16)
            for t in range(NT):
                for k in range(2):
                    pool.indirect_dma_start(out=home_buf, out_offset=at(home_slot, k, t),
                                            in_=home_sb[:, k * NT + t, :],
                                            in_offset=None).then_inc(homes_scattered, 16)
            def store_y(m):
                nc.gpsimd.tensor_copy(home[:], homes[:, bass.ds(2 * m, 1)]).then_inc(home_ready, 1)
                pool.wait_ge(home_ready, m + 1)
                pool.wait_ge(y_ready, m + 2)
                nc.gpsimd.tensor_tensor(home_seen[:], home[:], home[:], ALU.add).then_inc(home_read, 1)
                pool.indirect_dma_start(out=sums, out_offset=bass.IndirectOffsetOnAxis(ap=home[:, 0:1], axis=0),
                                        in_=yout, in_offset=None, compute_op=ALU.add).then_inc(y_stored, 16)

            pool.wait_ge(homes_loaded, 16)
            pool.wait_ge(L["zero_sums"], 16)
            pool.wait_ge(sums_ready, 16)
            store_y(0)
            with pool.Fori(1, MT) as m:
                pool.wait_ge(home_read, m)
                pool.wait_ge(y_stored, 16 * m)
                store_y(m)

        @block.scalar
        def _(act):
            def turned_out(phase):
                for part, half_ready in enumerate((front_nrmT, rear_nrmT)):
                    act.wait_ge(turned, 4 * phase + 2 * part + 1)
                    nc.scalar.copy(nrmT[:, 0, 512 * part:512 * part + 512], bank(part)).then_inc(half_ready, 1)

            def down_out(groups):
                for g in groups:
                    act.wait_ge(had_ready, g + 1)
                    nc.scalar.mul(down_w[:, 512 * g:512 * g + 512], bank((0, 1, 6, 7)[g]), 0.5 / H0 ** 0.5).then_inc(down_ready, 1)

            act.wait_ge(var_ready, 1)
            nc.scalar.activation(ln_s[:], ln_v[:], ACT.Sqrt).then_inc(sqrt_ready, 1)
            act.wait_ge(L["vec"], 16)
            nc.scalar.activation(amat[:], vec[:, V_ALOG:V_ALOG + 2 * NS], ACT.Exp).then_inc(act_chain, 1)
            act.wait_ge(act_chain, 1)
            nc.scalar.mul(amat[:], amat[:], -1.0).then_inc(amat_ready, 1)
            turned_out(0)
            for t in range(2):
                act.wait_ge(rank_ready, t + 1)
                nc.scalar.copy(area_f[0:RANK, 512 * t:512 * t + 512], bank(t)[0:RANK, :]).then_inc(rank_copied, 1)
            act.wait_ge(front_nrmT, 2)
            act.wait_ge(rear_nrmT, 2)
            for k in range(DH):
                nc.scalar.activation(yacc[:, k, :], nrmT[:, k, :], ACT.Copy, scale=vec[:, V_D + k:V_D + k + 1]).then_inc(y_added, 1)
            for k in range(DH):
                z, e = bank(2 + 2 * k, 2), area_g[:, TOK * k:TOK * k + TOK]
                act.wait_ge(z_ready, k + 1)
                nc.scalar.activation(e, z, ACT.Abs, bias=vec[:, V_BDT + k:V_BDT + k + 1]).then_inc(z_read, 1)
                act.wait_ge(z_read, 2 * k + 1)
                nc.scalar.activation(e, e, ACT.Exp, scale=-1.0).then_inc(absexp_done, 1)
                nc.scalar.activation(delta[:, k, :], z, ACT.Relu, bias=vec[:, V_BDT + k:V_BDT + k + 1]).then_inc(z_read, 1)
            act.wait_ge(bc_ready, 2)
            act.wait_ge(hid_ready, 2)
            nc.scalar.copy(bc_split[0:96, :], bank(6, 2)[0:96, :]).then_inc(bc_done, 1)
            down_out(range(2))
            for k in range(DH):
                act.wait_ge(onepl_done, k + 1)
                nc.scalar.activation(loan2[:, TOK * k:TOK * k + TOK], loan2[:, TOK * k:TOK * k + TOK],
                                     ACT.Ln).then_inc(log_done, 1)
            act.wait_ge(z2_ready, 1)
            nc.scalar.activation(lw[:, 1:2], lw[:, 0:1], ACT.Tanh, scale=0.5).then_inc(lw_ready, 1)
            down_out(range(2, 4))

            act.wait_ge(decay_zero, 1)
            act.wait_ge(delta_ready, 1)

            def decays(q, c):
                act.wait_ge(scan_done, q * UPQ + c + 1)
                nc.scalar.activation(decay[:, c % 2, :].rearrange("p (b t) -> p b t", b=BATCH)[:, :, 1:SEQ],
                                     delta[:, c % 2, :].rearrange("p (b t) -> p b t", b=BATCH)[:, :, 1:SEQ],
                                     ACT.Exp, scale=amat[:, bass.ds((c % DH) * NS + n_of(q, c), 1)]).then_inc(decay_ready, 1)

            def unit(q, c, last_quarter):
                u = q * UPQ + c
                if not (last_quarter and c == UPQ - 1):
                    decays(*((q, c + 1) if c + 1 < UPQ else (q + 1, 0)))
                act.wait_ge(up_ready, u + 1)
                act.wait_ge(hid_ready, u + 1)
                nc.scalar.copy(gl[c % 2], bank(6)).then_inc(up_read, 1)
                nc.scalar.activation(th[c % 2], bank(6)[:, 0:QW], ACT.Tanh, scale=0.5).then_inc(up_read, 1)
                act.wait_ge(up_read, 2 * u + 4)
                nc.scalar.add(th[c % 2], th[c % 2], 1.0).then_inc(th_ready, 1)

            def quarter(q, last_quarter):
                for c in range(1, UPQ):
                    unit(q, c, last_quarter)
                if not last_quarter:
                    unit(q + 1, 0, False)
                act.wait_ge(hid_used, q * UPQ + UPQ + 2)
                nc.scalar.copy(ffn_out[:, :, bass.ds(q * QW, QW)],
                               bank(7).rearrange("p (k t) -> p k t", k=DH)).then_inc(acc_free, 1)

            act.wait_ge(amat_ready, 1)
            decays(0, 0)
            act.wait_ge(delta1_ready, 1)
            unit(0, 0, False)
            with act.Fori(0, QT_ - 1) as q:
                quarter(q, False)
            quarter(QT_ - 1, True)

            act.wait_ge(var_ready, 2)
            nc.scalar.activation(ln_s[:], ln_v[:], ACT.Sqrt).then_inc(sqrt_ready, 1)
            turned_out(1)

            def qk_out(i):
                g, b = QK_ORDER[i]
                m, t = g // 2, g % 2
                act.wait_ge(qk_ready, i + 1)
                dst = (qT, kT)[m // 2][:, m % 2, 512 * t:512 * t + 512]
                nc.scalar.activation(dst, bank(b), ACT.Identity, bias=vec[:, V_QKB + m:V_QKB + m + 1]).then_inc(qk_done, 1)

            act.wait_ge(soft_in, 1)
            nc.scalar.activation(expd, logit, ACT.Exp).then_inc(soft_out, 1)
            for i in range(2):
                qk_out(i)
            act.wait_ge(top2_ready, 1)
            nc.scalar.activation(e2, top2, ACT.Exp).then_inc(e2_ready, 1)
            for i in range(2, 4):
                qk_out(i)

            def attention_round(steps):
                for which, step, b in steps:
                    a_bank, b_bank = (2 * b, 2 * b + 1) if which == 0 else (2 * b + 1, 2 * b)
                    if step == 0:
                        act.wait_ge(bias_ready, nth(which, b))
                        for i in range(2):
                            nc.scalar.activation(probs[:, b, i, :], bank(a_bank)[:, SEQ * i:SEQ * i + SEQ], ACT.Exp,
                                                 bias=smax[:, which, b, i:i + 1], scale=SCALE,
                                                 accum_out=ssum[:, which, b, i:i + 1]).then_inc(exp_done, 1)
                    if step == 1:
                        act.wait_ge(probsT_ready, nth(which, b))
                        nc.scalar.copy(probsT[:, b].rearrange("p k t -> p (k t)"), bank(b_bank)).then_inc(probsT_done, 1)
                    if step == 2 and which == 0:
                        act.wait_ge(context_ready, nth(0, b))
                        nc.scalar.activation(probs[:, b, 0, :], bank(a_bank)[:, 0:SEQ], ACT.Tanh,
                                             scale=vec[:, V_GATE:V_GATE + 1]).then_inc(tanh_done, 1)
                    if step == 2 and which == 1:
                        act.wait_ge(context_ready, nth(1, b))
                        act.wait_ge(slots_ready, 2)
                        nc.scalar.copy(ctxT[:, :, SEQ * b:SEQ * b + SEQ],
                                       bank(a_bank).rearrange("p (k t) -> p k t", k=DH)).then_inc(ctx_done, 1)


            first_round, *rounds = attention_steps()
            attention_round(first_round)
            for i in range(4, 8):
                qk_out(i)
            for steps in rounds:
                attention_round(steps)
            nc.scalar.activation(ln_s[:, 0:1], amat[:, 0:1], ACT.Gelu)

            def gelus(src, dst, bias_col, e, done):
                for k in range(KM):
                    last = nc.scalar.activation(dst[:, k, :], bank(src)[:, P * k:P * k + P], ACT.Gelu,
                                                bias=vec[:, bass.ds(bias_col + KM * e + k, 1)])
                last.then_inc(done, 1)

            def layer1_out(m, first_tile=False):
                e = act.value_load(owner[0:1, bass.ds(m, 1)], min_val=0, max_val=NE - 1)
                act.wait_ge(t1_ready, m + 1)
                if not first_tile:
                    act.wait_ge(l2_ready, m)
                gelus(2, h1T, V_B1, e, h1_ready)

            def layer2_out(m, first_tile=False):
                e = act.value_load(owner[0:1, bass.ds(m, 1)], min_val=0, max_val=NE - 1)
                act.wait_ge(t2_ready, m + 1)
                if not first_tile:
                    act.wait_ge(l3_ready, m)
                gelus(4, h2T, V_B2, e, h2_ready)

            act.wait_ge(owner_ready, 1)
            layer1_out(0, first_tile=True)
            layer1_out(1)
            layer2_out(0, first_tile=True)
            with act.Fori(1, MT - 1) as m:
                layer1_out(m + 1)
                layer2_out(m)
            layer2_out(MT - 1)
            act.wait_ge(y_stored, 16 * MT)
            act.dma_start(out[TOK // 2:], sums[TOK // 2:TOK]).then_inc(out_done, 16)

        @block.tensor
        def _(pe):
            pe.wait_ge(L["cst"], 16)

            def turn_tiles(phase):
                for part in range(2):
                    for k in range(DH):
                        for j in range(4):
                            t = 4 * part + j
                            if k == 0:
                                pe.wait_ge(nrm_ready, phase * NT + t + 1)
                            last = nc.tensor.transpose(bank(2 * k + part)[:, P * j:P * j + P], nrm[:, t, P * k:P * k + P], ident)
                        last.then_inc(turned, 1)

            def keep_warm(products):
                for _ in range(products):
                    nc.tensor.matmul(bank(7)[:, 0:2 * P], hadamard, cst[:, C_ID:C_ID + 2 * P], start=True, stop=True)

            keep_warm(7)
            turn_tiles(0)
            pe.wait_ge(L["wx"], 16)
            def project_norm(cols, b, ready):
                m = cols.stop - cols.start
                for t, half_ready in enumerate((front_nrmT, rear_nrmT)):
                    pe.wait_ge(half_ready, 2)
                    for k in range(DH):
                        last = nc.tensor.matmul(bank(b + t)[0:m, :], wx_sb[:, k, cols], nrmT[:, k, 512 * t:512 * t + 512],
                                                start=(k == 0), stop=(k == DH - 1))
                    last.then_inc(ready, 1)

            project_norm(slice(0, RANK), 0, rank_ready)
            pe.wait_ge(L["wdt"], 16)
            for k in range(DH):
                for t in range(2):
                    pe.wait_ge(rank_copied, t + 1)
                    last = nc.tensor.matmul(bank(2 + 2 * k + t), wdt_sb[:, P * k:P * k + P],
                                            area_f[0:RANK, 512 * t:512 * t + 512], start=True, stop=True)
                last.then_inc(z_ready, 1)
            project_norm(slice(RANK, RANK + 96), 6, bc_ready)
            pe.wait_ge(fly_ready, 6)
            for g, b in enumerate((0, 1, 6, 7)):
                if g == 2:
                    pe.wait_ge(bc_done, 2)
                nc.tensor.matmul(bank(b), hadamard, fly[:, 512 * g:512 * g + 512], start=True, stop=True).then_inc(had_ready, 1)

            def select(b, which, n):
                for t in range(2):
                    last = nc.tensor.matmul(bank(b + t), sel_w[:, bass.ds(which * NS + n, 1), :].rearrange("p s m -> p (s m)"),
                                            bc_split[:, 512 * t:512 * t + 512], start=True, stop=True)
                return last

            def up(q, c):
                for i, w in enumerate((gate_w, lin_w)):
                    for k in range(DH):
                        last = nc.tensor.matmul(bank(6)[:, QW * i:QW * i + QW], w[:, k, P * c:P * c + P],
                                                nrmT[:, k, bass.ds(q * QW, QW)], start=(k == 0), stop=(k == DH - 1))
                return last

            pe.wait_ge(L["sel"], 16)
            pe.wait_ge(L["w1"], 16)
            pe.wait_ge(L["w3"], 16)
            pe.wait_ge(hid_ready, 2)
            pe.wait_ge(bc_done, 5)
            pe.wait_ge(z_read, 4)
            pe.wait_ge(down_ready, 2)
            select(0, 0, 0).then_inc(b_ready, 1)
            select(2, 0, n_of(0, 1)).then_inc(b_ready, 1)
            select(4, 1, 0).then_inc(c_ready, 1)
            pe.wait_ge(down_ready, 4)
            up(0, 0).then_inc(up_ready, 1)
            pe.wait_ge(up_read, 4)
            up(0, 1).then_inc(up_ready, 1)

            def ahead(q, c, n):
                return (q, c + n) if c + n < UPQ else (q + 1, c + n - UPQ)

            def unit(q, c, last_quarter):
                u = q * UPQ + c
                left = UPQ - 1 - c if last_quarter else UPQ
                if left >= 2:
                    q2, c2 = ahead(q, c, 2)
                    pe.wait_ge(scan_done, u + 3)
                    select(2 * (c2 % 2), 0, n_of(q2, c2)).then_inc(b_ready, 1)
                pe.wait_ge(hid_ready, u + 3)
                if c == 0:
                    pe.wait_ge(acc_free, q + 1)
                for k in range(DH):
                    last = nc.tensor.matmul(bank(7)[:, QW * k:QW * k + QW], down_w[:, D * c + P * k:D * c + P * k + P], hid[c % 2],
                                            start=(c == 0 and k == 0), stop=(c == UPQ - 1), skip_group_check=True)
                last.then_inc(hid_used, 1)
                if left >= 1 and c % 2:
                    q1, c1 = ahead(q, c, 1)
                    pe.wait_ge(yc_done, u + 2)
                    select(4, 1, n_of(q1, c1)).then_inc(c_ready, 1)
                if left >= 2:
                    pe.wait_ge(up_read, 2 * u + 6)
                    up(q2, c2).then_inc(up_ready, 1)

            with pe.Fori(0, QT_ - 1) as q:
                for c in range(UPQ):
                    unit(q, c, False)
            for c in range(UPQ):
                unit(QT_ - 1, c, True)

            for j in range(NT):
                pe.wait_ge((sumT_ready, late_sumT_ready)[j // 4], j // 2 % 2 + 1)
                for k in range(DH):
                    last = nc.tensor.transpose(bank(j // 2)[:, D * (j % 2) + P * k:D * (j % 2) + P * k + P],
                                               yacc[:, k, P * j:P * j + P], ident)
                if j % 2:
                    last.then_inc(back_ready, 1)

            pe.wait_ge(x1_ready, NT)
            keep_warm(7)
            turn_tiles(1)
            pe.wait_ge(front_nrmT, 4)
            pe.wait_ge(L["cattn"], 16)
            pe.wait_ge(v_done, 1)
            for t in range(NT):
                if t == 4:
                    pe.wait_ge(rear_nrmT, 4)
                for k in range(DH):
                    last = nc.tensor.matmul(bank(BANK_OF_V[t])[:, 0:D + NE], nrmT[:, k, P * t:P * t + P],
                                            cattn_sb[:, k, 2 * D:3 * D + NE], start=(k == 0), stop=(k == DH - 1))
                last.then_inc(v_ready, 1)

            def qk(i):
                g, b = QK_ORDER[i]
                m, t = g // 2, g % 2
                pe.wait_ge(v_done, 1 + BANK_OF_V.index(b) + 1)
                if i == 7:
                    pe.wait_ge(qk_done, 5)
                for k in range(DH):
                    last = nc.tensor.matmul(bank(b), cattn_sb[:, k, P * m:P * m + P], nrmT[:, k, 512 * t:512 * t + 512],
                                            start=(k == 0), stop=(k == DH - 1))
                last.then_inc(qk_ready, 1)

            for i in range(3):
                qk(i)

            def project(b):
                pe.wait_ge(ctx_done, b + 1)
                for i in range(2):
                    o, own = bank(2 * b)[:, D * i:D * i + D], slice(SEQ * b + P * i, SEQ * b + P * i + P)
                    for k in range(DH):
                        last = nc.tensor.matmul(o, ctxT[:, k, own], cproj_sb[:, k, :], start=(k == 0), stop=(k == DH - 1))
                last.then_inc(proj_ready, 1)

            def attention_round(steps):
                for which, step, b in steps:
                    a, o = (bank(2 * b), bank(2 * b + 1)) if which == 0 else (bank(2 * b + 1), bank(2 * b))
                    tokens = slice(SEQ * b, SEQ * b + SEQ)
                    if step == 0:
                        if which == 0:
                            pe.wait_ge(qk_done, 2 if b < 2 else 8)
                        if which == 0 and b == 3:
                            pe.wait_ge(slots_ready, 1)
                        if which:
                            pe.wait_ge(query_done, b + 1)
                        for i in range(2):
                            own = slice(SEQ * b + P * i, SEQ * b + P * i + P)
                            for k in range(which + 1):
                                last = nc.tensor.matmul(a[:, SEQ * i:SEQ * i + SEQ], qT[:, k, own], kT[:, k, tokens],
                                                        start=(k == 0), stop=(k == which))
                        last.then_inc(scores_ready, 1)
                    if step == 1:
                        if which == 0 and b < 2:
                            pe.wait_ge(qk_done, 4)
                        pe.wait_ge(probs_ready, nth(which, b))
                        for i in range(2):
                            for k in range(2):
                                last = nc.tensor.transpose(o[:, SEQ * k + P * i:SEQ * k + P * i + P],
                                                           probs[:, b, i, P * k:P * k + P], ident)
                        last.then_inc(probsT_ready, 1)
                    if step == 2:
                        pe.wait_ge(probsT_done, nth(which, b))
                        for h in range(which + 1):
                            for k in range(2):
                                last = nc.tensor.matmul(a[:, SEQ * h:SEQ * h + SEQ], val[:, 2 * b + k, P * h:P * h + P],
                                                        probsT[:, b, k, :], start=(k == 0), stop=(k == 1))
                        last.then_inc(context_ready, 1)

            first_round, *rounds = attention_steps()
            attention_round(first_round)
            qk(3)
            pe.wait_ge(mask_ready, 1)
            pe.wait_ge(L["bcst"], 16)
            tri, ones = bcst[:, B_TRI:B_TRI + P], bcst[:, B_ONE:B_ONE + P]
            pe.wait_ge(v_done, 1 + NT)
            counts, totals = bank(7)[:, 0:NT * NE], bank(7)[:, NT * NE:NT * NE + NE]
            nc.tensor.matmul(counts, tri, mask[:].rearrange("p t e -> p (t e)"), start=True, stop=False)
            for i in range(NT - 1):
                later = counts[:, NE * (i + 1):].rearrange("p (t e) -> p t e", e=NE)
                nc.tensor.matmul(later, ones, mask[:, i:i + 1, :].to_broadcast([P, NT - 1 - i, NE]),
                                 start=False, stop=(i == NT - 2))
            for i in range(NT):
                last = nc.tensor.matmul(totals, ones, mask[:, i, :], start=(i == 0), stop=(i == NT - 1))
            last.then_inc(prefix_ready, 1)
            for i in range(4, 8):
                qk(i)
            for steps in rounds:
                attention_round(steps)
            pe.wait_ge(L["cproj"], 16)
            for b in range(BATCH // 2):
                project(b)

            def turn_x(m, buffer=3):
                pe.wait_ge(x_loaded, 16 * 4 if buffer < 3 else 16 * m + 16)
                for k in range(DH):
                    last = nc.tensor.transpose(bank(0)[:, P * k:P * k + P], xin[buffer][:, P * k:P * k + P], ident)
                last.then_inc(x_turned, 1)

            def expert_of(m):
                return pe.value_load(owner[0:1, bass.ds(m, 1)], min_val=0, max_val=NE - 1)

            def layer1(m):
                e = expert_of(m)
                pe.wait_ge(xT_ready, m + 1)
                for k in range(DH):
                    last = nc.tensor.matmul(bank(1), xT[:, k, :], moe_w1[:, bass.ds(e, 1), k, :].rearrange("p e n -> p (e n)"),
                                            start=(k == 0), stop=(k == DH - 1))
                last.then_inc(l1_ready, 1)

            def turn(src, dst, need, ready, m):
                pe.wait_ge(need, m + 1)
                for k in range(KM):
                    last = nc.tensor.transpose(bank(dst)[:, P * k:P * k + P], src[:, P * k:P * k + P], ident)
                last.then_inc(ready, 1)

            def layer2(m):
                e = expert_of(m)
                pe.wait_ge(h1_ready, m + 1)
                for k in range(KM):
                    last = nc.tensor.matmul(bank(3), h1T[:, k, :], moe_w2[:, bass.ds(e, 1), k, :].rearrange("p e n -> p (e n)"),
                                            start=(k == 0), stop=(k == KM - 1))
                last.then_inc(l2_ready, 1)

            def layer3(m):
                e = expert_of(m)
                pe.wait_ge(h2_ready, m + 1)
                pe.wait_ge(y_read, m + 1)
                for k in range(KM):
                    last = nc.tensor.matmul(bank(5)[:, 0:D], h2T[:, k, :], moe_w3[:, bass.ds(e, 1), k, :].rearrange("p e n -> p (e n)"),
                                            start=(k == 0), stop=(k == KM - 1))
                last.then_inc(l3_ready, 1)

            def loaded(*names):
                for n in names:
                    pe.wait_ge(L[n], 16 * {"mw1": 6, "mw2": 6, "mw1_late": 2, "mw3": NE, "mw2_late": 2}[n])

            def expert_step(m, first_tile=False, left=MT):
                layer2(m)
                if left >= 1:
                    turn(raw1, 2, r1_ready, t1_ready, m + 1)
                if not first_tile:
                    layer3(m - 1)
                if left >= 2:
                    layer1(m + 2)
                turn(raw2, 4, r2_ready, t2_ready, m)
                if left >= 3:
                    turn_x(m + 3)

            pe.wait_ge(owner_ready, 1)
            pe.wait_ge(proj_added, 1)
            turn_x(0, buffer=0)
            project(2)
            loaded("mw1", "mw1_late")
            layer1(0)
            project(3)
            turn_x(1, buffer=1)
            pe.wait_ge(proj_added, 2)
            turn(raw1, 2, r1_ready, t1_ready, 0)
            layer1(1)
            turn_x(2, buffer=2)
            pe.wait_ge(proj_added, 3)
            loaded("mw2", "mw2_late")
            expert_step(0, first_tile=True)
            loaded("mw3")
            with pe.Fori(1, MT - 3) as m:
                expert_step(m)
            for left in (2, 1, 0):
                expert_step(MT - 1 - left, left=left)
            layer3(MT - 1)

        @block.vector
        def _(dve):
            chain = [0]

            def link(ins):
                chain[0] += 1
                ins.then_inc(dve_chain, 1)
                dve.wait_ge(dve_chain, chain[0])

            def turned_out(phase):
                for part, half_ready in enumerate((front_nrmT, rear_nrmT)):
                    dve.wait_ge(turned, 4 * phase + 2 * part + 2)
                    nc.vector.tensor_copy(nrmT[:, 1, 512 * part:512 * part + 512], bank(2 + part)).then_inc(half_ready, 1)

            def normalise(phase):
                dve.wait_ge(stats_done, (phase + 1) * NT)
                for t in range(NT):
                    ins = nc.vector.bn_aggr(mv[:, t, :], st6[:, t, :])
                link(ins)
                nc.vector.tensor_scalar(ln_v[:], mv[:, :, 1], EPS, None, ALU.add).then_inc(var_ready, 1)
                dve.wait_ge(sqrt_ready, phase + 1)
                link(nc.vector.reciprocal(ln_r[:], ln_s[:]))
                link(nc.vector.tensor_tensor(ln_t[:], ln_r[:], ln_r[:], ALU.mult))
                link(nc.vector.tensor_tensor(ln_t[:], ln_t[:], ln_v[:], ALU.mult))
                link(nc.vector.tensor_scalar(ln_t[:], ln_t[:], -0.5, 1.5, ALU.mult, ALU.add))
                link(nc.vector.tensor_tensor(ln_r[:], ln_r[:], ln_t[:], ALU.mult))
                for t in range(NT):
                    nc.vector.tensor_scalar(nrm[:, t, :], res[:, t, :], mv[:, t, 0:1], ln_r[:, t:t + 1],
                                            ALU.subtract, ALU.mult).then_inc(nrm_ready, 1)

            for t in range(NT):
                if t == 0:
                    dve.wait_ge(L["x"], 16)
                if t == 4:
                    dve.wait_ge(L["x2"], 16)
                nc.vector.bn_stats(st6[:, t, :], res[:, t, :]).then_inc(stats_done, 1)
            normalise(0)
            turned_out(0)
            dve.wait_ge(L["vec"], 16)
            nc.vector.tensor_copy(cattn_sb[:, :, 3 * D:3 * D + NE],
                                  vec[:, V_WG:V_WG + DH * NE].rearrange("p (k e) -> p k e", k=DH)).then_inc(v_done, 1)
            nc.vector.scalar_tensor_tensor(lw[:, 0:1], vec[:, V_W1:V_W1 + 1], 0.5, vec[:, V_W0:V_W0 + 1],
                                           ALU.mult, ALU.add).then_inc(z2_ready, 1)
            nc.vector.memset(ln_t[:, 0:1], 0.0).then_inc(scan_done, 2)
            nc.vector.memset(ln_t[:, 1:2], 0.0).then_inc(hid_used, 2)
            nc.vector.memset(ln_t[:, 2:3], 0.0).then_inc(up_read, 2)
            nc.vector.memset(ln_t[:, 3:4], 0.0).then_inc(acc_free, 1)
            nc.vector.memset(ln_t[:, 5:6], 0.0).then_inc(own_added, 1)
            u1 = loan2[:, 0:2048].rearrange("p (k t) -> p k t", k=DH)
            e = area_g[:].rearrange("p (k t) -> p k t", k=DH)
            for k in range(DH):
                dve.wait_ge(absexp_done, k + 1)
                link(nc.vector.tensor_scalar(u1[:, k, :], e[:, k, :], 1.0, None, ALU.add))
                nc.vector.scalar_tensor_tensor(e[:, k, :], u1[:, k, :], -1.0, e[:, k, :], ALU.add,
                                               ALU.subtract).then_inc(onepl_done, 1)
            v = bank(6, 2)
            dve.wait_ge(bc_done, 1)
            nc.vector.tensor_tensor(area_e[0:96, 0:TOK], v[0:96, :], bc_split[0:96, :], ALU.subtract).then_inc(bc_done, 1)
            dve.wait_ge(bc_done, 2)
            nc.vector.tensor_copy(bc_split[32:64, :], area_e[32:64, 0:TOK]).then_inc(bc_done, 1)
            nc.vector.tensor_copy(bc_split[64:96, :], area_e[64:96, 0:TOK]).then_inc(bc_done, 1)
            dve.wait_ge(bc_done, 4)
            link(nc.vector.tensor_tensor(area_e[64:96, 0:TOK], area_e[64:96, 0:TOK], bc_split[64:96, :], ALU.subtract))
            nc.vector.tensor_copy(bc_split[64:96, :], area_e[64:96, 0:TOK]).then_inc(bc_done, 1)
            nc.vector.memset(decay.rearrange("p i (b t) -> p (i b) t", b=BATCH)[:, :, 0:1], 0.0).then_inc(decay_zero, 1)
            dve.wait_ge(bc_done, 5)
            dve.wait_ge(front_nrmT, 2)
            dve.wait_ge(rear_nrmT, 2)
            dve.wait_ge(less_lost, 1)
            dve.wait_ge(log_done, 1)
            nc.vector.tensor_tensor(delta[:, 0, :], delta[:, 0, :], u1[:, 0, :], ALU.add).then_inc(delta_ready, 1)
            dve.wait_ge(delta_ready, 1)
            link(nc.vector.tensor_tensor(du[:, 0, :], delta[:, 0, :], nrmT[:, 0, :], ALU.mult))

            def product(q, c):
                u = q * UPQ + c
                dve.wait_ge(b_ready, u + 1)
                if c % 2:
                    dve.wait_ge(du1_ready, 1)
                b = bank(2 * (c % 2), 2)
                nc.vector.tensor_tensor(b, du[:, c % DH, :], b, ALU.mult).then_inc(bx_done, 1)

            product(0, 0)

            dve.wait_ge(lw_ready, 1)
            nc.vector.tensor_scalar(lw[:, 1:2], lw[:, 1:2], 0.5, 0.5, ALU.mult, ALU.add).then_inc(lw_ready, 1)

            def add_own(c):
                return nc.vector.tensor_tensor(yacc[:, c % 2, 0:OWN], yacc[:, c % 2, 0:OWN], state[:, c % 2, 0:OWN], ALU.add)

            dve.wait_ge(less_lost, 2)
            nc.vector.memset(state[:, 1, 0:OWN], 0.0).then_inc(yc_done, 1)

            def unit(q, c, last_quarter):
                u = q * UPQ + c
                dve.wait_ge(bx_done, u + 1)
                dve.wait_ge(decay_ready, u + 1)
                dve.wait_ge(y_added, u + 1)
                dve.wait_ge(own_added, u + 1)
                nc.vector.tensor_tensor_scan(state[:, c % 2, :], decay[:, c % 2, :], bank(2 * (c % 2), 2), 0.0,
                                             ALU.mult, ALU.add).then_inc(scan_done, 1)
                dve.wait_ge(yc_done, u + 1)
                add_own(c + 1).then_inc(own_added, 1)
                if not (last_quarter and c == UPQ - 1):
                    product(*((q, c + 1) if c + 1 < UPQ else (q + 1, 0)))
                dve.wait_ge(scan_done, u + 3)
                dve.wait_ge(c_ready, q * (UPQ // DH) + c // DH + 1)
                nc.vector.tensor_tensor(state[:, c % 2, :], state[:, c % 2, :], bank(4, 2), ALU.mult).then_inc(yc_done, 1)

            with dve.Fori(0, QT_ - 1) as q:
                for c in range(UPQ):
                    unit(q, c, False)
            for c in range(UPQ):
                unit(QT_ - 1, c, True)

            dve.wait_ge(yc_done, UNITS + 1)
            dve.wait_ge(own_added, UNITS + 1)
            dve.wait_ge(y_added, UNITS)
            nc.vector.tensor_tensor(yacc[:, 1, :], yacc[:, 1, :], state[:, 1, :], ALU.add).then_inc(y_added, 1)
            dve.wait_ge(acc_free, QT_ + 1)
            dve.wait_ge(y_added, UNITS + 2)
            for g in (0, 1):
                t = slice(g * QW, g * QW + QW)
                nc.vector.tensor_tensor(yacc[:, :, t], yacc[:, :, t], ffn_out[:, :, t], ALU.add).then_inc(sumT_ready, 1)

            def statistics(g):
                dve.wait_ge(x1_ready, 2 * g + 2)
                for t in (2 * g, 2 * g + 1):
                    nc.vector.bn_stats(st6[:, t, :], res[:, t, :]).then_inc(stats_done, 1)

            for g in range(4):
                dve.wait_ge(back_ready, g + 1)
                nc.vector.tensor_tensor(res[:, 2 * g:2 * g + 2, :].rearrange("p t d -> p (t d)"),
                                        res[:, 2 * g:2 * g + 2, :].rearrange("p t d -> p (t d)"), bank(g), ALU.add).then_inc(x1_ready, 2)
                if g:
                    statistics(g - 1)
            statistics(3)

            normalise(1)
            turned_out(1)

            dve.wait_ge(L["row"], 16)
            wide = lambda a: a.unsqueeze(2).to_broadcast([P, NT, NE])
            over_tiles = lambda a: a.unsqueeze(1).to_broadcast([P, NT, NE])
            key = over_tiles(cst[:, C_KEY:C_KEY + NE])
            for t in range(NT):
                dve.wait_ge(v_ready, t + 1)
                nc.vector.tensor_tensor(logit[:, t, :], bank(BANK_OF_V[t])[:, D:D + NE], row[:, R_BG:R_BG + NE],
                                        ALU.add).then_inc(dve_chain, 1)
                chain[0] += 1
                nc.vector.tensor_tensor(val[:, t, :], bank(BANK_OF_V[t])[:, 0:D], row[:, R_VB:R_VB + D], ALU.add).then_inc(v_done, 1)
            dve.wait_ge(dve_chain, chain[0])
            link(nc.vector.tensor_reduce(top, logit, AX.X, ALU.max))
            link(nc.vector.tensor_tensor(logit, logit, wide(top), ALU.subtract))
            nc.vector.tensor_scalar(first, logit, 0.0, None, ALU.is_equal).then_inc(soft_in, 1)
            dve.wait_ge(soft_in, 1)

            def lowest(choice):
                link(nc.vector.tensor_tensor(keyed, choice, key, ALU.mult))
                link(nc.vector.tensor_reduce(keymax, keyed, AX.X, ALU.max))
                link(nc.vector.tensor_tensor(choice, keyed, wide(keymax), ALU.is_equal))

            lowest(first)
            dve.wait_ge(soft_out, 1)
            link(nc.vector.scalar_tensor_tensor(logit, first, -1e30, logit, ALU.mult, ALU.add))
            nc.vector.tensor_reduce(top2, logit, AX.X, ALU.max).then_inc(top2_ready, 1)
            dve.wait_ge(top2_ready, 1)
            link(nc.vector.tensor_tensor(second, logit, wide(top2), ALU.is_equal))
            lowest(second)
            nc.vector.tensor_tensor(mask[:], first, second, ALU.add).then_inc(mask_ready, 1)
            link(nc.vector.tensor_reduce(esum, expd, AX.X, ALU.add))
            dve.wait_ge(L["home"], 16)
            link(nc.vector.reciprocal(gain[:, 0, :], esum))
            dve.wait_ge(e2_ready, 1)
            link(nc.vector.tensor_tensor(gain[:, 1, :], gain[:, 0, :], e2, ALU.mult))
            def attention_round(steps):
                for which, step, b in steps:
                    if step == 0:
                        src = bank(2 * b + which).rearrange("p (i t) -> p i t", i=2)
                        dve.wait_ge(scores_ready, nth(which, b))
                        link(nc.vector.tensor_reduce(smax[:, which, b, :], src, AX.X, ALU.max))
                        nc.vector.tensor_scalar(smax[:, which, b, :], smax[:, which, b, :], -SCALE, None,
                                                ALU.mult).then_inc(bias_ready, 1)
                for which, step, b in steps:
                    if step == 0:
                        dve.wait_ge(exp_done, 2 * nth(which, b))
                        link(nc.vector.reciprocal(sinv[:, which, b, :], ssum[:, which, b, :]))
                        for i in range(2):
                            ins = nc.vector.tensor_scalar(probs[:, b, i, :], probs[:, b, i, :], sinv[:, which, b, i:i + 1], None,
                                                          ALU.mult)
                        ins.then_inc(probs_ready, 1)
                for which, step, b in steps:
                    if step == 2 and which == 0:
                        dve.wait_ge(tanh_done, b + 1)
                        q0 = qT[:, 0, SEQ * b:SEQ * b + SEQ]
                        nc.vector.scalar_tensor_tensor(q0, probs[:, b, 0, :], lw[:, 1:2], q0, ALU.mult, ALU.add).then_inc(query_done, 1)


            first_round, *rounds = attention_steps()
            attention_round(first_round)
            dve.wait_ge(prefix_ready, 1)
            link(nc.vector.tensor_scalar(tile_int, bank(7)[:, NT * NE:NT * NE + NE], float(P - 1), None, ALU.add))
            link(nc.vector.tensor_scalar(tile_int, tile_int, 7, None, ALU.logical_shift_right))
            link(nc.vector.tensor_copy(tiles8, tile_int))
            link(nc.vector.tensor_scalar(ones8, tiles8, 0.0, None, ALU.is_ge))
            link(nc.vector.tensor_tensor_scan(upto8, ones8, tiles8, 0.0, ALU.mult, ALU.add))
            link(nc.vector.tensor_tensor(base8, upto8, tiles8, ALU.subtract))
            link(nc.vector.tensor_scalar(base8, base8, float(P), None, ALU.mult))
            link(nc.vector.tensor_tensor(place, bank(7)[:, 0:NT * NE].rearrange("p (t e) -> p t e", e=NE),
                                         over_tiles(base8), ALU.add))
            for k, choice in enumerate((first, second)):
                link(nc.vector.tensor_tensor(tmp64, choice, place, ALU.mult))
                link(nc.vector.tensor_reduce(slotf, tmp64, AX.X, ALU.add))
                ins = nc.vector.tensor_copy(slot[:, k, :], slotf)
                if k == 0:
                    link(ins)
                else:
                    ins.then_inc(slots_ready, 1)
            link(nc.vector.tensor_tensor(hits, upto8.unsqueeze(1).to_broadcast([P, MT, NE]),
                                         cst[:, C_TILE:C_TILE + MT].unsqueeze(2).to_broadcast([P, MT, NE]), ALU.is_le))
            link(nc.vector.tensor_reduce(owner_f, hits, AX.X, ALU.add))
            link(nc.vector.tensor_scalar(owner_f, owner_f, float(NE - 1), None, ALU.min))
            nc.vector.tensor_copy(owner[:], owner_f).then_inc(owner_ready, 1)
            dve.wait_ge(owner_ready, 1)
            row_of, tile_of = (area_g[:, 900 + 16 * i:916 + 16 * i].bitcast(U32).rearrange("p (k t) -> p k t", k=2)
                               for i in range(2))
            nc.vector.tensor_scalar(row_of, slot[:], P - 1, None, ALU.bitwise_and).then_inc(dve_chain, 1)
            chain[0] += 1
            link(nc.vector.tensor_scalar(tile_of, slot[:], 7, None, ALU.logical_shift_right))
            link(nc.vector.scalar_tensor_tensor(home_slot[:], row_of, float(MT), tile_of, ALU.mult, ALU.add))
            nc.vector.memset(ln_t[:, 4:5], 0.0).then_inc(slots_ready, 1)

            for steps in rounds:
                attention_round(steps)
            nc.vector.memset(ln_t[:, 5:6], 0.0).then_inc(y_ready, 1)
            nc.vector.memset(ln_t[:, 6:7], 0.0).then_inc(y_read, 1)

            def x_out(m, first_tile):
                dve.wait_ge(x_turned, m + 1)
                if not first_tile:
                    dve.wait_ge(l1_ready, m)
                nc.vector.tensor_copy(xT.rearrange("p k t -> p (k t)"), bank(0)[:, 0:D]).then_inc(xT_ready, 1)

            def raw_out(dst, src, product, used, done, m, first_tile):
                dve.wait_ge(product, m + 1)
                if not first_tile:
                    dve.wait_ge(used, m)
                nc.vector.tensor_copy(dst, bank(src)).then_inc(done, 1)

            def y_out(m):
                e = dve.value_load(owner[0:1, bass.ds(m, 1)], min_val=0, max_val=NE - 1)
                dve.wait_ge(l3_ready, m + 1)
                dve.wait_ge(y_ready, m + 1)
                nc.vector.tensor_tensor(yraw, bank(5)[:, 0:D], b3_sb[:, bass.ds(e, 1), :].rearrange("p e d -> p (e d)"),
                                        ALU.add).then_inc(y_read, 1)
                dve.wait_ge(y_read, m + 2)
                dve.wait_ge(home_ready, m + 1)
                nc.vector.tensor_scalar(yout, yraw, home_gain[:, bass.ds(2 * m + 1, 1)], None, ALU.mult).then_inc(y_ready, 1)

            def expert_step(m, first_tile=False, left=MT):
                raw_out(raw2, 3, l2_ready, t2_ready, r2_ready, m, first_tile)
                if not first_tile:
                    y_out(m - 1)
                if left >= 2:
                    raw_out(raw1, 1, l1_ready, t1_ready, r1_ready, m + 2, False)
                if left >= 3:
                    x_out(m + 3, False)

            def add_projection(b):
                dve.wait_ge(proj_ready, b + 1)
                both = res[:, 2 * b:2 * b + 2, :].rearrange("p t d -> p (t d)")
                nc.vector.tensor_tensor(both, both, bank(2 * b), ALU.add).then_inc(proj_added, 1)

            dve.wait_ge(bias_added, 1)
            add_projection(0)
            add_projection(1)
            x_out(0, True)
            add_projection(2)
            raw_out(raw1, 1, l1_ready, t1_ready, r1_ready, 0, True)
            add_projection(3)
            x_out(1, False)
            raw_out(raw1, 1, l1_ready, t1_ready, r1_ready, 1, False)
            x_out(2, False)
            expert_step(0, first_tile=True)
            dve.wait_ge(homes_loaded, 16)
            dve.wait_ge(L["b3"], 16)
            with dve.Fori(1, MT - 3) as m:
                expert_step(m)
            for left in (2, 1, 0):
                expert_step(MT - 1 - left, left=left)
            y_out(MT - 1)


def _layouts(v):
    import numpy as np

    f = lambda n: np.ascontiguousarray(v[n])
    wx = f("L0_attn_W_x")
    bc = wx[RANK:].T
    cols = lambda a: a.reshape(-1, P).T
    attn_b = f("L1_attn_c_attn_b")
    one = lambda n: np.broadcast_to(f(n).reshape(1, 1), (P, 1))
    vecs = np.concatenate([
        cols(f("L0_attn_b_dt")), cols(f("L0_attn_D")),
        f("L0_attn_A_log").reshape(DH, P, NS).transpose(1, 0, 2).reshape(P, DH * NS),
        cols(attn_b[:2 * D]), f("L1_attn_cam_gate").reshape(P, 1), one("L1_attn_cam_w0"), one("L1_attn_cam_w1"),
        cols(f("L1_ffn_b1").reshape(-1)), cols(f("L1_ffn_b2").reshape(-1)),
        f("L1_ffn_Wg").reshape(DH, P, NE).transpose(1, 0, 2).reshape(P, DH * NE)], axis=1)
    rows = np.concatenate([attn_b[2 * D:], f("L1_attn_c_proj_b"), f("L1_ffn_bg")])
    had = np.ones((1, 1), np.float32)
    while had.shape[0] < P:
        had = np.block([[had, had], [had, -had]])
    consts = np.concatenate([np.eye(P), had, np.broadcast_to(np.arange(NE, 0, -1), (P, NE)),
                             np.broadcast_to(np.arange(MT), (P, MT))], axis=1).astype(np.float32)
    one_bf16 = 0x3F80
    bconsts = (np.concatenate([np.triu(np.ones((P, P)), 1), np.ones((P, P))], axis=1) * one_bf16).astype(np.uint16)
    sel = np.zeros((P, 2 * NS, P), np.uint16)
    for s in range(2 * NS):
        for part in range(3):
            sel[32 * part + s, s, :] = one_bf16
    return {
        "x": f("L0_attn_x").reshape(TOK, D), "wx": np.concatenate([wx[:RANK].T, bc, bc, bc], axis=1),
        "wdt": f("L0_attn_W_dt").T, "w1": f("L0_ffn_W1").T, "w3": f("L0_ffn_W3").T, "w2": f("L0_ffn_W2").T,
        "vecs": vecs, "rows": np.broadcast_to(rows[None], (P, R_END)), "consts": consts, "bconsts": bconsts,
        "sel": sel.reshape(P, -1), "cattn": f("L1_attn_c_attn_w"), "cproj": f("L1_attn_c_proj_w"),
        "mw1": f("L1_ffn_W1"), "mw2": f("L1_ffn_W2"), "mw3": f("L1_ffn_W3"), "b3": f("L1_ffn_b3"),
        "zeros": np.zeros((MT * P, D), np.float32),
        "home_of": np.stack([np.arange(2 * NT)[None] % NT * P + np.arange(P)[:, None], np.zeros((P, 2 * NT))],
                            axis=2).astype(np.int32).reshape(P, 4 * NT),
        "no_home": np.stack([np.arange(TOK, TOK + MT * P).reshape(MT, P).T, np.zeros((P, MT))],
                            axis=2).astype(np.int32).reshape(P * MT, 2),
    }


def kernel(**inputs):
    import numpy as np
    import concourse.bacc as bacc
    from concourse.bass_utils import run_bass_kernel_spmd

    nc = bacc.Bacc("TRN2", target_bir_lowering=False, num_devices=1)
    arrays = {f"in_{n}": np.ascontiguousarray(a) for n, a in _layouts(inputs).items()}
    args = [nc.dram_tensor(n, a.shape, mybir.dt.from_np(a.dtype), kind="ExternalInput").ap() for n, a in arrays.items()]
    result = nc.dram_tensor("out_0", (TOK, D), F32, kind="ExternalOutput").ap()
    build(nc, *args, result)
    got = run_bass_kernel_spmd(nc, [arrays], core_ids=[0]).results[0]["out_0"]
    return got.reshape(BATCH, SEQ, D)
```
